# Optimizing a Trainium2 kernel written in Bass

```python
import numpy as np
import jax
import jax.numpy as jnp

def _softmax(x, axis=-1):
    return jax.nn.softmax(x, axis=axis)

def _gelu(x):
    return jax.nn.gelu(x, approximate=True)

def _silu(x):
    return jax.nn.silu(x)

def _sigmoid(x):
    return jax.nn.sigmoid(x)

def _layernorm(x, axis=-1, eps=1e-05):
    m = jnp.mean(x, axis=axis, keepdims=True)
    v = jnp.var(x, axis=axis, keepdims=True)
    return (x - m) / jnp.sqrt(v + eps)

def _scatter_add(tgt, idx, src, axis=0):
    return tgt.at[idx].add(src)

def _segment_sum(src, seg, n):
    return jax.ops.segment_sum(src, seg, n)
kernel_name = 'mk_decoder_postln_d2_seqx_r8_7671fb'

def setup_inputs(seed: int=0):
    np.random.seed(seed)
    _w = jnp.asarray

    def _rec_inputs():
        import jax
        import jax.numpy as jnp
        _rk = jax.random.key(seed)
        x = 7.22e-05 + 1 * jax.random.normal(jax.random.fold_in(_rk, 1), (16, 128, 256), jnp.float32)
        _lenS = 128 - jax.random.randint(jax.random.fold_in(_rk, 7), (16,), 0, max(1, 128 // 4) + 1, jnp.int32)
        _lenS2 = 128 - jax.random.randint(jax.random.fold_in(_rk, 8), (16,), 0, max(1, 128 // 4) + 1, jnp.int32)
        _ctx_2048P = jax.random.normal(jax.random.fold_in(_rk, 11), (16, 16, 256), jnp.float32)
        _ctx_2048c = jax.random.dirichlet(jax.random.fold_in(_rk, 511), 0.3 * jnp.ones((16,), jnp.float32), (16, 128))
        _ctx_2048t = jnp.einsum('bsk,bkd->bsd', _ctx_2048c, _ctx_2048P)
        _ctx_2048t = _ctx_2048t * jax.lax.rsqrt(jnp.mean(jnp.square(_ctx_2048t)) + 1e-12) * 0.953939
        ctx_2048 = 4.13588e-05 + 0.999923 * (_ctx_2048t + 0.3 * jax.random.normal(jax.random.fold_in(_rk, 611), (16, 128, 256), jnp.float32))
        _validS = jnp.arange(128)[None, :] < _lenS[:, None]
        _validS2 = jnp.arange(128)[None, :] < _lenS2[:, None]
        _causal = jnp.tril(jnp.ones((128, 128), dtype=bool))
        mask_BxS2_bk0 = jnp.logical_not(jnp.broadcast_to(_validS2[:, :], (16, 128)))
        return (x, ctx_2048, mask_BxS2_bk0)
    x, ctx_2048, mask_BxS2_bk0 = _rec_inputs()

    def _L0_attn_setup():
        import jax, jax.numpy as jnp
        import numpy as np
        N_HEAD = 32
        HEAD_ID = 0
        MASKED_BIAS = -10000.0
        key = jax.random.key(seed)
        k1, k2, k3 = jax.random.split(key, 3)
        B, S, E = (1, 256, 256)
        hidden_states = jax.random.normal(k1, (B, S, E), dtype=jnp.float32)
        W_attn = jax.random.normal(k2, (E, 3 * E), dtype=jnp.float32) * (1.0 / np.sqrt(E))
        b_attn = jnp.zeros((3 * E,), dtype=jnp.float32)
        W_proj = jax.random.normal(k3, (E, E), dtype=jnp.float32) * (1.0 / np.sqrt(E))
        b_proj = jnp.zeros((E,), dtype=jnp.float32)
        return {'hidden_states': hidden_states, 'W_attn': W_attn, 'b_attn': b_attn, 'W_proj': W_proj, 'b_proj': b_proj}
    _L0_attn_all = _L0_attn_setup()
    _L0_attn_in = {k: v for k, v in _L0_attn_all.items() if k in ('W_attn', 'b_attn', 'W_proj', 'b_proj')}
    del _L0_attn_all

    def _L0_xattn_setup():
        import jax, jax.numpy as jnp
        import numpy as np
        N_HEAD = 8
        key = jax.random.key(seed)
        k1, k2, k3 = jax.random.split(key, 3)
        b, d, m = (4, 128, 256)
        c, n = (128, 256)
        q = jax.random.normal(k1, (b, d, m), dtype=jnp.float32)
        k = jax.random.normal(k2, (d // d * b, d, n), dtype=jnp.float32).reshape(b, d, n)
        v = jax.random.normal(k3, (b, c, n), dtype=jnp.float32)
        return {'q': q, 'k': k, 'v': v}
    _L0_xattn_all = _L0_xattn_setup()
    _L0_xattn_in = {k: v for k, v in _L0_xattn_all.items() if k in ()}
    del _L0_xattn_all

    def _L0_ffn_setup():
        import jax, jax.numpy as jnp
        import numpy as np
        HIDDEN = 256
        INTER = 704
        B, S = (2, 256)

        def _ternary(key, shape):
            return jax.random.randint(key, shape, -1, 2).astype(jnp.float32)
        key = jax.random.key(seed)
        ks = jax.random.split(key, 7)
        x = jax.random.normal(ks[0], (B, S, HIDDEN), dtype=jnp.float32)
        gate_w = _ternary(ks[1], (INTER, HIDDEN))
        up_w = _ternary(ks[2], (INTER, HIDDEN))
        down_w = _ternary(ks[3], (HIDDEN, INTER))
        gate_s = jax.random.uniform(ks[4], (INTER,), minval=0.01, maxval=0.1, dtype=jnp.float32)
        up_s = jax.random.uniform(ks[5], (INTER,), minval=0.01, maxval=0.1, dtype=jnp.float32)
        down_s = jax.random.uniform(ks[6], (HIDDEN,), minval=0.01, maxval=0.1, dtype=jnp.float32)
        return {'x': x, 'gate_w': gate_w, 'up_w': up_w, 'down_w': down_w, 'gate_s': gate_s, 'up_s': up_s, 'down_s': down_s}
    _L0_ffn_all = _L0_ffn_setup()
    _L0_ffn_in = {k: v for k, v in _L0_ffn_all.items() if k in ('gate_w', 'up_w', 'down_w', 'gate_s', 'up_s', 'down_s')}
    del _L0_ffn_all

    def _L1_attn_setup():
        import math
        import jax, jax.numpy as jnp
        import numpy as np
        B, N, D_MODEL, H = (2, 512, 256, 16)
        HEAD_DIM = D_MODEL // H
        CHUNK = 128

        def _slopes(n_heads):
            start = 2.0 ** (-2.0 ** (-(math.log2(n_heads) - 3)))
            return np.array([start ** (i + 1) for i in range(n_heads)], dtype=np.float32)

        def _lightning_attn(q, k, v):
            b, h, n, d = q.shape
            nc = n // CHUNK
            lam = jnp.exp(-jnp.asarray(_slopes(h)))
            pos = jnp.arange(CHUNK, dtype=jnp.float32)
            decay_q = lam[:, None] ** (pos + 1.0)
            decay_k = lam[:, None] ** (CHUNK - 1.0 - pos)
            diff = pos[:, None] - pos[None, :]
            causal = diff >= 0
            dmask = jnp.where(causal, lam[:, None, None] ** jnp.maximum(diff, 0.0), 0.0)
            lam_c = lam ** CHUNK

            def to_chunks(t):
                return t.reshape(b, h, nc, CHUNK, d).transpose(2, 0, 1, 3, 4)
            qc, kc, vc = (to_chunks(q), to_chunks(k), to_chunks(v))

            def step(S, inp):
                qb, kb, vb = inp
                inter = jnp.einsum('bhcd,bhde->bhce', qb * decay_q[None, :, :, None], S)
                scores = jnp.einsum('bhcd,bhed->bhce', qb, kb) * dmask[None]
                intra = jnp.einsum('bhce,bhed->bhcd', scores, vb)
                S_new = lam_c[None, :, None, None] * S + jnp.einsum('bhcd,bhce->bhde', kb * decay_k[None, :, :, None], vb)
                return (S_new, inter + intra)
            S0 = jnp.zeros((b, h, d, d), dtype=q.dtype)
            _, out = jax.lax.scan(step, S0, (qc, kc, vc))
            return out.transpose(1, 2, 0, 3, 4).reshape(b, h, n, d)
        key = jax.random.key(seed)
        kx, k1, k2, k3, k4 = jax.random.split(key, 5)
        scale = 1.0 / math.sqrt(D_MODEL)
        x = jax.random.normal(kx, (B, N, D_MODEL), dtype=jnp.float32)
        w_qkv = jax.random.normal(k1, (3 * D_MODEL, D_MODEL), dtype=jnp.float32) * scale
        b_qkv = jax.random.normal(k2, (3 * D_MODEL,), dtype=jnp.float32) * 0.01
        w_out = jax.random.normal(k3, (D_MODEL, D_MODEL), dtype=jnp.float32) * scale
        b_out = jax.random.normal(k4, (D_MODEL,), dtype=jnp.float32) * 0.01
        return {'x': x, 'w_qkv': w_qkv, 'b_qkv': b_qkv, 'w_out': w_out, 'b_out': b_out}
    _L1_attn_all = _L1_attn_setup()
    _L1_attn_in = {k: v for k, v in _L1_attn_all.items() if k in ('w_qkv', 'b_qkv', 'w_out', 'b_out')}
    del _L1_attn_all

    def _L1_xattn_setup():
        import jax, jax.numpy as jnp
        import numpy as np
        H = 256
        NH = 16
        HD = H // NH
        EPS = 1e-06

        def rmsnorm(x, w, eps=EPS):
            var = jnp.mean(x * x, axis=-1, keepdims=True)
            return x * jax.lax.rsqrt(var + eps) * w
        key = jax.random.key(seed)
        ks = jax.random.split(key, 9)
        B, L, M = (4, 512, 32)
        s = 1.0 / np.sqrt(H)
        return {'hidden_states': jax.random.normal(ks[0], (B, L, H), dtype=jnp.float32), 'memory_tokens': jax.random.normal(ks[1], (B, M, H), dtype=jnp.float32), 'memory_mask': jax.random.randint(ks[2], (B, M), 0, 2).astype(bool), 'norm_w': jnp.ones((H,), dtype=jnp.float32), 'wq': jax.random.normal(ks[3], (H, H), dtype=jnp.float32) * s, 'wk': jax.random.normal(ks[4], (H, H), dtype=jnp.float32) * s, 'wv': jax.random.normal(ks[5], (H, H), dtype=jnp.float32) * s, 'wo': jax.random.normal(ks[6], (H, H), dtype=jnp.float32) * s, 'wg': jax.random.normal(ks[7], (H, H), dtype=jnp.float32) * s}
    _L1_xattn_all = _L1_xattn_setup()
    _L1_xattn_in = {k: v for k, v in _L1_xattn_all.items() if k in ('norm_w', 'wq', 'wk', 'wv', 'wo', 'wg')}
    del _L1_xattn_all

    def _L1_ffn_setup():
        import jax, jax.numpy as jnp
        import numpy as np
        NUM_EXPERTS = 8
        RANK = 16
        TOP_K = 2
        SCALING = 32.0 / RANK
        IN_F = 256
        OUT_F = 256
        key = jax.random.key(seed)
        k1, k2, k3, k4, k5 = jax.random.split(key, 5)
        B, T = (4, 256)
        x = jax.random.normal(k1, (B, T, IN_F), dtype=jnp.float32)
        bound_w = 1.0 / np.sqrt(IN_F)
        weight = jax.random.uniform(k2, (OUT_F, IN_F), jnp.float32, -bound_w, bound_w)
        lora_A = jax.random.uniform(k3, (NUM_EXPERTS, RANK, IN_F), jnp.float32, -bound_w, bound_w)
        lora_B = 0.02 * jax.random.normal(k4, (NUM_EXPERTS, OUT_F, RANK), dtype=jnp.float32)
        router_w = jax.random.uniform(k5, (NUM_EXPERTS, IN_F), jnp.float32, -bound_w, bound_w)
        return {'x': x, 'weight': weight, 'lora_A': lora_A, 'lora_B': lora_B, 'router_w': router_w}
    _L1_ffn_all = _L1_ffn_setup()
    _L1_ffn_in = {k: v for k, v in _L1_ffn_all.items() if k in ('weight', 'lora_A', 'lora_B', 'router_w')}
    del _L1_ffn_all
    return {'x': x, 'ctx_2048': ctx_2048, 'mask_BxS2_bk0': mask_BxS2_bk0, 'L0_attn_W_attn': _L0_attn_in['W_attn'], 'L0_attn_b_attn': _L0_attn_in['b_attn'], 'L0_attn_W_proj': _L0_attn_in['W_proj'], 'L0_attn_b_proj': _L0_attn_in['b_proj'], 'L0_ffn_gate_w': _L0_ffn_in['gate_w'], 'L0_ffn_up_w': _L0_ffn_in['up_w'], 'L0_ffn_down_w': _L0_ffn_in['down_w'], 'L0_ffn_gate_s': _L0_ffn_in['gate_s'], 'L0_ffn_up_s': _L0_ffn_in['up_s'], 'L0_ffn_down_s': _L0_ffn_in['down_s'], 'L1_attn_w_qkv': _L1_attn_in['w_qkv'], 'L1_attn_b_qkv': _L1_attn_in['b_qkv'], 'L1_attn_w_out': _L1_attn_in['w_out'], 'L1_attn_b_out': _L1_attn_in['b_out'], 'L1_xattn_norm_w': _L1_xattn_in['norm_w'], 'L1_xattn_wq': _L1_xattn_in['wq'], 'L1_xattn_wk': _L1_xattn_in['wk'], 'L1_xattn_wv': _L1_xattn_in['wv'], 'L1_xattn_wo': _L1_xattn_in['wo'], 'L1_xattn_wg': _L1_xattn_in['wg'], 'L1_ffn_weight': _L1_ffn_in['weight'], 'L1_ffn_lora_A': _L1_ffn_in['lora_A'], 'L1_ffn_lora_B': _L1_ffn_in['lora_B'], 'L1_ffn_router_w': _L1_ffn_in['router_w']}

def reference(x, ctx_2048, mask_BxS2_bk0, L0_attn_W_attn, L0_attn_b_attn, L0_attn_W_proj, L0_attn_b_proj, L0_ffn_gate_w, L0_ffn_up_w, L0_ffn_down_w, L0_ffn_gate_s, L0_ffn_up_s, L0_ffn_down_s, L1_attn_w_qkv, L1_attn_b_qkv, L1_attn_w_out, L1_attn_b_out, L1_xattn_norm_w, L1_xattn_wq, L1_xattn_wk, L1_xattn_wv, L1_xattn_wo, L1_xattn_wg, L1_ffn_weight, L1_ffn_lora_A, L1_ffn_lora_B, L1_ffn_router_w):
    import jax
    import jax.numpy as jnp

    def _L0_attn_ref(hidden_states, W_attn, b_attn, W_proj, b_proj):
        import jax, jax.numpy as jnp
        import numpy as np
        N_HEAD = 32
        HEAD_ID = 0
        MASKED_BIAS = -10000.0
        B, S, E = hidden_states.shape
        H = N_HEAD
        D = E // H
        m = 2.0 ** (-(8.0 / H) * (HEAD_ID + 1))
        qkv = hidden_states @ W_attn + b_attn
        q, k, v = jnp.split(qkv, 3, axis=-1)
        q = q.reshape(B, S, H, D).transpose(0, 2, 1, 3)
        k = k.reshape(B, S, H, D).transpose(0, 2, 1, 3)
        v = v.reshape(B, S, H, D).transpose(0, 2, 1, 3)
        scores = jnp.einsum('bhqd,bhkd->bhqk', q, k) / jnp.sqrt(jnp.float32(D))
        rows = jnp.arange(S)[:, None]
        cols = jnp.arange(S)[None, :]
        causal = cols <= rows
        scores = jnp.where(causal, scores, jnp.float32(MASKED_BIAS))
        alibi = jnp.where(causal, (cols - rows).astype(scores.dtype), 0.0)
        scores = scores + alibi * m
        probs = jax.nn.softmax(scores, axis=-1)
        attn = jnp.einsum('bhqk,bhkd->bhqd', probs, v)
        attn = attn.transpose(0, 2, 1, 3).reshape(B, S, E)
        out = attn @ W_proj + b_proj
        return out

    def _L0_xattn_ref(q, k, v):
        import jax, jax.numpy as jnp
        import numpy as np
        N_HEAD = 8
        b, d, m = q.shape
        c = v.shape[1]
        h = N_HEAD
        qh = q.reshape(b * h, d // h, m)
        kh = k.reshape(b * h, d // h, -1)
        vh = v.reshape(b * h, c // h, -1)
        scale = 1.0 / jnp.sqrt(jnp.asarray(d // h, dtype=q.dtype))
        qk = jnp.einsum('bdm,bdn->bmn', qh, kh) * scale
        sm = jax.nn.softmax(qk, axis=-1)
        ret = jnp.einsum('bmn,bcn->bcm', sm, vh)
        return ret.reshape(b, c, m)

    def _L0_ffn_ref(x, gate_w, up_w, down_w, gate_s, up_s, down_s):
        import jax, jax.numpy as jnp
        import numpy as np
        HIDDEN = 256
        INTER = 704
        B, S = (2, 256)

        def _ternary(key, shape):
            return jax.random.randint(key, shape, -1, 2).astype(jnp.float32)
        b, s, h = x.shape
        xf = x.reshape(b * s, h)
        g = jnp.einsum('th,ih->ti', xf, gate_w) * gate_s
        u = jnp.einsum('th,ih->ti', xf, up_w) * up_s
        hdn = jax.nn.silu(g) * u
        out = jnp.einsum('ti,hi->th', hdn, down_w) * down_s
        return out.reshape(b, s, -1)

    def _L1_attn_ref(x, w_qkv, b_qkv, w_out, b_out):
        import math
        import jax, jax.numpy as jnp
        import numpy as np
        B, N, D_MODEL, H = (2, 512, 256, 16)
        HEAD_DIM = D_MODEL // H
        CHUNK = 128

        def _slopes(n_heads):
            start = 2.0 ** (-2.0 ** (-(math.log2(n_heads) - 3)))
            return np.array([start ** (i + 1) for i in range(n_heads)], dtype=np.float32)

        def _lightning_attn(q, k, v):
            b, h, n, d = q.shape
            nc = n // CHUNK
            lam = jnp.exp(-jnp.asarray(_slopes(h)))
            pos = jnp.arange(CHUNK, dtype=jnp.float32)
            decay_q = lam[:, None] ** (pos + 1.0)
            decay_k = lam[:, None] ** (CHUNK - 1.0 - pos)
            diff = pos[:, None] - pos[None, :]
            causal = diff >= 0
            dmask = jnp.where(causal, lam[:, None, None] ** jnp.maximum(diff, 0.0), 0.0)
            lam_c = lam ** CHUNK

            def to_chunks(t):
                return t.reshape(b, h, nc, CHUNK, d).transpose(2, 0, 1, 3, 4)
            qc, kc, vc = (to_chunks(q), to_chunks(k), to_chunks(v))

            def step(S, inp):
                qb, kb, vb = inp
                inter = jnp.einsum('bhcd,bhde->bhce', qb * decay_q[None, :, :, None], S)
                scores = jnp.einsum('bhcd,bhed->bhce', qb, kb) * dmask[None]
                intra = jnp.einsum('bhce,bhed->bhcd', scores, vb)
                S_new = lam_c[None, :, None, None] * S + jnp.einsum('bhcd,bhce->bhde', kb * decay_k[None, :, :, None], vb)
                return (S_new, inter + intra)
            S0 = jnp.zeros((b, h, d, d), dtype=q.dtype)
            _, out = jax.lax.scan(step, S0, (qc, kc, vc))
            return out.transpose(1, 2, 0, 3, 4).reshape(b, h, n, d)
        b, n, dm = x.shape
        qkv = x @ w_qkv.T + b_qkv
        q, k, v = jnp.split(qkv, 3, axis=-1)

        def heads(t):
            return t.reshape(b, n, H, HEAD_DIM).transpose(0, 2, 1, 3)
        attn = _lightning_attn(heads(q), heads(k), heads(v))
        attn = attn.transpose(0, 2, 1, 3).reshape(b, n, dm)
        return attn @ w_out.T + b_out

    def _L1_xattn_ref(hidden_states, memory_tokens, memory_mask, norm_w, wq, wk, wv, wo, wg):
        import jax, jax.numpy as jnp
        import numpy as np
        H = 256
        NH = 16
        HD = H // NH
        EPS = 1e-06

        def rmsnorm(x, w, eps=EPS):
            var = jnp.mean(x * x, axis=-1, keepdims=True)
            return x * jax.lax.rsqrt(var + eps) * w
        B, L, C = hidden_states.shape
        M = memory_tokens.shape[1]
        scale = HD ** (-0.5)
        x = rmsnorm(hidden_states, norm_w)
        q = (x @ wq.T).reshape(B, L, NH, HD)
        k = (memory_tokens @ wk.T).reshape(B, M, NH, HD)
        v = (memory_tokens @ wv.T).reshape(B, M, NH, HD)
        attn = jnp.einsum('blhd,bmhd->bhlm', q, k) * scale
        attn = jnp.where(memory_mask[:, None, None, :], attn, -jnp.inf)
        attn = jax.nn.softmax(attn, axis=-1)
        attn = jnp.nan_to_num(attn, nan=0.0)
        out = jnp.einsum('bhlm,bmhd->blhd', attn, v).reshape(B, L, C)
        out = out @ wo.T
        gate = jax.nn.sigmoid(x @ wg.T)
        return gate * out

    def _L1_ffn_ref(x, weight, lora_A, lora_B, router_w):
        import jax, jax.numpy as jnp
        import numpy as np
        NUM_EXPERTS = 8
        RANK = 16
        TOP_K = 2
        SCALING = 32.0 / RANK
        IN_F = 256
        OUT_F = 256
        B, T, D = x.shape
        N = B * T
        base = jnp.einsum('btd,od->bto', x, weight)
        logits = jnp.einsum('btd,ed->bte', x, router_w)
        probs = jax.nn.softmax(logits, axis=-1)
        topk_vals, topk_idx = jax.lax.top_k(probs, TOP_K)
        topk_vals = topk_vals / topk_vals.sum(axis=-1, keepdims=True)
        w_dense = jnp.zeros((N, NUM_EXPERTS), dtype=x.dtype).at[jnp.arange(N)[:, None], topk_idx.reshape(N, TOP_K)].set(topk_vals.reshape(N, TOP_K))
        x_flat = x.reshape(N, D)
        Ax = jnp.einsum('nd,erd->ner', x_flat, lora_A)
        expert_out = jnp.einsum('ner,ne,eor->no', Ax, w_dense, lora_B) * SCALING
        return base + expert_out.reshape(B, T, OUT_F)
    x = _layernorm(x + _L0_attn_ref(x, L0_attn_W_attn, L0_attn_b_attn, L0_attn_W_proj, L0_attn_b_proj), axis=-1)
    x = _layernorm(x + _L0_xattn_ref(x, ctx_2048, ctx_2048), axis=-1)
    x = _layernorm(x + _L0_ffn_ref(x, L0_ffn_gate_w, L0_ffn_up_w, L0_ffn_down_w, L0_ffn_gate_s, L0_ffn_up_s, L0_ffn_down_s), axis=-1)
    x = _layernorm(x + _L1_attn_ref(x, L1_attn_w_qkv, L1_attn_b_qkv, L1_attn_w_out, L1_attn_b_out), axis=-1)
    x = _layernorm(x + _L1_xattn_ref(x, ctx_2048, mask_BxS2_bk0, L1_xattn_norm_w, L1_xattn_wq, L1_xattn_wk, L1_xattn_wv, L1_xattn_wo, L1_xattn_wg), axis=-1)
    x = _layernorm(x + _L1_ffn_ref(x, L1_ffn_weight, L1_ffn_lora_A, L1_ffn_lora_B, L1_ffn_router_w), axis=-1)
    return x

_drawn_inputs = setup_inputs


def setup_inputs(seed=0):
    import zlib

    import numpy as np

    out = dict(_drawn_inputs(seed))
    spreads = {'L0_attn_b_attn': (0.0, 0.1), 'L0_attn_b_proj': (0.0, 0.1), 'L1_xattn_norm_w': (1.0, 0.2)}
    factors = {'L1_attn_b_out': 63.957}
    for name, (base, spread) in spreads.items():
        noise = np.random.default_rng([zlib.crc32(name.encode()), seed]).standard_normal(out[name].shape)
        drawn = base * np.exp(spread * noise) if base else spread * noise
        out[name] = jnp.asarray(drawn.astype(out[name].dtype))
    for name, factor in factors.items():
        out[name] = (out[name] * factor).astype(out[name].dtype)
    return out
```

```python
import numpy as np
import concourse.bass as bass
from concourse import mybir
from contextlib import ExitStack

f32, bf16, u8, u32 = mybir.dt.float32, mybir.dt.bfloat16, mybir.dt.uint8, mybir.dt.uint32
ACT = mybir.ActivationFunctionType
ALU = mybir.AluOpType
AX = mybir.AxisListType

B, T, D = 16, 128, 256
U = 4
NIT = B // U
KT = D // 128
H0, HX0, H1 = 32, 8, 16
INTER, FT = 704, 6
E, R = 8, 16
MW = D + E * R + E
NEG = -1e30
LN_EPS, RMS_EPS = 1e-5, 1e-6
SLOPE = 2.0 ** (-8.0 / H0)
SCALE0, SCALEX = float(8) ** -0.5, 0.25
HD0, HD1 = 8, 16
K0 = 9 * HD0
K1 = 6 * HD1

STAGES = ["ctxT", "l0_xT", "l0_qk", "l0_r", "l0_c", "l0_ld", "l0_S", "l0_mx", "l0_P", "l0_n", "l0_o", "l0_ln",
          "x0_a", "x0_r", "x0_c", "x0_ld", "x0_S", "x0_mx", "x0_P", "x0_n", "x0_ln",
          "f_xT", "f_gu", "f_o", "f_ln",
          "l1_xT", "l1_qk", "l1_r", "l1_c", "l1_ld", "l1_P", "l1_n", "l1_o", "l1_ln",
          "c_rms", "c_xT", "c_qk", "c_r", "c_c", "c_ld", "c_S", "c_mx", "c_P", "c_n", "c_o", "c_ln",
          "m_xT", "m_a", "m_b", "m_o", "m_ln"]


def in_order():
    order = []
    for s in STAGES:
        if s in ("m_a", "m_b"):
            continue
        if s == "m_o":
            for u in range(0, U, 2):
                order += [(g, v) for g in ("m_a", "m_b", "m_o") for v in (u, u + 1)]
            continue
        order += [(s, u) for u in range(U)]
    return order


ORDER = in_order()

SLOTS = {"sc": 2, "pr": 2, "o": 2, "p": 3}
TAKES = {
    "sc": {"l0_S": 4, "l0_P": 4, "x0_S": 4, "x0_P": 4, "f_gu": 2, "l1_P": 2, "c_S": 2, "c_P": 2, "m_a": 1},
    "pr": {"ctxT": 1, "l0_xT": 1, "l0_qk": 2, "l0_mx": 1, "l0_o": 1, "x0_mx": 1, "f_xT": 1, "f_o": 1, "l1_xT": 1,
           "l1_qk": 2, "l1_o": 1, "c_xT": 1, "c_qk": 2, "c_mx": 1, "c_o": 1, "m_xT": 1, "m_b": 1},
    "o": {"l0_P": 1, "x0_P": 1, "l1_P": 1, "c_P": 1},
    "p": {"l0_P": 4, "x0_P": 4, "l1_P": 2, "c_P": 2},
}


def first_use():
    at, total = {}, {}
    for ring, takes in TAKES.items():
        n = 0
        for stage, u in ORDER:
            at[ring, stage, u] = n
            n += takes.get(stage, 0)
        assert n % SLOTS[ring] == 0
        total[ring] = n
    return at, total


RING_AT, RING_TOTAL = first_use()

X_USE = {"l0": 1, "x0": 2, "f": 3, "l1": 4, "c": 5}
SPLIT_USE = {"l0": 1, "x0": 2, "l1": 3, "c": 4}
MAX_USE = {"l0": 1, "x0": 2, "c": 3}
NORM_USE = {"l0": 1, "x0": 2, "f": 3, "l1": 4, "c_rms": 5, "c": 6, "m": 7}
LOADS_UP_TO = {"l0": 5, "x0": 11, "l1": 17, "c": 23}
VEC_STEPS = 144


def decoder_kernel(nc, t, out):
    ctx = ExitStack()
    with ctx:
        def sb(name, shape, dt=f32):
            return ctx.enter_context(nc.sbuf_tensor(name, shape, dt))

        def sem(name):
            return ctx.enter_context(nc.semaphore(name))

        def per_u(name):
            return [sem(f"{name}{u}") for u in range(U)]

        w_qk0, w_v0, w_p0 = sb("w_qk0", [128, KT, 512]), sb("w_v0", [128, KT, D]), sb("w_p0", [128, KT, D])
        w_gu, w_dn = sb("w_gu", [128, KT, 2 * FT * 128]), sb("w_dn", [128, FT, D])
        w_qk1, w_v1, w_o1 = sb("w_qk1", [128, KT, 512]), sb("w_v1", [128, KT, D]), sb("w_o1", [128, KT, D])
        w_qkc, w_vgc, w_oc = sb("w_qkc", [128, KT, 512]), sb("w_vgc", [128, KT, 512]), sb("w_oc", [128, KT, D])
        w_m, w_b = sb("w_m", [128, KT, MW]), sb("w_b", [128, D])
        b_qk0, b_qk1 = sb("b_qk0", [128, 4]), sb("b_qk1", [128, 4])
        bc_v0, bc_p0, bc_v1, bc_o1 = (sb(n, [128, D]) for n in ("bc_v0", "bc_p0", "bc_v1", "bc_o1"))
        norm_w = sb("norm_w", [128, KT])
        ident, identb = sb("ident", [128, 128]), sb("identb", [128, 128], bf16)
        decay = sb("decay", [128, H1, 128])
        causal_kq, alibi_qk = sb("causal_kq", [128, 128], bf16), sb("alibi_qk", [128, 128], bf16)
        key_bias, iota8 = sb("key_bias", [128, 1]), sb("iota8", [128, E])
        ones8, ones16 = sb("ones8", [128, 4, 32]), sb("ones16", [128, 2, 32])
        ones_row, minus_half = sb("ones_row", [1, 128], bf16), sb("minus_half", [128, 1])

        xc = [sb(f"xc{u}", [128, 2 * D]) for u in range(U)]
        ct = [sb(f"ct{u}", [128, KT, 128]) for u in range(U)]
        xt = [sb(f"xt{u}", [128, KT, 128]) for u in range(U)]
        qf = [sb(f"qf{u}", [128, 512]) for u in range(U)]
        pt = [sb(f"pt{u}", [128, 3, 512], bf16) for u in range(U)]
        sq = [sb(f"sq{u}", [128, 4096], bf16) for u in range(U)]
        sk = [sb(f"sk{u}", [128, 4096], bf16) for u in range(U)]
        v0 = [sb(f"v0{u}", [128, H0, 32]) for u in range(U)]
        vb = [sb(f"vb{u}", [128, H1, 32]) for u in range(U)]
        yb = [sb(f"yb{u}", [128, D]) for u in range(U)]
        nm = [sb(f"nm{u}", [128, H0]) for u in range(U)]
        st = [sb(f"st{u}", [128, 40]) for u in range(U)]
        ix = [sb(f"ix{u}", [128, 8], u32) for u in range(U)]
        mk8 = [sb(f"mk8{u}", [128, 1], u8) for u in range(U)]
        mr8 = [sb(f"mr8{u}", [1, 128], u8) for u in range(U)]
        mk = [sb(f"mk{u}", [128, 1]) for u in range(U)]
        mr = [sb(f"mr{u}", [1, 128], bf16) for u in range(U)]
        pb = sb("pb", [128, SLOTS["p"], 1024])

        sc = ctx.enter_context(nc.psum_tensor("sc", [128, 2, 1024], f32))
        pr = ctx.enter_context(nc.psum_tensor("pr", [128, 2, 512], f32))
        ob = ctx.enter_context(nc.psum_tensor("ob", [128, 2, 512], f32))
        scratch = [nc.dram_tensor(f"scratch{u}", (2 * 3 * 128 * 256,), bf16, kind="Internal").ap() for u in range(U)]

        ring_full = {r: [sem(f"{r}_full{i}") for i in range(n)] for r, n in SLOTS.items()}
        ring_free = {r: [sem(f"{r}_free{i}") for i in range(n)] for r, n in SLOTS.items()}
        w_loaded, scales_loaded, w_scaled = sem("w_loaded"), sem("scales_loaded"), sem("w_scaled")
        pads_zero, ones_set, keys_ones = sem("pads_zero"), sem("ones_set"), sem("keys_ones")
        vec_held, sp_held = sem("vec_held"), sem("sp_held")
        in_loaded, out_stored = per_u("in_loaded"), per_u("out_stored")
        x_ready, xn_ready = per_u("x_ready"), per_u("xn_ready")
        pa_ready, r_ready = per_u("pa_ready"), per_u("r_ready")
        pb_ready, parts_ready = per_u("pb_ready"), per_u("parts_ready")
        parts_stored, stack_loaded = per_u("parts_stored"), per_u("stack_loaded")
        ct_ready = per_u("ct_ready")
        mh_ready, max_loaded = per_u("mh_ready"), per_u("max_loaded")
        var_ready, rstd_ready, xb_ready = per_u("var_ready"), per_u("rstd_ready"), per_u("xb_ready")
        tanh_ready, mask_ready = per_u("tanh_ready"), per_u("mask_ready")
        gap_ready, egap_ready, axw_ready, axt_ready = per_u("gap_ready"), per_u("egap_ready"), per_u("axw_ready"), per_u("axt_ready")
        expert_ready, o_ready, vec_step = per_u("expert_ready"), per_u("o_ready"), sem("vec_step")

        wide_masks = [pb[:, 2, D + 128 * i:D + 128 * i + 128] for i in range(2)]
        weights = [(w_qk0, "w_qk0"), (w_v0, "w_v0"), (w_p0, "w_p0"), (w_gu, "w_gu"), (w_dn, "w_dn"), (w_qk1, "w_qk1"),
                   (w_v1, "w_v1"), (w_o1, "w_o1"), (w_qkc, "w_qkc"), (w_vgc, "w_vgc"), (w_oc, "w_oc"), (w_m, "w_m")]
        plain = [(w_b, "w_b"), (b_qk0, "b_qk0"), (b_qk1, "b_qk1"), (ident, "ident"), (decay, "decay"), (wide_masks[0], "causal_kq"),
                 (wide_masks[1], "alibi_qk"), (key_bias, "key_bias"), (iota8, "iota8"),
                 (ones8, "ones8"), (ones16, "ones16"), (norm_w, "norm_w")]
        spread = [(bc_v0, "b_v0"), (bc_p0, "b_p0"), (bc_v1, "b_v1"), (bc_o1, "b_o1")]
        N_SCALED = 2 + 4 * KT + FT + 3 + 1 + 2 * KT
        N_W = 16 * (len(weights) + len(plain) + len(spread))
        bc_gs, bc_us, bc_ds = pb[:, 0, 0:FT * 128], pb[:, 1, 0:FT * 128], pb[:, 2, 0:D]

        def ffn_space(u):
            return qf[u][:, :], pt[u][:, :, :].rearrange("p a n -> p (a n)").bitcast(f32)[:, 0:D]

        def on_all(name, n):
            return bass.AP(t[name].tensor, 0, [[0, 128], [1, n]])

        def flat(tensor, u_offset, *dims):
            return bass.AP(tensor, u_offset, [list(d) for d in dims])

        def pads(tensor, blocks, per, width):
            return bass.AP(tensor, 0, [[blocks * per * 32, 128], [per * 32, blocks], [32 + width, per], [1, width]])

        def at_slot(ring, stage, u, k=0):
            n = RING_AT[ring, stage, u] + k
            return n % SLOTS[ring], n // SLOTS[ring]

        def wait_full(eng, it, ring, stage, u, k=0):
            slot, before = at_slot(ring, stage, u, k)
            eng.wait_ge(ring_full[ring][slot], it * (RING_TOTAL[ring] // SLOTS[ring]) + (before + 1))
            return slot

        def wait_free(eng, it, ring, stage, u, k=0):
            slot, before = at_slot(ring, stage, u, k)
            eng.wait_ge(ring_free[ring][slot], it * (RING_TOTAL[ring] // SLOTS[ring]) + (before + 1))
            return slot

        def wait_attended(eng, it, stage, u):
            p, before = at_slot("p", stage, u, TAKES["p"][stage] - 1)
            eng.wait_ge(ring_free["p"][p], it * (RING_TOTAL["p"] // SLOTS["p"]) + (before + 2))
            return at_slot("o", stage, u)[0]

        def wait_use(eng, it, semaphore, use, per_iteration, step=1):
            eng.wait_ge(semaphore, it * (per_iteration * step) + use * step)

        block = ctx.enter_context(nc.Block())

        @block.sync
        def _(sp):
            sp.dma_start(bc_gs[:, 0:INTER], on_all("gate_s", INTER)).then_inc(scales_loaded, 16)
            sp.dma_start(bc_us[:, 0:INTER], on_all("up_s", INTER)).then_inc(scales_loaded, 16)
            sp.dma_start(bc_ds, on_all("down_s", D)).then_inc(scales_loaded, 16)
            for dst, name in weights:
                sp.dma_start(dst[:, :, :], t[name].rearrange("(k p) n -> p k n", p=128)).then_inc(w_loaded, 16)
            for dst, name in plain:
                dims = "p a b -> p (a b)"
                d = dst[:, :, :].rearrange(dims) if len(dst.shape) == 3 else dst[:, :]
                s = t[name].rearrange(dims) if len(dst.shape) == 3 else t[name]
                sp.dma_start(d, s).then_inc(w_loaded, 16)
            for dst, name in spread:
                sp.dma_start(dst[:, :], on_all(name, D)).then_inc(w_loaded, 16)

            def store_parts(it, u, layer, hd):
                wait_use(sp, it, parts_ready[u], SPLIT_USE[layer], 4)
                row = 128 // hd * 256
                for c in range(3):
                    for side in range(2):
                        dst = flat(scratch[u].tensor, (3 * side + c) * hd * row, (256, 128 // hd), (row, hd), (1, 256))
                        sp.dma_start(dst, pt[u][:, c, 256 * side:256 * side + 256]).then_inc(parts_stored[u], 16)

            def load_stacks(it, u, layer):
                wait_use(sp, it, parts_stored[u], SPLIT_USE[layer], 4, 96)
                dram = scratch[u].tensor
                if layer == "l0":
                    row, keys = 4096, 3 * 8 * 4096
                    for c in range(3):
                        sp.dma_start(sq[u][24 * c:24 * c + 24, :], flat(dram, c * 8 * row, (0, 3), (row, 8), (1, row)))\
                          .then_inc(stack_loaded[u], 16)
                    sp.dma_start(sk[u][0:72, :], flat(dram, keys, (0, 3), (row, 24), (1, row))).then_inc(stack_loaded[u], 16)
                    sp.dma_start(sk[u][72:74, :], sk[u][96:98, :]).then_inc(stack_loaded[u], 16)
                    return
                row, part, keys = 2048, 16 * 2048, 3 * 16 * 2048
                for first, n, c in ((0, 3, 0), (48, 2, 1), (80, 1, 2)):
                    sp.dma_start(sq[u][first:first + 16 * n, 0:2048], flat(dram, c * part, (0, n), (row, 16), (1, row)))\
                      .then_inc(stack_loaded[u], 16)
                    sp.dma_start(sk[u][first:first + 16 * n, 0:2048], flat(dram, keys, (row, 16 * n), (1, row)))\
                      .then_inc(stack_loaded[u], 16)

            def load_max(it, u, layer, rows, first):
                slot, before = at_slot("pr", f"{layer}_mx", u)
                sp.wait_ge(ring_free["pr"][slot], it * (RING_TOTAL["pr"] // 2) + (before + 2))
                for j in range(2):
                    sp.dma_start(sq[u][first + j:first + j + 1, 0:rows * 128], pt[u][0:rows, j, 0:128])\
                      .then_inc(max_loaded[u], 16)

            sp.wait_ge(keys_ones, U)
            with sp.Fori(0, NIT) as it:
                for u in range(U):
                    b = it * U + u
                    sp.dma_start(xc[u][:, 0:D], t["x"][b]).then_inc(in_loaded[u], 16)
                    sp.dma_start(xc[u][:, D:2 * D], t["ctx"][b]).then_inc(in_loaded[u], 16)
                    sp.dma_start(mk8[u][:, :], t["mask_col"][b]).then_inc(in_loaded[u], 16)
                    sp.dma_start(mr8[u][:, :], t["mask_row"][b]).then_inc(in_loaded[u], 16)
                for stage, u in ORDER:
                    if stage == "l0_c":
                        store_parts(it, u, "l0", HD0)
                    elif stage in ("x0_c", "l1_c", "c_c"):
                        store_parts(it, u, stage[:-2], HD1)
                    elif stage in ("l0_ld", "x0_ld", "l1_ld", "c_ld"):
                        load_stacks(it, u, stage[:-3])
                    elif stage == "l0_mx":
                        load_max(it, u, "l0", H0, K0)
                    elif stage in ("x0_mx", "c_mx"):
                        load_max(it, u, stage[:-3], 16, K1)
                    elif stage == "m_ln":
                        wait_use(sp, it, o_ready[u], 1, 1)
                        sp.dma_start(out[it * U + u], qf[u][:, 0:D]).then_inc(out_stored[u], 16)
                for u in range(U):
                    wait_use(sp, it, out_stored[u], 1, 1, 16)
                    sp.sem_inc(sp_held, 1)

        @block.gpsimd
        def _(pool):
            for u in range(U):
                nc.gpsimd.memset(v0[u][:, :, :], 0.0).then_inc(pads_zero, 1)
                nc.gpsimd.memset(vb[u][:, :, :], 0.0).then_inc(pads_zero, 1)
            nc.gpsimd.memset(ones_row[:, :], 1.0).then_inc(ones_set, 1)
            nc.gpsimd.memset(minus_half[:, :], -0.5).then_inc(ones_set, 1)
            pool.wait_ge(w_loaded, N_W)
            pool.wait_ge(ones_set, 2)

            def rstd(it, u, layer):
                wait_use(pool, it, var_ready[u], NORM_USE[layer], 7)
                nc.gpsimd.tensor_tensor(st[u][:, 11:12], st[u][:, 10:11], minus_half[:, :], ALU.pow).then_inc(rstd_ready[u], 1)

            with pool.Fori(0, NIT) as it:
                for stage, u in ORDER:
                    if stage == "l0_xT":
                        wait_use(pool, it, in_loaded[u], 4, 4, 16)
                        nc.gpsimd.tensor_tensor(yb[u][:, :], xc[u][:, 0:D], bc_p0[:, :], ALU.add).then_inc(xb_ready[u], 1)
                    elif stage == "l1_xT":
                        wait_use(pool, it, x_ready[u], X_USE["f"], 5)
                        nc.gpsimd.tensor_tensor(yb[u][:, :], xc[u][:, 0:D], bc_o1[:, :], ALU.add).then_inc(xb_ready[u], 1)
                    elif stage in ("l0_o", "f_o", "l1_o", "c_o", "m_o"):
                        rstd(it, u, stage[:-2])
                    elif stage == "x0_n":
                        rstd(it, u, "x0")
                    elif stage == "c_rms":
                        rstd(it, u, "c_rms")

        @block.scalar
        def _(act):
            act.wait_ge(w_loaded, N_W)
            act.wait_ge(pads_zero, 2 * U)

            def transposed(it, u, stage, dst, ready):
                slot = wait_full(act, it, "pr", stage, u)
                src = pr[:, slot, 0:D].rearrange("p (k n) -> p k n", k=KT)
                nc.scalar.activation(dst[:, :, :], src, ACT.Copy).then_inc(ready, 1)
                return slot

            def second_part(it, u, layer):
                wait_use(act, it, r_ready[u], SPLIT_USE[layer], 4)
                nc.scalar.activation(pt[u][:, 1, :], qf[u][:, :], ACT.Copy).then_inc(pb_ready[u], 1)

            def max_high(it, u, layer, rows):
                slot = wait_full(act, it, "pr", f"{layer}_mx", u)
                nc.scalar.activation(pt[u][0:rows, 0, 0:128], pr[0:rows, slot, 0:128], ACT.Copy).then_inc(mh_ready[u], 1)

            def exps(it, u, layer, chunks, scale, bias):
                for c in range(chunks):
                    s = wait_full(act, it, "sc", f"{layer}_P", u, c)
                    p = wait_free(act, it, "p", f"{layer}_P", u, c)
                    nc.scalar.activation(pb[:, p, :], sc[:, s, :], ACT.Exp, bias=bias, scale=scale)\
                      .then_inc(ring_full["p"][p], 1)

            with act.Fori(0, NIT) as it:
                for stage, u in ORDER:
                    if stage == "ctxT":
                        slot = transposed(it, u, stage, ct[u], ct_ready[u])
                        src = pr[:, slot, 0:D].rearrange("p (b h c) -> p b h c", b=8, h=2)
                        nc.scalar.activation(pads(vb[u], 8, 2, 16), src, ACT.Copy).then_inc(ring_free["pr"][slot], 1)
                    elif stage in ("l0_xT", "f_xT", "l1_xT", "c_xT", "m_xT"):
                        slot = wait_full(act, it, "pr", stage, u)
                        src = pr[:, slot, 0:D].rearrange("p (k n) -> p k n", k=KT)
                        nc.scalar.activation(xt[u][:, :, :], src, ACT.Copy).then_inc(ring_free["pr"][slot], 1)
                    elif stage in ("l0_qk", "l1_qk"):
                        slot, before = at_slot("pr", stage, u, 0)
                        act.wait_ge(ring_free["pr"][slot], it * (RING_TOTAL["pr"] // 2) + (before + 2))
                        nc.scalar.activation(pt[u][:, 0, :], qf[u][:, :], ACT.Copy).then_inc(pa_ready[u], 1)
                    elif stage == "x0_a":
                        wait_use(act, it, x_ready[u], X_USE["l0"], 5)
                        nc.scalar.activation(pt[u][:, 0, :], xc[u][:, :], ACT.Copy).then_inc(pa_ready[u], 1)
                    elif stage == "c_qk":
                        slot = wait_full(act, it, "pr", stage, u, 0)
                        nc.scalar.activation(pt[u][:, 0, :], pr[:, slot, :], ACT.Copy).then_inc(pa_ready[u], 1)
                        slot = wait_full(act, it, "pr", stage, u, 1)
                        src = pr[:, slot, 0:D].rearrange("p (b h c) -> p b h c", b=8, h=2)
                        nc.scalar.activation(pads(vb[u], 8, 2, 16), src, ACT.Copy)
                        nc.scalar.activation(yb[u][:, :], pr[:, slot, D:2 * D], ACT.Tanh, scale=0.5).then_inc(ring_free["pr"][slot], 1)
                    elif stage in ("l0_r", "x0_r", "l1_r", "c_r"):
                        second_part(it, u, stage[:-2])
                    elif stage == "l0_mx":
                        max_high(it, u, "l0", H0)
                    elif stage in ("x0_mx", "c_mx"):
                        max_high(it, u, stage[:-3], 16)
                    elif stage == "l0_P":
                        exps(it, u, "l0", 4, SCALE0, key_bias[:, 0:1])
                    elif stage == "x0_P":
                        exps(it, u, "x0", 4, SCALEX, 0.0)
                    elif stage == "c_P":
                        wait_use(act, it, mask_ready[u], 1, 1)
                        exps(it, u, "c", 2, SCALEX, mk[u][:, 0:1])
                    elif stage == "f_gu":
                        for c in range(2):
                            n = 512 if c == 0 else 256
                            s = wait_full(act, it, "sc", stage, u, c)
                            nc.scalar.activation(ffn_space(u)[c], sc[:, s, 0:n], ACT.Tanh, scale=0.5).then_inc(tanh_ready[u], 1)
                    elif stage == "l1_n":
                        slot = wait_attended(act, it, "l1_P", u)
                        src = ob[:, slot, 0:D].rearrange("p (k n) -> p k n", k=KT)
                        nc.scalar.activation(xt[u][:, :, :], src, ACT.Copy).then_inc(ring_free["o"][slot], 1)
                    elif stage == "m_a":
                        wait_use(act, it, gap_ready[u], 1, 1)
                        nc.scalar.activation(st[u][:, 20:21], st[u][:, 19:20], ACT.Exp).then_inc(egap_ready[u], 1)
                    elif stage == "m_b":
                        slot = wait_full(act, it, "pr", stage, u)
                        nc.scalar.activation(yb[u][:, 128:256], pr[:, slot, 0:128], ACT.Copy).then_inc(ring_free["pr"][slot], 1)

        @block.vector
        def _(dve):
            for r, n in SLOTS.items():
                for i in range(n):
                    dve.sem_inc(ring_free[r][i], 1)
            for u in range(U):
                nc.vector.memset(sk[u][96:98, :], 1.0).then_inc(keys_ones, 1)
            dve.wait_ge(w_loaded, N_W)
            dve.wait_ge(scales_loaded, 48)
            nc.vector.memset(pb[:, 0, INTER:FT * 128], 0.0).then_inc(w_scaled, 1)
            nc.vector.memset(pb[:, 1, INTER:FT * 128], 0.0).then_inc(w_scaled, 1)
            dve.wait_ge(w_scaled, 2)
            for k in range(KT):
                for first, tiles, scales, tile in ((0, 4, bc_gs, 0), (512, 4, bc_us, 0), (1024, 2, bc_gs, 4), (1280, 2, bc_us, 4)):
                    cols = w_gu[:, k, first:first + 128 * tiles]
                    nc.vector.tensor_tensor(cols, cols, scales[:, 128 * tile:128 * (tile + tiles)], ALU.mult).then_inc(w_scaled, 1)
            for j in range(FT):
                nc.vector.scalar_tensor_tensor(w_dn[:, j, :], w_dn[:, j, :], 0.5, bc_ds, ALU.mult, ALU.mult).then_inc(w_scaled, 1)
            for narrow, wide in ((causal_kq, wide_masks[0]), (alibi_qk, wide_masks[1]), (identb, ident)):
                nc.vector.tensor_copy(narrow[:, :], wide[:, :]).then_inc(w_scaled, 1)
            nc.vector.tensor_scalar(w_oc[:, :, :], w_oc[:, :, :], 0.5, None, ALU.mult).then_inc(w_scaled, 1)
            for k in range(KT):
                for cols in (w_qkc[:, k, 0:D], w_vgc[:, k, D:2 * D]):
                    nc.vector.tensor_scalar(cols, cols, norm_w[:, k:k + 1], None, ALU.mult).then_inc(w_scaled, 1)
            dve.wait_ge(w_scaled, N_SCALED)
            dve.wait_ge(pads_zero, 2 * U)

            with dve.Fori(0, NIT) as it:
                steps = [0]

                def link(ins):
                    ins.then_inc(vec_step, 1)
                    steps[0] += 1
                    dve.wait_ge(vec_step, it * VEC_STEPS + steps[0])

                def link_alone(ins):
                    link(ins)
                    dve.sem_inc(vec_held, 1)

                def residual(it, u, layer, use):
                    wait_use(dve, it, pa_ready[u], use, 4)
                    nc.vector.tensor_tensor(qf[u][:, :], qf[u][:, :], pt[u][:, 0, :], ALU.subtract).then_inc(r_ready[u], 1)

                def third_part(it, u, layer):
                    wait_use(dve, it, pb_ready[u], SPLIT_USE[layer], 4)
                    nc.vector.tensor_tensor(pt[u][:, 2, :], qf[u][:, :], pt[u][:, 1, :], ALU.subtract).then_inc(parts_ready[u], 1)

                def statistics(u, src, eps):
                    link_alone(nc.vector.bn_stats(st[u][:, 0:6], src))
                    link(nc.vector.bn_aggr(st[u][:, 8:10], st[u][:, 0:6]))
                    nc.vector.tensor_scalar(st[u][:, 10:11], st[u][:, 9:10], eps, None, ALU.add).then_inc(var_ready[u], 1)

                def layer_norm(it, u, layer, dst, ready):
                    wait_use(dve, it, rstd_ready[u], NORM_USE[layer], 7)
                    nc.vector.tensor_scalar(dst, yb[u][:, :], st[u][:, 8:9], st[u][:, 11:12], ALU.subtract, ALU.mult)\
                      .then_inc(ready, 1)

                def maxima(it, u, layer, chunks):
                    for c in range(chunks):
                        s = wait_full(dve, it, "sc", f"{layer}_S", u, c)
                        if layer == "l0":
                            half, i0 = c // 2, 2 * (c % 2)
                            dst = nm[u][:, :].rearrange("p (t g i) -> p t i g", t=2, g=4)[:, half, i0:i0 + 2, :]
                            src = sc[:, s, :].rearrange("p (i g n) -> p i g n", i=2, g=4)
                        elif layer == "x0":
                            dst = nm[u][:, 4 * c:4 * c + 4]
                            src = sc[:, s, :].rearrange("p (a n) -> p a n", a=4)
                        else:
                            dst = nm[u][:, 8 * c:8 * c + 8]
                            src = sc[:, s, :].rearrange("p (a n) -> p a n", a=8)
                        ins = nc.vector.tensor_reduce(dst, src, AX.X, ALU.max, negate=True)
                        ins.then_inc(ring_free["sc"][s], 1)

                def max_low(it, u, layer, rows):
                    slot, _ = at_slot("pr", f"{layer}_mx", u)
                    wait_use(dve, it, mh_ready[u], MAX_USE[layer], 3)
                    nc.vector.tensor_tensor(pt[u][0:rows, 1, 0:128], pr[0:rows, slot, 0:128], pt[u][0:rows, 0, 0:128], ALU.subtract)\
                      .then_inc(ring_free["pr"][slot], 1)

                def add_residual(it, u, stage, x):
                    slot = wait_full(dve, it, "pr", stage, u)
                    ins = nc.vector.tensor_tensor(yb[u][:, :], pr[:, slot, 0:D], x, ALU.add)
                    ins.then_inc(ring_free["pr"][slot], 1)
                    slot, before = at_slot("pr", stage, u)
                    dve.wait_ge(ring_free["pr"][slot], it * (RING_TOTAL["pr"] // 2) + (before + 2))

                for stage, u in ORDER:
                    x = xc[u][:, 0:D]
                    if stage == "ctxT":
                        wait_use(dve, it, in_loaded[u], 4, 4, 16)
                        nc.vector.tensor_scalar(mr[u][:, :], mr8[u][:, :], -1.0, -NEG, ALU.add, ALU.mult).then_inc(mask_ready[u], 1)
                        nc.vector.tensor_scalar(mk[u][:, :], mk8[u][:, :], -1.0, -NEG, ALU.add, ALU.mult).then_inc(mask_ready[u], 1)
                    elif stage in ("l0_qk", "l1_qk"):
                        layer = stage[:-3]
                        b_qk, bc_v = (b_qk0, bc_v0) if layer == "l0" else (b_qk1, bc_v1)
                        slot = wait_full(dve, it, "pr", stage, u, 0)
                        src = pr[:, slot, :].rearrange("p (a n) -> p a n", a=4)
                        bias = b_qk[:, :].unsqueeze(2).broadcast_to([128, 4, 128])
                        nc.vector.tensor_tensor(qf[u][:, :].rearrange("p (a n) -> p a n", a=4), src, bias, ALU.add)\
                          .then_inc(ring_free["pr"][slot], 1)
                        slot = wait_full(dve, it, "pr", stage, u, 1)
                        if layer == "l0":
                            dst, dims, kw = pads(v0[u], 8, 4, 8), "p (b h c) -> p b h c", dict(b=8, h=4)
                        else:
                            dst, dims, kw = pads(vb[u], 8, 2, 16), "p (b h c) -> p b h c", dict(b=8, h=2)
                        nc.vector.tensor_tensor(dst, pr[:, slot, 0:D].rearrange(dims, **kw), bc_v[:, :].rearrange(dims, **kw), ALU.add)\
                          .then_inc(ring_free["pr"][slot], 1)
                    elif stage in ("l0_r", "l1_r"):
                        residual(it, u, stage[:-2], SPLIT_USE[stage[:-2]])
                    elif stage == "x0_r":
                        wait_use(dve, it, pa_ready[u], SPLIT_USE["x0"], 4)
                        nc.vector.tensor_tensor(qf[u][:, :], xc[u][:, :], pt[u][:, 0, :], ALU.subtract).then_inc(r_ready[u], 1)
                    elif stage == "c_r":
                        wait_use(dve, it, pa_ready[u], SPLIT_USE["c"], 4)
                        slot, _ = at_slot("pr", "c_qk", u, 0)
                        link(nc.vector.tensor_tensor(qf[u][:, :], pr[:, slot, :], pt[u][:, 0, :], ALU.subtract))
                        dve.sem_inc(ring_free["pr"][slot], 1)
                        dve.sem_inc(r_ready[u], 1)
                    elif stage in ("l0_c", "x0_c", "l1_c", "c_c"):
                        third_part(it, u, stage[:-2])
                    elif stage in ("l0_S", "x0_S", "c_S"):
                        maxima(it, u, stage[:-2], 2 if stage == "c_S" else 4)
                    elif stage in ("l0_mx", "x0_mx", "c_mx"):
                        max_low(it, u, stage[:-3], H0 if stage == "l0_mx" else 16)
                    elif stage == "l0_n":
                        slot = wait_attended(dve, it, "l0_P", u)
                        link(nc.vector.reciprocal(qf[u][:, 0:D], ob[:, slot, D:2 * D]))
                        nc.vector.tensor_tensor(xt[u][:, :, :].rearrange("p k n -> p (k n)"), ob[:, slot, 0:D], qf[u][:, 0:D], ALU.mult)\
                          .then_inc(ring_free["o"][slot], 1)
                    elif stage == "x0_n":
                        slot = wait_attended(dve, it, "x0_P", u)
                        link(nc.vector.reciprocal(qf[u][:, 0:D], ob[:, slot, D:2 * D]))
                        link(nc.vector.tensor_tensor(yb[u][:, :], ob[:, slot, 0:D], qf[u][:, 0:D], ALU.mult))
                        dve.sem_inc(ring_free["o"][slot], 1)
                        link(nc.vector.tensor_tensor(yb[u][:, :], yb[u][:, :], x, ALU.add))
                        statistics(u, yb[u][:, :], LN_EPS)
                    elif stage == "c_n":
                        slot = wait_attended(dve, it, "c_P", u)
                        link(nc.vector.tensor_scalar(qf[u][:, D:2 * D], ob[:, slot, D:2 * D], 1e-30, None, ALU.max))
                        link(nc.vector.reciprocal(qf[u][:, 0:D], qf[u][:, D:2 * D]))
                        nc.vector.tensor_tensor(xt[u][:, :, :].rearrange("p k n -> p (k n)"), ob[:, slot, 0:D], qf[u][:, 0:D], ALU.mult)\
                          .then_inc(ring_free["o"][slot], 1)
                    elif stage in ("l0_o", "l1_o"):
                        wait_use(dve, it, xb_ready[u], 1 if stage == "l0_o" else 2, 2)
                        add_residual(it, u, stage, yb[u][:, :])
                        statistics(u, yb[u][:, :], LN_EPS)
                    elif stage == "f_o":
                        add_residual(it, u, stage, x)
                        statistics(u, yb[u][:, :], LN_EPS)
                    elif stage == "c_o":
                        slot = wait_full(dve, it, "pr", stage, u)
                        link(nc.vector.scalar_tensor_tensor(yb[u][:, :], yb[u][:, :], 1.0, pr[:, slot, 0:D], ALU.add, ALU.mult))
                        dve.sem_inc(ring_free["pr"][slot], 1)
                        link(nc.vector.tensor_tensor(yb[u][:, :], yb[u][:, :], x, ALU.add))
                        statistics(u, yb[u][:, :], LN_EPS)
                    elif stage in ("l0_ln", "x0_ln", "f_ln", "l1_ln", "c_ln"):
                        layer_norm(it, u, stage[:-3], x, x_ready[u])
                    elif stage == "c_rms":
                        wait_use(dve, it, x_ready[u], X_USE["l1"], 5)
                        link_alone(nc.vector.bn_stats(st[u][:, 0:6], x))
                        link(nc.vector.bn_aggr(st[u][:, 8:10], st[u][:, 0:6]))
                        link(nc.vector.scalar_tensor_tensor(st[u][:, 12:13], st[u][:, 8:9], st[u][:, 8:9], st[u][:, 9:10], ALU.mult, ALU.add))
                        nc.vector.tensor_scalar(st[u][:, 10:11], st[u][:, 12:13], RMS_EPS, None, ALU.add).then_inc(var_ready[u], 1)
                    elif stage == "c_xT":
                        wait_use(dve, it, rstd_ready[u], NORM_USE["c_rms"], 7)
                        nc.vector.tensor_scalar(yb[u][:, :], x, st[u][:, 11:12], None, ALU.mult)\
                          .then_inc(xn_ready[u], 1)
                    elif stage == "f_gu":
                        ht = sq[u][:, :].bitcast(f32)
                        for c in range(2):
                            n, first = (512, 0) if c == 0 else (256, 512)
                            s, _ = at_slot("sc", stage, u, c)
                            space = ffn_space(u)[c]
                            wait_use(dve, it, tanh_ready[u], c + 1, 2)
                            link(nc.vector.scalar_tensor_tensor(space, space, 1.0, sc[:, s, 0:n], ALU.add, ALU.mult))
                            nc.vector.tensor_tensor(ht[:, first:first + n], space, sc[:, s, n:2 * n], ALU.mult)\
                              .then_inc(ring_free["sc"][s], 1)
                    elif stage == "l1_P":
                        for c in range(2):
                            s = wait_full(dve, it, "sc", stage, u, c)
                            p = wait_free(dve, it, "p", stage, u, c)
                            nc.vector.tensor_tensor(pb[:, p, :], sc[:, s, :], decay[:, 8 * c:8 * c + 8, :].rearrange("p h n -> p (h n)"), ALU.mult)\
                              .then_inc(ring_full["p"][p], 1)
                    elif stage == "m_a":
                        s = wait_full(dve, it, "sc", stage, u)
                        dve.sem_inc(vec_held, 1)
                        logits = sc[:, s, MW - E:MW]
                        link_alone(nc.vector.max(st[u][:, 24:32], logits))
                        link(nc.vector.max_index(ix[u][:, :], st[u][:, 24:32], logits))
                        link(nc.vector.tensor_copy(st[u][:, 32:34], ix[u][:, 0:2]))
                        nc.vector.tensor_tensor(st[u][:, 19:20], st[u][:, 25:26], st[u][:, 24:25], ALU.subtract).then_inc(gap_ready[u], 1)
                    elif stage == "m_b":
                        s, _ = at_slot("sc", "m_a", u)
                        wait_use(dve, it, egap_ready[u], 1, 1)
                        link(nc.vector.tensor_scalar(st[u][:, 21:22], st[u][:, 20:21], 1.0, 0.5, ALU.add, ALU.mult))
                        link(nc.vector.reciprocal(st[u][:, 22:23], st[u][:, 21:22]))
                        link(nc.vector.tensor_tensor(st[u][:, 23:24], st[u][:, 22:23], st[u][:, 20:21], ALU.mult))
                        link(nc.vector.tensor_scalar(st[u][:, 0:8], iota8[:, :], st[u][:, 32:33], st[u][:, 22:23], ALU.is_equal, ALU.mult))
                        link(nc.vector.tensor_scalar(st[u][:, 24:32], iota8[:, :], st[u][:, 33:34], st[u][:, 23:24], ALU.is_equal, ALU.mult))
                        link(nc.vector.tensor_tensor(st[u][:, 0:8], st[u][:, 0:8], st[u][:, 24:32], ALU.add))
                        nc.vector.tensor_tensor(yb[u][:, 0:128].rearrange("p (e r) -> p e r", e=E),
                                                sc[:, s, D:D + E * R].rearrange("p (e r) -> p e r", e=E),
                                                st[u][:, 0:8].unsqueeze(2).broadcast_to([128, E, R]), ALU.mult).then_inc(axw_ready[u], 1)
                    elif stage == "m_o":
                        s, _ = at_slot("sc", "m_a", u)
                        wait_use(dve, it, expert_ready[u], 1, 1)
                        link(nc.vector.tensor_tensor(yb[u][:, :], sc[:, s, 0:D], x, ALU.add))
                        dve.sem_inc(ring_free["sc"][s], 1)
                        statistics(u, yb[u][:, :], LN_EPS)
                    elif stage == "m_ln":
                        layer_norm(it, u, "m", qf[u][:, 0:D], o_ready[u])
                assert steps[0] == VEC_STEPS, steps[0]

        @block.tensor
        def _(pe):
            pe.wait_ge(w_loaded, N_W)
            pe.wait_ge(w_scaled, N_SCALED)
            pe.wait_ge(ones_set, 2)
            pe.wait_ge(keys_ones, U)

            def transpose2(it, u, stage, src):
                slot = wait_free(pe, it, "pr", stage, u)
                for k in range(KT):
                    ins = nc.tensor.transpose(pr[:, slot, 128 * k:128 * k + 128], src[:, 128 * k:128 * k + 128], ident[:, :])
                ins.then_inc(ring_full["pr"][slot], 1)

            def project(it, u, stage, k, work):
                slot = wait_free(pe, it, "pr", stage, u, k)
                for cols, left, right, tiles in work:
                    for i in range(tiles):
                        ins = nc.tensor.matmul(pr[:, slot, cols], left(i), right(i), start=(i == 0), stop=(i == tiles - 1))
                ins.then_inc(ring_full["pr"][slot], 1)

            def qk_work(u, w):
                return [(slice(128 * a, 128 * a + 128), lambda i, a=a: w[:, i, 128 * a:128 * a + 128], lambda i: xt[u][:, i, :], KT)
                        for a in range(4)]

            def out_work(u, w, src, tiles=KT):
                return [(slice(0, D), lambda i: src[:, i, :], lambda i: w[:, i, :], tiles)]

            def head0(n):
                half, i, g = n // 16, n // 4 % 4, n % 4
                return (4 * half + g) * 4 + i

            def head1(n):
                half, i, g = n // 8, n // 4 % 2, n % 4
                return (4 * half + g) * 2 + i

            def scores0(it, u, stage, c, k, left, right, mask):
                s = wait_free(pe, it, "sc", stage, u, c)
                for j in range(2):
                    nc.tensor.matmul(sc[:, s, 512 * j:512 * j + 512], identb[:, :], mask[:, :].unsqueeze(1).broadcast_to([128, 4, 128]),
                                     start=True, stop=False, skip_group_check=True)
                for n in range(8):
                    h = head0(8 * c + n)
                    cols = slice(128 * h, 128 * h + 128)
                    ins = nc.tensor.matmul(sc[:, s, 128 * n:128 * n + 128], left[0:k, cols], right[0:k, cols],
                                           start=False, stop=(n % 4 == 3), skip_group_check=True)
                ins.then_inc(ring_full["sc"][s], 1)

            def scores_x(it, u, stage, c, k, left, right):
                s = wait_free(pe, it, "sc", stage, u, c)
                for n in range(2):
                    h = 2 * c + n if stage == "x0_S" else headx(2 * c + n)
                    for half in range(2):
                        a = 256 * h + 128 * half
                        ins = nc.tensor.matmul(sc[:, s, 512 * n + 256 * half:512 * n + 256 * half + 256], left[0:k, a:a + 128],
                                               right[0:k, 256 * h:256 * h + 256], start=True, stop=True)
                ins.then_inc(ring_full["sc"][s], 1)

            def headx(n):
                return 2 * (n % 4) + n // 4

            def scores1(it, u, stage, c, k, left, right, row=None):
                s = wait_free(pe, it, "sc", stage, u, c)
                if row is not None:
                    for j in range(2):
                        nc.tensor.matmul(sc[:, s, 512 * j:512 * j + 512], ones_row[:, :], row[:, :].unsqueeze(1).broadcast_to([1, 4, 128]),
                                         start=True, stop=False, skip_group_check=True)
                for n in range(8):
                    h = 8 * c + n if row is not None else head1(8 * c + n)
                    cols = slice(128 * h, 128 * h + 128)
                    ins = nc.tensor.matmul(sc[:, s, 128 * n:128 * n + 128], left[0:k, cols], right[0:k, cols],
                                           start=(row is None), stop=True, skip_group_check=True)
                ins.then_inc(ring_full["sc"][s], 1)

            def values(it, u, stage, c, chunks, todo):
                slot, _ = at_slot("o", stage, u)
                p = wait_full(pe, it, "p", stage, u, c)
                pe.sem_inc(ring_free["sc"][at_slot("sc", stage, u, c)[0]], 1)
                for kind in range(2):
                    for g, src, cols, first, v, ones in todo:
                        w = v if kind == 0 else ones
                        if w is None:
                            continue
                        dst = cols if kind == 0 else slice(cols.start + D, cols.stop + D)
                        ins = nc.tensor.matmul(ob[32 * g:32 * g + 32, slot, dst], w, pb[:, p, src],
                                               start=(first and kind == 0), stop=True, skip_group_check=True)
                ins.then_inc(ring_free["p"][p], 1)

            def values_of(u, layer, c):
                todo = []
                if layer == "l0":
                    for n in range(8):
                        h, m = head0(8 * c + n), 8 * c + n
                        half, i, g = m // 16, m // 4 % 4, m % 4
                        todo.append((g, slice(128 * n, 128 * n + 128), slice(128 * half, 128 * half + 128), half == 0 and i == 0,
                                     v0[u][:, h, :], ones8[:, i, :]))
                elif layer == "x0":
                    for n in range(2):
                        h = headx(2 * c + n)
                        for half in range(2):
                            todo.append((h // 2, slice(512 * n + 256 * half, 512 * n + 256 * half + 256), slice(0, D), h % 2 == 0 and half == 0,
                                         vb[u][:, 8 * half + h, :], ones16[:, h % 2, :]))
                else:
                    for n in range(8):
                        h, m = head1(8 * c + n), 8 * c + n
                        half, i, g = m // 8, m // 4 % 2, m % 4
                        todo.append((g, slice(128 * n, 128 * n + 128), slice(128 * half, 128 * half + 128), half == 0 and i == 0,
                                     vb[u][:, h, :], ones16[:, i, :] if layer == "c" else None))
                return todo

            def attend(it, u, layer, chunks, scores):
                stage = f"{layer}_P"
                slot, before = at_slot("pr", "ctxT", u) if layer == "x0" else at_slot("pr", f"{layer}_qk", u, 1)
                pe.wait_ge(ring_free["pr"][slot], it * (RING_TOTAL["pr"] // 2) + (before + 2))
                for c in range(chunks + 1):
                    if c < chunks:
                        scores(c)
                    if c == 1:
                        wait_free(pe, it, "o", stage, u)
                    if c >= 1:
                        values(it, u, stage, c - 1, chunks, values_of(u, layer, c - 1))

            def xt_in(it, u, stage):
                slot, before = at_slot("pr", stage.split("_")[0] + "_xT", u)
                pe.wait_ge(ring_free["pr"][slot], it * (RING_TOTAL["pr"] // 2) + (before + 2))

            def stack_in(it, u, layer):
                pe.wait_ge(stack_loaded[u], it * (16 * 23) + 16 * LOADS_UP_TO[layer])

            with pe.Fori(0, NIT) as it:
                for stage, u in ORDER:
                    x = xc[u][:, 0:D]
                    if stage == "ctxT":
                        wait_use(pe, it, in_loaded[u], 4, 4, 16)
                        transpose2(it, u, stage, xc[u][:, D:2 * D])
                    elif stage == "l0_xT":
                        transpose2(it, u, stage, x)
                    elif stage in ("f_xT", "l1_xT", "m_xT"):
                        before = {"f": "x0", "l1": "f", "m": "c"}[stage[:-3]]
                        wait_use(pe, it, x_ready[u], X_USE[before], 5)
                        transpose2(it, u, stage, x)
                    elif stage == "c_xT":
                        wait_use(pe, it, xn_ready[u], 1, 1)
                        transpose2(it, u, stage, yb[u][:, :])
                    elif stage in ("l0_qk", "l1_qk"):
                        w_qk, w_v = (w_qk0, w_v0) if stage == "l0_qk" else (w_qk1, w_v1)
                        xt_in(it, u, stage)
                        project(it, u, stage, 0, qk_work(u, w_qk))
                        project(it, u, stage, 1, out_work(u, w_v, xt[u]))
                    elif stage == "c_qk":
                        xt_in(it, u, stage)
                        wait_use(pe, it, ct_ready[u], 1, 1)
                        q_and_k = qk_work(u, w_qkc)
                        q_and_k = q_and_k[:2] + [(cols, left, lambda i: ct[u][:, i, :], KT) for cols, left, _, _ in q_and_k[2:]]
                        project(it, u, stage, 0, q_and_k)
                        project(it, u, stage, 1, [(slice(0, D), lambda i: ct[u][:, i, :], lambda i: w_vgc[:, i, 0:D], KT),
                                                  (slice(D, 2 * D), lambda i: xt[u][:, i, :], lambda i: w_vgc[:, i, D:2 * D], KT)])
                    elif stage == "l0_S":
                        stack_in(it, u, "l0")
                        for c in range(4):
                            scores0(it, u, stage, c, K0, sq[u], sk[u], alibi_qk)
                    elif stage == "x0_S":
                        stack_in(it, u, "x0")
                        for c in range(4):
                            scores_x(it, u, stage, c, K1, sq[u], sk[u])
                    elif stage == "c_S":
                        stack_in(it, u, "c")
                        wait_use(pe, it, mask_ready[u], 1, 1, 2)
                        for c in range(2):
                            scores1(it, u, stage, c, K1, sq[u], sk[u], mr[u])
                    elif stage in ("l0_mx", "x0_mx", "c_mx"):
                        layer, rows = stage[:-3], H0 if stage == "l0_mx" else 16
                        last = TAKES["sc"][f"{layer}_S"] - 1
                        for c in (last - 1, last):
                            s, before = at_slot("sc", f"{layer}_S", u, c)
                            pe.wait_ge(ring_free["sc"][s], it * (RING_TOTAL["sc"] // 2) + (before + 2))
                        slot = wait_free(pe, it, "pr", stage, u)
                        nc.tensor.transpose(pr[0:rows, slot, 0:128], nm[u][:, 0:rows], ident[:, :]).then_inc(ring_full["pr"][slot], 1)
                    elif stage == "l0_P":
                        wait_use(pe, it, max_loaded[u], 1, 3, 32)
                        attend(it, u, "l0", 4, lambda c: scores0(it, u, stage, c, K0 + 2, sk[u], sq[u], causal_kq))
                    elif stage == "x0_P":
                        wait_use(pe, it, max_loaded[u], 2, 3, 32)
                        attend(it, u, "x0", 4, lambda c: scores_x(it, u, stage, c, K1 + 2, sk[u], sq[u]))
                    elif stage == "l1_P":
                        stack_in(it, u, "l1")
                        attend(it, u, "l1", 2, lambda c: scores1(it, u, stage, c, K1, sk[u], sq[u]))
                    elif stage == "c_P":
                        wait_use(pe, it, max_loaded[u], 3, 3, 32)
                        attend(it, u, "c", 2, lambda c: scores1(it, u, stage, c, K1 + 2, sk[u], sq[u]))
                    elif stage in ("l0_o", "l1_o", "c_o"):
                        layer = stage[:-2]
                        slot, before = at_slot("o", f"{layer}_P", u)
                        pe.wait_ge(ring_free["o"][slot], it * (RING_TOTAL["o"] // 2) + (before + 2))
                        project(it, u, stage, 0, out_work(u, {"l0": w_p0, "l1": w_o1, "c": w_oc}[layer], xt[u]))
                    elif stage == "f_gu":
                        xt_in(it, u, stage)
                        for c in range(2):
                            s = wait_free(pe, it, "sc", stage, u, c)
                            first, tiles = (0, 8) if c == 0 else (1024, 4)
                            for a in range(tiles):
                                for i in range(KT):
                                    ins = nc.tensor.matmul(sc[:, s, 128 * a:128 * a + 128], w_gu[:, i, first + 128 * a:first + 128 * a + 128],
                                                           xt[u][:, i, :], start=(i == 0), stop=(i == KT - 1))
                            ins.then_inc(ring_full["sc"][s], 1)
                    elif stage == "f_o":
                        for c in range(2):
                            s, before = at_slot("sc", "f_gu", u, c)
                            pe.wait_ge(ring_free["sc"][s], it * (RING_TOTAL["sc"] // 2) + (before + 2))
                        ht = sq[u][:, :].bitcast(f32)
                        slot = wait_free(pe, it, "pr", stage, u)
                        for j in range(FT):
                            ins = nc.tensor.matmul(pr[:, slot, 0:D], ht[:, 128 * j:128 * j + 128], w_dn[:, j, :], start=(j == 0), stop=(j == FT - 1))
                        ins.then_inc(ring_full["pr"][slot], 1)
                    elif stage == "m_a":
                        xt_in(it, u, stage)
                        s = wait_free(pe, it, "sc", stage, u)
                        for i in range(KT):
                            ins = nc.tensor.matmul(sc[:, s, 0:MW], xt[u][:, i, :], w_m[:, i, :], start=(i == 0), stop=(i == KT - 1), skip_group_check=True)
                        ins.then_inc(ring_full["sc"][s], 1)
                    elif stage == "m_b":
                        wait_use(pe, it, axw_ready[u], 1, 1)
                        slot = wait_free(pe, it, "pr", stage, u)
                        nc.tensor.transpose(pr[:, slot, 0:128], yb[u][:, 0:128], ident[:, :]).then_inc(ring_full["pr"][slot], 1)
                    elif stage == "m_o":
                        slot, before = at_slot("pr", "m_b", u)
                        pe.wait_ge(ring_free["pr"][slot], it * (RING_TOTAL["pr"] // 2) + (before + 2))
                        s, _ = at_slot("sc", "m_a", u)
                        nc.tensor.matmul(sc[:, s, 0:D], yb[u][:, 128:256], w_b[:, :], start=False, stop=True, skip_group_check=True)\
                          .then_inc(expert_ready[u], 1)


def layouts(a):
    def heads(hd):
        p = np.arange(128)
        return np.concatenate([(2 * (p // hd) + tile) * hd + p % hd for tile in range(2)])

    def tiled(v):
        return np.ascontiguousarray(v.reshape(-1, 128).T)

    p0, p1 = heads(HD0), heads(HD1)
    q0, k0 = p0, D + p0
    q1, k1 = p1, D + p1
    wa, ba = a["L0_attn_W_attn"], a["L0_attn_b_attn"]
    w1, b1 = a["L1_attn_w_qkv"].T, a["L1_attn_b_qkv"]
    wide = np.zeros((D, FT * 128 - INTER), np.float32)
    g, up = np.concatenate([a["L0_ffn_gate_w"].T, wide], 1), np.concatenate([a["L0_ffn_up_w"].T, wide], 1)
    down = np.concatenate([a["L0_ffn_down_w"].T, np.zeros((FT * 128 - INTER, D), np.float32)], 0)
    mask = a["mask_BxS2_bk0"]
    start = 2.0 ** (-2.0 ** (-(np.log2(H1) - 3)))
    slopes = np.array([start ** (i + 1) for i in range(H1)], np.float32)
    lam = np.exp(-slopes).astype(np.float32)
    i = np.arange(128)
    diff = (i[None, :] - i[:, None]).astype(np.float32)
    n = np.arange(H1)
    order = (4 * (n // 8) + n % 4) * 2 + n // 4 % 2
    decay = np.where(diff[:, None, :] >= 0, lam[order][None, :, None] ** np.maximum(diff, 0)[:, None, :], 0).astype(np.float32)
    causal = np.where(diff >= 0, 0.0, NEG)
    alibi = np.where(i[None, :] <= i[:, None], i[None, :] * (SLOPE / SCALE0), NEG)
    ones8, ones16 = np.zeros((128, 4, 32), np.float32), np.zeros((128, 2, 32), np.float32)
    for j in range(4):
        ones8[:, j, 8 * j:8 * j + 8] = 1
    for j in range(2):
        ones16[:, j, 16 * j:16 * j + 16] = 1
    return {
        "x": a["x"], "ctx": a["ctx_2048"], "mask_col": mask.reshape(B, 128, 1), "mask_row": mask.reshape(B, 1, 128),
        "w_qk0": wa[:, np.concatenate([q0, k0])], "w_v0": wa[:, 2 * D:], "w_p0": a["L0_attn_W_proj"],
        "b_qk0": tiled(ba[np.concatenate([q0, k0])]), "b_v0": ba[2 * D:], "b_p0": a["L0_attn_b_proj"],
        "w_gu": np.concatenate([g[:, :512], up[:, :512], g[:, 512:], up[:, 512:]], 1), "w_dn": down,
        "gate_s": a["L0_ffn_gate_s"], "up_s": a["L0_ffn_up_s"], "down_s": a["L0_ffn_down_s"],
        "w_qk1": w1[:, np.concatenate([q1, k1])], "w_v1": w1[:, 2 * D:], "w_o1": a["L1_attn_w_out"].T,
        "b_qk1": tiled(b1[np.concatenate([q1, k1])]), "b_v1": b1[2 * D:], "b_o1": a["L1_attn_b_out"],
        "norm_w": tiled(a["L1_xattn_norm_w"]),
        "w_qkc": np.concatenate([a["L1_xattn_wq"].T[:, p1], a["L1_xattn_wk"].T[:, p1]], 1),
        "w_vgc": np.concatenate([a["L1_xattn_wv"].T, a["L1_xattn_wg"].T], 1), "w_oc": a["L1_xattn_wo"].T,
        "w_m": np.concatenate([a["L1_ffn_weight"].T, a["L1_ffn_lora_A"].reshape(E * R, D).T, a["L1_ffn_router_w"].T], 1),
        "w_b": a["L1_ffn_lora_B"].transpose(0, 2, 1).reshape(E * R, D),
        "ident": np.eye(128, dtype=np.float32), "decay": decay,
        "causal_kq": causal.astype(np.float32), "alibi_qk": alibi.astype(np.float32), "key_bias": (i * SLOPE).astype(np.float32).reshape(128, 1),
        "iota8": np.tile(np.arange(E, dtype=np.float32), (128, 1)), "ones8": ones8, "ones16": ones16,
    }


def kernel(**inputs):
    import concourse.bacc as bacc
    from concourse.bass_utils import run_bass_kernel_spmd

    nc = bacc.Bacc("TRN2", target_bir_lowering=False, num_devices=1)
    arrays, t = {}, {}
    for name, a in layouts({k: np.asarray(v) for k, v in inputs.items()}).items():
        a = np.ascontiguousarray(a)
        arrays[f"in_{name}"] = a
        t[name] = nc.dram_tensor(f"in_{name}", a.shape, mybir.dt.from_np(a.dtype), kind="ExternalInput").ap()
    out = nc.dram_tensor("out", (B, T, D), f32, kind="ExternalOutput").ap()
    decoder_kernel(nc, t, out)
    r = run_bass_kernel_spmd(nc, [arrays], core_ids=[0])
    return r.results[0]["out"]
```

```python
import numpy as np
import concourse.bass as bass
from concourse import mybir
from contextlib import ExitStack

f32, bf16, u8, u32 = mybir.dt.float32, mybir.dt.bfloat16, mybir.dt.uint8, mybir.dt.uint32
ACT = mybir.ActivationFunctionType
ALU = mybir.AluOpType
AX = mybir.AxisListType

B, T, D = 16, 128, 256
U = 4
NIT = B // U
KT = D // 128
H0, HX0, H1 = 32, 8, 16
INTER, FT = 704, 6
E, R = 8, 16
MW = D + E * R + E
NEG = -1e30
LN_EPS, RMS_EPS = 1e-5, 1e-6
SLOPE = 2.0 ** (-8.0 / H0)
SCALE0, SCALEX = float(8) ** -0.5, 0.25
HD0, HD1 = 8, 16
K0 = 9 * HD0
K1 = 6 * HD1


def scores(layer, chunks):
    return [f"{layer}_{step}{c}" for c in range(chunks) for step in "PV"]


QUARTERS = [
    ["load", "ctxT", "l0_xT", "l0_qk", "l0_r", "l0_c", "l0_ld", "l0_S0", "l0_S1", "l0_S2", "l0_S3", "l0_mx",
     *scores("l0", 4), "l0_n", "l0_o", "l0_ln"],
    ["x0_a", "x0_r", "x0_c", "x0_ld", "x0_S0", "x0_S1", "x0_S2", "x0_S3", "x0_mx", *scores("x0", 4), "x0_n", "x0_ln"],
    ["f_xT", "f_gu0", "f_gu1", "f_o", "f_ln",
     "l1_xT", "l1_qk", "l1_r", "l1_c", "l1_ld", *scores("l1", 2), "l1_n", "l1_o", "l1_ln", "c_rms"],
    ["c_xT", "c_qk", "c_r", "c_c", "c_ld", "c_S0", "c_S1", "c_mx", *scores("c", 2), "c_n", "c_o", "c_ln",
     "m_xT", "m_a", "m_b", "m_o", "m_ln"],
]
LASTS = {"load": 4, "ctxT": 1, "l0_xT": 1.5, "l0_qk": 4.2, "l0_r": 1, "l0_c": 1.5, "l0_ld": 6, "l0_S0": 1.3, "l0_S1": 1.3,
         "l0_S2": 1.3, "l0_S3": 1.3, "l0_mx": 5, "l0_P0": 1.3, "l0_V0": 1.3, "l0_P1": 1.3, "l0_V1": 1.4, "l0_P2": 1.3,
         "l0_V2": 1.3, "l0_P3": 1.3, "l0_V3": 1.4, "l0_n": 2.5, "l0_o": 3, "l0_ln": 2, "x0_a": 1, "x0_r": 1, "x0_c": 3,
         "x0_ld": 6, "x0_S0": 1.3, "x0_S1": 1.3, "x0_S2": 1.3, "x0_S3": 1.3, "x0_mx": 5, "x0_P0": 1.3, "x0_V0": 0.9,
         "x0_P1": 1.3, "x0_V1": 1.3, "x0_P2": 1.3, "x0_V2": 0.2, "x0_P3": 2.1, "x0_V3": 1.3, "x0_n": 9.5, "x0_ln": 2,
         "f_xT": 3.0, "f_gu0": 6.1, "f_gu1": 4, "f_o": 4, "f_ln": 2, "l1_xT": 1.5, "l1_qk": 5.5, "l1_r": 1.9, "l1_c": 3,
         "l1_ld": 6, "l1_P0": 1.3, "l1_V0": 1.3, "l1_P1": 1.3, "l1_V1": 1.1, "l1_n": 1, "l1_o": 3, "l1_ln": 2, "c_rms": 2,
         "c_xT": 3.7, "c_qk": 0, "c_r": 1, "c_c": 3, "c_ld": 6, "c_S0": 0.2, "c_S1": 2.3, "c_mx": 5, "c_P0": 2.6,
         "c_V0": 2.6, "c_P1": 3.1, "c_V1": 3.6, "c_n": 2.5, "c_o": 4, "c_ln": 2, "m_xT": 1.2, "m_a": 1.5, "m_b": 4,
         "m_o": 3, "m_ln": 2}
BEGINS = [0.0, 0.0, 0.0, 0.016]


SLOTS = {"sc": 2, "pr": 2, "o": 2, "p": 3}
TAKES = {
    "sc": {"f_gu0": 1, "f_gu1": 1},
    "pr": {"ctxT": 1, "l0_xT": 1, "l0_qk": 2, "l0_mx": 1, "l0_o": 1, "x0_mx": 1, "f_xT": 1, "f_o": 1, "l1_xT": 1,
           "l1_qk": 2, "l1_o": 1, "c_xT": 1, "c_qk": 2, "c_mx": 1, "c_o": 1, "m_xT": 1, "m_b": 1},
    "o": {"l0_P0": 1, "x0_P0": 1, "l1_P0": 1, "c_P0": 1, "m_a": 1},
    "p": {},
}
CHUNKS = {"l0": 4, "x0": 4, "l1": 2, "c": 2}
for _layer, _chunks in CHUNKS.items():
    for _c in range(_chunks):
        TAKES["sc"][f"{_layer}_S{_c}"] = TAKES["sc"][f"{_layer}_P{_c}"] = TAKES["p"][f"{_layer}_P{_c}"] = 1
RING_TOTAL = {ring: U * sum(takes[s] for q in QUARTERS for s in q if s in takes) for ring, takes in TAKES.items()}
RELEASED_BY = {("o", "m_a"): "m_o", ("pr", "c_qk"): "c_r"}
for _layer, _chunks in CHUNKS.items():
    RELEASED_BY["o", f"{_layer}_P0"] = f"{_layer}_n"
    for _c in range(_chunks):
        RELEASED_BY["sc", f"{_layer}_P{_c}"] = RELEASED_BY["p", f"{_layer}_P{_c}"] = f"{_layer}_V{_c}"


def merged():
    due = []
    for q, quarter in enumerate(QUARTERS):
        lasts = [LASTS.get(s, 1.3) for s in quarter]
        at, times = BEGINS[q], []
        for n in lasts:
            times.append(at)
            at += n * (1 - BEGINS[q]) / sum(lasts)
        due.append(times)
    steps, done, at = [], {"load"}, [0] * len(QUARTERS)
    held = {ring: ["load"] * n for ring, n in SLOTS.items()}
    while len(steps) < sum(len(q) for q in QUARTERS):
        for _, q in sorted((due[q][at[q]], q) for q in range(len(QUARTERS)) if at[q] < len(QUARTERS[q])):
            step = QUARTERS[q][at[q]]
            takes = {ring: TAKES[ring].get(step, 0) for ring in SLOTS}
            if all(RELEASED_BY.get((ring, s), s) in done for ring, n in takes.items() if n for s in held[ring][-SLOTS[ring]:][:n]):
                break
        else:
            raise ValueError("no step can be next")
        for ring, n in takes.items():
            held[ring] += [step] * n
        steps.append((step, q))
        done.add(step)
        at[q] += 1
    return steps


def sections():
    steps = []
    for k in range(4):
        for s, q in merged():
            u = (q - k) % 4
            steps.append((s, u, 1 if u + k >= 4 else 0))
    return {"first": [e for e in steps if e[2] == 1], "body": steps, "last": [e for e in steps if e[2] == 0]}


ORDER = sections()



def first_use():
    at = {}
    for ring, takes in TAKES.items():
        n = 0
        for section, steps in ORDER.items():
            if section == "last":
                n += (NIT - 2) * RING_TOTAL[ring]
            for stage, u, _ in steps:
                at[section, ring, stage, u] = n
                n += takes.get(stage, 0)
        assert RING_TOTAL[ring] % SLOTS[ring] == 0
    return at


RING_AT = first_use()

X_USE = {"l0": 1, "x0": 2, "f": 3, "l1": 4, "c": 5}
SPLIT_USE = {"l0": 1, "x0": 2, "l1": 3, "c": 4}
MAX_USE = {"l0": 1, "x0": 2, "c": 3}
NORM_USE = {"l0": 1, "x0": 2, "f": 3, "l1": 4, "c_rms": 5, "c": 6, "m": 7}
PART = 128 * 256
STORES_UP_TO, STORES = {"l0": 1, "x0": 7, "l1": 8, "c": 9}, 9
LOADS_UP_TO = {"l0": 5, "x0": 11, "l1": 17, "c": 23}
VEC_STEPS = 144 + 3 * U


class When:

    def __init__(self, section, group, lead, loop):
        self.section, self.group, self.lead, self.loop = section, group, lead, loop

    def at(self, per_group, extra):
        return self.group * per_group + (self.lead * per_group + extra)

    def batch(self, u):
        return self.group * U + (self.lead * U + u)


def run(engine, step):
    for stage, u, _ in ORDER["first"]:
        step(stage, u, When("first", 0, 0, 0))
    with engine.Fori(0, NIT - 1) as it:
        for stage, u, lead in ORDER["body"]:
            step(stage, u, When("body", it, lead, it))
    for stage, u, _ in ORDER["last"]:
        step(stage, u, When("last", NIT - 1, 0, 0))


def decoder_kernel(nc, t, out):
    ctx = ExitStack()
    with ctx:
        def sb(name, shape, dt=f32):
            return ctx.enter_context(nc.sbuf_tensor(name, shape, dt))

        def sem(name):
            return ctx.enter_context(nc.semaphore(name))

        def per_u(name):
            return [sem(f"{name}{u}") for u in range(U)]

        w_qk0, w_v0, w_p0 = sb("w_qk0", [128, KT, 512]), sb("w_v0", [128, KT, D]), sb("w_p0", [128, KT, D])
        w_gu, w_dn = sb("w_gu", [128, KT, 2 * FT * 128]), sb("w_dn", [128, FT, D])
        w_qk1, w_v1, w_o1 = sb("w_qk1", [128, KT, 512]), sb("w_v1", [128, KT, D]), sb("w_o1", [128, KT, D])
        w_qkc, w_vgc, w_oc = sb("w_qkc", [128, KT, 512]), sb("w_vgc", [128, KT, 512]), sb("w_oc", [128, KT, D])
        w_m, w_b = sb("w_m", [128, KT, MW]), sb("w_b", [128, D])
        b_qk0, b_qk1 = sb("b_qk0", [128, 4]), sb("b_qk1", [128, 4])
        bc_v0, bc_p0, bc_v1, bc_o1 = (sb(n, [128, D]) for n in ("bc_v0", "bc_p0", "bc_v1", "bc_o1"))
        norm_w = sb("norm_w", [128, KT])
        ident, identb = sb("ident", [128, 128]), sb("identb", [128, 128], bf16)
        decay = sb("decay", [128, H1, 128])
        causal_kq, alibi_qk = sb("causal_kq", [128, 128], bf16), sb("alibi_qk", [128, 128], bf16)
        key_bias, iota8 = sb("key_bias", [128, 1]), sb("iota8", [128, E])
        ones8, ones16 = sb("ones8", [128, 4, 32]), sb("ones16", [128, 2, 32])
        ones_row, minus_half = sb("ones_row", [1, 128], bf16), sb("minus_half", [128, 1])

        xc = [sb(f"xc{u}", [128, 2 * D]) for u in range(U)]
        ct = [sb(f"ct{u}", [128, KT, 128]) for u in range(U)]
        xt = [sb(f"xt{u}", [128, KT, 128]) for u in range(U)]
        qf = [sb(f"qf{u}", [128, 512]) for u in range(U)]
        pt = [sb(f"pt{u}", [128, 2, 3, 256], bf16) for u in range(U)]
        sq = [sb(f"sq{u}", [128, 4096], bf16) for u in range(U)]
        sk = [sb(f"sk{u}", [128, 4096], bf16) for u in range(U)]
        v0 = [sb(f"v0{u}", [128, H0, 32]) for u in range(U)]
        vb = [sb(f"vb{u}", [128, H1, 32]) for u in range(U)]
        yb = [sb(f"yb{u}", [128, D]) for u in range(U)]
        nm = [sb(f"nm{u}", [128, H0]) for u in range(U)]
        nh = [sb(f"nh{u}", [128, 2 * H0], bf16) for u in range(U)]
        mx = [sb(f"mx{u}", [2 * H0, 128], bf16) for u in range(U)]
        st = [sb(f"st{u}", [128, 40]) for u in range(U)]
        ix = [sb(f"ix{u}", [128, 8], u32) for u in range(U)]
        mk8 = [sb(f"mk8{u}", [128, 1], u8) for u in range(U)]
        mr8 = [sb(f"mr8{u}", [1, 128], u8) for u in range(U)]
        mk = [sb(f"mk{u}", [128, 1]) for u in range(U)]
        mr = [sb(f"mr{u}", [1, 128], bf16) for u in range(U)]
        pb = sb("pb", [128, SLOTS["p"], 1024])

        sc = ctx.enter_context(nc.psum_tensor("sc", [128, 2, 1024], f32))
        pr = ctx.enter_context(nc.psum_tensor("pr", [128, 2, 512], f32))
        ob = ctx.enter_context(nc.psum_tensor("ob", [128, 2, 512], f32))
        scratch = [nc.dram_tensor(f"scratch{u}", (2 * 3 * 128 * 256,), bf16, kind="Internal").ap() for u in range(U)]

        ring_full = {r: [sem(f"{r}_full{i}") for i in range(n)] for r, n in SLOTS.items()}
        ring_free = {r: [sem(f"{r}_free{i}") for i in range(n)] for r, n in SLOTS.items()}
        w_loaded, scales_loaded, w_scaled = sem("w_loaded"), sem("scales_loaded"), sem("w_scaled")
        pads_zero, ones_set, keys_ones = sem("pads_zero"), sem("ones_set"), sem("keys_ones")
        vec_held, sp_held = sem("vec_held"), sem("sp_held")
        in_loaded, out_stored = per_u("in_loaded"), per_u("out_stored")
        x_ready, xn_ready = per_u("x_ready"), per_u("xn_ready")
        pa_ready, r_ready = per_u("pa_ready"), per_u("r_ready")
        pb_ready, parts_ready = per_u("pb_ready"), per_u("parts_ready")
        parts_stored, stack_loaded = per_u("parts_stored"), per_u("stack_loaded")
        ct_ready = per_u("ct_ready")
        mh_ready, max_loaded = per_u("mh_ready"), per_u("max_loaded")
        var_ready, rstd_ready, xb_ready = per_u("var_ready"), per_u("rstd_ready"), per_u("xb_ready")
        tanh_ready, mask_ready = per_u("tanh_ready"), per_u("mask_ready")
        gap_ready, egap_ready, axw_ready, axt_ready = per_u("gap_ready"), per_u("egap_ready"), per_u("axw_ready"), per_u("axt_ready")
        logits_ready, expert_ready, o_ready, vec_step = per_u("logits_ready"), per_u("expert_ready"), per_u("o_ready"), sem("vec_step")

        wide_masks = [pb[:, 2, D + 128 * i:D + 128 * i + 128] for i in range(2)]
        weights = [(w_qk0, "w_qk0"), (w_v0, "w_v0"), (w_p0, "w_p0"), (w_gu, "w_gu"), (w_dn, "w_dn"), (w_qk1, "w_qk1"),
                   (w_v1, "w_v1"), (w_o1, "w_o1"), (w_qkc, "w_qkc"), (w_vgc, "w_vgc"), (w_oc, "w_oc"), (w_m, "w_m")]
        plain = [(w_b, "w_b"), (b_qk0, "b_qk0"), (b_qk1, "b_qk1"), (ident, "ident"), (decay, "decay"), (wide_masks[0], "causal_kq"),
                 (wide_masks[1], "alibi_qk"), (key_bias, "key_bias"), (iota8, "iota8"),
                 (ones8, "ones8"), (ones16, "ones16"), (norm_w, "norm_w")]
        spread = [(bc_v0, "b_v0"), (bc_p0, "b_p0"), (bc_v1, "b_v1"), (bc_o1, "b_o1")]
        N_SCALED = 2 + 4 * KT + FT + 3 + 1 + 2 * KT
        N_W = 16 * (len(weights) + len(plain) + len(spread))
        bc_gs, bc_us, bc_ds = pb[:, 0, 0:FT * 128], pb[:, 1, 0:FT * 128], pb[:, 2, 0:D]

        def ffn_space(u):
            return qf[u][:, :], pt[u][:, :, :, :].rearrange("p a b n -> p (a b n)").bitcast(f32)[:, 0:D]

        def part(u, c):
            return pt[u][:, :, c, :]

        def sides(ap):
            return ap.rearrange("p (s n) -> p s n", s=2)

        def on_all(name, n):
            return bass.AP(t[name].tensor, 0, [[0, 128], [1, n]])

        def flat(tensor, u_offset, *dims):
            return bass.AP(tensor, u_offset, [list(d) for d in dims])

        def pads(tensor, blocks, per, width):
            return bass.AP(tensor, 0, [[blocks * per * 32, 128], [per * 32, blocks], [32 + width, per], [1, width]])

        def at_slot(w, ring, stage, u, k=0):
            n = RING_AT[w.section, ring, stage, u] + k
            return n % SLOTS[ring], w.loop * (RING_TOTAL[ring] // SLOTS[ring]) + n // SLOTS[ring]

        def wait_full(eng, w, ring, stage, u, k=0):
            slot, before = at_slot(w, ring, stage, u, k)
            eng.wait_ge(ring_full[ring][slot], before + 1)
            return slot

        def wait_free(eng, w, ring, stage, u, k=0):
            slot, before = at_slot(w, ring, stage, u, k)
            eng.wait_ge(ring_free[ring][slot], before + 1)
            return slot

        def wait_freed(eng, w, ring, stage, u, k=0):
            slot, before = at_slot(w, ring, stage, u, k)
            eng.wait_ge(ring_free[ring][slot], before + 2)
            return slot

        def wait_attended(eng, w, layer, u):
            wait_freed(eng, w, "p", f"{layer}_P{CHUNKS[layer] - 1}", u)
            return at_slot(w, "o", f"{layer}_P0", u)[0]

        def wait_use(eng, w, semaphore, use, per_group, step=1):
            eng.wait_ge(semaphore, w.at(per_group * step, use * step))

        block = ctx.enter_context(nc.Block())

        @block.sync
        def _(sp):
            sp.dma_start(bc_gs[:, 0:INTER], on_all("gate_s", INTER)).then_inc(scales_loaded, 16)
            sp.dma_start(bc_us[:, 0:INTER], on_all("up_s", INTER)).then_inc(scales_loaded, 16)
            sp.dma_start(bc_ds, on_all("down_s", D)).then_inc(scales_loaded, 16)
            for dst, name in weights:
                sp.dma_start(dst[:, :, :], t[name].rearrange("(k p) n -> p k n", p=128)).then_inc(w_loaded, 16)
            for dst, name in plain:
                dims = "p a b -> p (a b)"
                d = dst[:, :, :].rearrange(dims) if len(dst.shape) == 3 else dst[:, :]
                s = t[name].rearrange(dims) if len(dst.shape) == 3 else t[name]
                sp.dma_start(d, s).then_inc(w_loaded, 16)
            for dst, name in spread:
                sp.dma_start(dst[:, :], on_all(name, D)).then_inc(w_loaded, 16)

            def store_parts(w, u, layer):
                wait_use(sp, w, parts_ready[u], SPLIT_USE[layer], 4)
                dst = flat(scratch[u].tensor, 0, (256, 128), (PART, 6), (1, 256))
                sp.dma_start(dst, pt[u][:, :, :, :].rearrange("p s c n -> p (s c) n")).then_inc(parts_stored[u], 16)

            def store_groups(w, u):
                wait_use(sp, w, parts_ready[u], SPLIT_USE["x0"], 4)
                for side in range(2):
                    for c in range(3):
                        dst = flat(scratch[u].tensor, (3 * side + c) * PART, (256, 8), (2048, 16), (1, 256))
                        sp.dma_start(dst, pt[u][:, side, c, :]).then_inc(parts_stored[u], 16)

            def load_stacks(w, u, layer):
                sp.wait_ge(parts_stored[u], w.at(16 * STORES, 16 * STORES_UP_TO[layer]))
                dram = scratch[u].tensor
                if layer == "l0":
                    for c in range(3):
                        sp.dma_start(sq[u][24 * c:24 * c + 24, :], flat(dram, c * PART, (0, 3), (4096, 8), (1, 4096)))\
                          .then_inc(stack_loaded[u], 16)
                    sp.dma_start(sk[u][0:72, :], flat(dram, 3 * PART, (0, 3), (4096, 24), (1, 4096))).then_inc(stack_loaded[u], 16)
                    sp.dma_start(sk[u][72:74, :], sk[u][96:98, :]).then_inc(stack_loaded[u], 16)
                    return
                for first, n, c in ((0, 3, 0), (48, 2, 1), (80, 1, 2)):
                    sp.dma_start(sq[u][first:first + 16 * n, 0:2048], flat(dram, c * PART, (0, n), (2048, 16), (1, 2048)))\
                      .then_inc(stack_loaded[u], 16)
                    sp.dma_start(sk[u][first:first + 16 * n, 0:2048], flat(dram, 3 * PART, (2048, 16 * n), (1, 2048)))\
                      .then_inc(stack_loaded[u], 16)

            def load_max(w, u, layer, rows, first):
                wait_freed(sp, w, "pr", f"{layer}_mx", u)
                sp.dma_start(sq[u][first:first + 2, 0:rows * 128], mx[u][0:2 * rows, :]).then_inc(max_loaded[u], 16)

            def step(stage, u, w):
                if stage == "load":
                    sp.wait_ge(out_stored[u], w.at(16, 16))
                    sp.dma_start(xc[u][:, :], t["xc"][w.batch(u)]).then_inc(in_loaded[u], 16)
                    sp.dma_start(mk8[u][:, :], t["mask_col"][w.batch(u)]).then_inc(in_loaded[u], 16)
                    sp.dma_start(mr8[u][:, :], t["mask_row"][w.batch(u)]).then_inc(in_loaded[u], 16)
                elif stage in ("l0_c", "l1_c", "c_c"):
                    store_parts(w, u, stage[:-2])
                elif stage == "x0_c":
                    store_groups(w, u)
                elif stage in ("l0_ld", "x0_ld", "l1_ld", "c_ld"):
                    load_stacks(w, u, stage[:-3])
                elif stage == "l0_mx":
                    load_max(w, u, "l0", H0, K0)
                elif stage in ("x0_mx", "c_mx"):
                    load_max(w, u, stage[:-3], 16, K1)
                elif stage == "m_ln":
                    wait_use(sp, w, o_ready[u], 1, 1)
                    sp.dma_start(out[w.batch(u)], qf[u][:, 0:D]).then_inc(out_stored[u], 16)

            run(sp, step)
            for u in range(U):
                sp.wait_ge(out_stored[u], 16 * (NIT + 1))

        @block.gpsimd
        def _(pool):
            for u in range(U):
                nc.gpsimd.memset(v0[u][:, :, :], 0.0).then_inc(pads_zero, 1)
                nc.gpsimd.memset(vb[u][:, :, :], 0.0).then_inc(pads_zero, 1)
            nc.gpsimd.memset(ones_row[:, :], 1.0).then_inc(ones_set, 1)
            nc.gpsimd.memset(minus_half[:, :], -0.5).then_inc(ones_set, 1)
            pool.wait_ge(w_loaded, N_W)
            pool.wait_ge(ones_set, 2)

            def rstd(w, u, layer):
                wait_use(pool, w, var_ready[u], NORM_USE[layer], 7)
                nc.gpsimd.tensor_tensor(st[u][:, 11:12], st[u][:, 10:11], minus_half[:, :], ALU.pow).then_inc(rstd_ready[u], 1)

            def step(stage, u, w):
                if stage == "l0_xT":
                    wait_use(pool, w, in_loaded[u], 3, 3, 16)
                    nc.gpsimd.tensor_tensor(yb[u][:, :], xc[u][:, 0:D], bc_p0[:, :], ALU.add).then_inc(xb_ready[u], 1)
                elif stage == "l1_xT":
                    wait_use(pool, w, x_ready[u], X_USE["f"], 5)
                    nc.gpsimd.tensor_tensor(yb[u][:, :], xc[u][:, 0:D], bc_o1[:, :], ALU.add).then_inc(xb_ready[u], 1)
                elif stage in ("l0_o", "f_o", "l1_o", "c_o", "m_o"):
                    rstd(w, u, stage[:-2])
                elif stage == "x0_n":
                    rstd(w, u, "x0")
                elif stage == "c_rms":
                    rstd(w, u, "c_rms")

            run(pool, step)

        @block.scalar
        def _(act):
            act.wait_ge(w_loaded, N_W)
            act.wait_ge(pads_zero, 2 * U)

            def transposed(w, u, stage, dst, ready):
                slot = wait_full(act, w, "pr", stage, u)
                src = pr[:, slot, 0:D].rearrange("p (k n) -> p k n", k=KT)
                nc.scalar.activation(dst[:, :, :], src, ACT.Copy).then_inc(ready, 1)
                return slot

            def second_part(w, u, layer):
                wait_use(act, w, r_ready[u], SPLIT_USE[layer], 4)
                nc.scalar.activation(part(u, 1), sides(qf[u][:, :]), ACT.Copy).then_inc(pb_ready[u], 1)

            def max_rows(w, u, layer, rows):
                slot = wait_full(act, w, "pr", f"{layer}_mx", u)
                nc.scalar.activation(mx[u][0:2 * rows, :], pr[0:2 * rows, slot, 0:128], ACT.Copy).then_inc(ring_free["pr"][slot], 1)

            def exps(w, u, stage, scale, bias):
                s = wait_full(act, w, "sc", stage, u)
                p = wait_free(act, w, "p", stage, u)
                nc.scalar.activation(pb[:, p, :], sc[:, s, :], ACT.Exp, bias=bias, scale=scale).then_inc(ring_full["p"][p], 1)

            def step(stage, u, w):
                if stage == "ctxT":
                    slot = transposed(w, u, stage, ct[u], ct_ready[u])
                    src = pr[:, slot, 0:D].rearrange("p (b h c) -> p b h c", b=8, h=2)
                    nc.scalar.activation(pads(vb[u], 8, 2, 16), src, ACT.Copy).then_inc(ring_free["pr"][slot], 1)
                elif stage in ("l0_xT", "f_xT", "l1_xT", "c_xT", "m_xT"):
                    slot = wait_full(act, w, "pr", stage, u)
                    src = pr[:, slot, 0:D].rearrange("p (k n) -> p k n", k=KT)
                    nc.scalar.activation(xt[u][:, :, :], src, ACT.Copy).then_inc(ring_free["pr"][slot], 1)
                elif stage in ("l0_qk", "l1_qk"):
                    slot = wait_freed(act, w, "pr", stage, u, 0)
                    nc.scalar.activation(part(u, 0), sides(qf[u][:, :]), ACT.Copy).then_inc(pa_ready[u], 1)
                elif stage == "x0_a":
                    wait_use(act, w, x_ready[u], X_USE["l0"], 5)
                    nc.scalar.activation(part(u, 0), sides(xc[u][:, :]), ACT.Copy).then_inc(pa_ready[u], 1)
                elif stage == "c_qk":
                    slot = wait_full(act, w, "pr", stage, u, 0)
                    nc.scalar.activation(part(u, 0), sides(pr[:, slot, :]), ACT.Copy).then_inc(pa_ready[u], 1)
                    slot = wait_full(act, w, "pr", stage, u, 1)
                    src = pr[:, slot, 0:D].rearrange("p (b h c) -> p b h c", b=8, h=2)
                    nc.scalar.activation(pads(vb[u], 8, 2, 16), src, ACT.Copy)
                    nc.scalar.activation(yb[u][:, :], pr[:, slot, D:2 * D], ACT.Tanh, scale=0.5).then_inc(ring_free["pr"][slot], 1)
                elif stage in ("l0_r", "x0_r", "l1_r", "c_r"):
                    second_part(w, u, stage[:-2])
                elif stage == "l0_mx":
                    max_rows(w, u, "l0", H0)
                elif stage in ("x0_mx", "c_mx"):
                    max_rows(w, u, stage[:-3], 16)
                elif stage[:-1] == "l0_P":
                    exps(w, u, stage, SCALE0, key_bias[:, 0:1])
                elif stage[:-1] == "x0_P":
                    exps(w, u, stage, SCALEX, 0.0)
                elif stage[:-1] == "c_P":
                    if stage == "c_P0":
                        wait_use(act, w, mask_ready[u], 2, 2)
                    exps(w, u, stage, SCALEX, mk[u][:, 0:1])
                elif stage in ("f_gu0", "f_gu1"):
                    c = int(stage[-1])
                    n = 512 if c == 0 else 256
                    s = wait_full(act, w, "sc", stage, u)
                    nc.scalar.activation(ffn_space(u)[c], sc[:, s, 0:n], ACT.Tanh, scale=0.5).then_inc(tanh_ready[u], 1)
                elif stage == "l1_n":
                    slot = wait_attended(act, w, "l1", u)
                    src = ob[:, slot, 0:D].rearrange("p (k n) -> p k n", k=KT)
                    nc.scalar.activation(xt[u][:, :, :], src, ACT.Copy).then_inc(ring_free["o"][slot], 1)
                elif stage == "m_a":
                    wait_use(act, w, gap_ready[u], 1, 1)
                    nc.scalar.activation(st[u][:, 20:21], st[u][:, 19:20], ACT.Exp).then_inc(egap_ready[u], 1)
                elif stage == "m_b":
                    slot = wait_full(act, w, "pr", stage, u)
                    nc.scalar.activation(yb[u][:, 128:256], pr[:, slot, 0:128], ACT.Copy).then_inc(ring_free["pr"][slot], 1)

            run(act, step)

        @block.vector
        def _(dve):
            for r, n in SLOTS.items():
                for i in range(n):
                    dve.sem_inc(ring_free[r][i], 1)
            for u in range(U):
                dve.sem_inc(out_stored[u], 16)
            for u in range(U):
                nc.vector.memset(sk[u][96:98, :], 1.0).then_inc(keys_ones, 1)
            dve.wait_ge(w_loaded, N_W)
            dve.wait_ge(scales_loaded, 48)
            nc.vector.memset(pb[:, 0, INTER:FT * 128], 0.0).then_inc(w_scaled, 1)
            nc.vector.memset(pb[:, 1, INTER:FT * 128], 0.0).then_inc(w_scaled, 1)
            dve.wait_ge(w_scaled, 2)
            for k in range(KT):
                for first, tiles, scales, tile in ((0, 4, bc_gs, 0), (512, 4, bc_us, 0), (1024, 2, bc_gs, 4), (1280, 2, bc_us, 4)):
                    cols = w_gu[:, k, first:first + 128 * tiles]
                    nc.vector.tensor_tensor(cols, cols, scales[:, 128 * tile:128 * (tile + tiles)], ALU.mult).then_inc(w_scaled, 1)
            for j in range(FT):
                nc.vector.scalar_tensor_tensor(w_dn[:, j, :], w_dn[:, j, :], 0.5, bc_ds, ALU.mult, ALU.mult).then_inc(w_scaled, 1)
            for narrow, wide in ((causal_kq, wide_masks[0]), (alibi_qk, wide_masks[1]), (identb, ident)):
                nc.vector.tensor_copy(narrow[:, :], wide[:, :]).then_inc(w_scaled, 1)
            nc.vector.tensor_scalar(w_oc[:, :, :], w_oc[:, :, :], 0.5, None, ALU.mult).then_inc(w_scaled, 1)
            for k in range(KT):
                for cols in (w_qkc[:, k, 0:D], w_vgc[:, k, D:2 * D]):
                    nc.vector.tensor_scalar(cols, cols, norm_w[:, k:k + 1], None, ALU.mult).then_inc(w_scaled, 1)
            dve.wait_ge(w_scaled, N_SCALED)
            dve.wait_ge(pads_zero, 2 * U)

            steps, here = [0], [None]

            def link(ins):
                ins.then_inc(vec_step, 1)
                steps[0] += 1
                w = here[0]
                dve.wait_ge(vec_step, w.loop * VEC_STEPS + steps[0] + (w.section == "last") * (NIT - 2) * VEC_STEPS)

            def link_alone(ins):
                link(ins)
                dve.sem_inc(vec_held, 1)

            def residual(w, u, layer, use):
                wait_use(dve, w, pa_ready[u], use, 4)
                nc.vector.tensor_tensor(sides(qf[u][:, :]), sides(qf[u][:, :]), part(u, 0), ALU.subtract).then_inc(r_ready[u], 1)

            def third_part(w, u, layer):
                wait_use(dve, w, pb_ready[u], SPLIT_USE[layer], 4)
                nc.vector.tensor_tensor(part(u, 2), sides(qf[u][:, :]), part(u, 1), ALU.subtract).then_inc(parts_ready[u], 1)

            def statistics(u, src, eps):
                link_alone(nc.vector.bn_stats(st[u][:, 0:6], src))
                link(nc.vector.bn_aggr(st[u][:, 8:10], st[u][:, 0:6]))
                nc.vector.tensor_scalar(st[u][:, 10:11], st[u][:, 9:10], eps, None, ALU.add).then_inc(var_ready[u], 1)

            def layer_norm(w, u, layer, dst, ready):
                wait_use(dve, w, rstd_ready[u], NORM_USE[layer], 7)
                nc.vector.tensor_scalar(dst, yb[u][:, :], st[u][:, 8:9], st[u][:, 11:12], ALU.subtract, ALU.mult)\
                  .then_inc(ready, 1)

            def maxima(w, u, stage):
                layer, c = stage[:-3], int(stage[-1])
                s = wait_full(dve, w, "sc", stage, u)
                if layer == "l0":
                    half, i0 = c // 2, 2 * (c % 2)
                    dst = nm[u][:, :].rearrange("p (t g i) -> p t i g", t=2, g=4)[:, half, i0:i0 + 2, :]
                    src = sc[:, s, :].rearrange("p (i g n) -> p i g n", i=2, g=4)
                elif layer == "x0":
                    dst = nm[u][:, 4 * c:4 * c + 4]
                    src = sc[:, s, :].rearrange("p (a n) -> p a n", a=4)
                else:
                    dst = nm[u][:, 8 * c:8 * c + 8]
                    src = sc[:, s, :].rearrange("p (a n) -> p a n", a=8)
                nc.vector.tensor_reduce(dst, src, AX.X, ALU.max, negate=True).then_inc(ring_free["sc"][s], 1)

            def max_parts(w, u, layer, rows):
                for c in range(CHUNKS[layer] - 2, CHUNKS[layer]):
                    wait_freed(dve, w, "sc", f"{layer}_S{c}", u)
                link(nc.vector.tensor_copy(nh[u][:, 0:rows], nm[u][:, 0:rows]))
                nc.vector.tensor_tensor(nh[u][:, rows:2 * rows], nm[u][:, 0:rows], nh[u][:, 0:rows], ALU.subtract).then_inc(mh_ready[u], 1)

            def add_residual(w, u, stage, x):
                slot = wait_full(dve, w, "pr", stage, u)
                ins = nc.vector.tensor_tensor(yb[u][:, :], pr[:, slot, 0:D], x, ALU.add)
                ins.then_inc(ring_free["pr"][slot], 1)
                slot = wait_freed(dve, w, "pr", stage, u)

            def step(stage, u, w):
                here[0] = w
                x = xc[u][:, 0:D]
                if stage == "ctxT":
                    wait_use(dve, w, in_loaded[u], 3, 3, 16)
                    nc.vector.tensor_scalar(mr[u][:, :], mr8[u][:, :], -1.0, -NEG, ALU.add, ALU.mult).then_inc(mask_ready[u], 1)
                    nc.vector.tensor_scalar(mk[u][:, :], mk8[u][:, :], -1.0, -NEG, ALU.add, ALU.mult).then_inc(mask_ready[u], 1)
                elif stage in ("l0_qk", "l1_qk"):
                    layer = stage[:-3]
                    b_qk, bc_v = (b_qk0, bc_v0) if layer == "l0" else (b_qk1, bc_v1)
                    slot = wait_full(dve, w, "pr", stage, u, 0)
                    src = pr[:, slot, :].rearrange("p (a n) -> p a n", a=4)
                    bias = b_qk[:, :].unsqueeze(2).broadcast_to([128, 4, 128])
                    nc.vector.tensor_tensor(qf[u][:, :].rearrange("p (a n) -> p a n", a=4), src, bias, ALU.add)\
                      .then_inc(ring_free["pr"][slot], 1)
                    slot = wait_full(dve, w, "pr", stage, u, 1)
                    if layer == "l0":
                        dst, dims, kw = pads(v0[u], 8, 4, 8), "p (b h c) -> p b h c", dict(b=8, h=4)
                    else:
                        dst, dims, kw = pads(vb[u], 8, 2, 16), "p (b h c) -> p b h c", dict(b=8, h=2)
                    nc.vector.tensor_tensor(dst, pr[:, slot, 0:D].rearrange(dims, **kw), bc_v[:, :].rearrange(dims, **kw), ALU.add)\
                      .then_inc(ring_free["pr"][slot], 1)
                elif stage in ("l0_r", "l1_r"):
                    residual(w, u, stage[:-2], SPLIT_USE[stage[:-2]])
                elif stage == "x0_r":
                    wait_use(dve, w, pa_ready[u], SPLIT_USE["x0"], 4)
                    nc.vector.tensor_tensor(sides(qf[u][:, :]), sides(xc[u][:, :]), part(u, 0), ALU.subtract).then_inc(r_ready[u], 1)
                elif stage == "c_r":
                    wait_use(dve, w, pa_ready[u], SPLIT_USE["c"], 4)
                    slot, _ = at_slot(w, "pr", "c_qk", u, 0)
                    link(nc.vector.tensor_tensor(sides(qf[u][:, :]), sides(pr[:, slot, :]), part(u, 0), ALU.subtract))
                    dve.sem_inc(ring_free["pr"][slot], 1)
                    dve.sem_inc(r_ready[u], 1)
                elif stage in ("l0_c", "x0_c", "l1_c", "c_c"):
                    third_part(w, u, stage[:-2])
                elif stage[:-1] in ("l0_S", "x0_S", "c_S"):
                    maxima(w, u, stage)
                elif stage in ("l0_mx", "x0_mx", "c_mx"):
                    max_parts(w, u, stage[:-3], H0 if stage == "l0_mx" else 16)
                elif stage == "l0_n":
                    slot = wait_attended(dve, w, "l0", u)
                    link(nc.vector.reciprocal(qf[u][:, 0:D], ob[:, slot, D:2 * D]))
                    nc.vector.tensor_tensor(xt[u][:, :, :].rearrange("p k n -> p (k n)"), ob[:, slot, 0:D], qf[u][:, 0:D], ALU.mult)\
                      .then_inc(ring_free["o"][slot], 1)
                elif stage == "x0_n":
                    slot = wait_attended(dve, w, "x0", u)
                    link(nc.vector.reciprocal(qf[u][:, 0:D], ob[:, slot, D:2 * D]))
                    link(nc.vector.tensor_tensor(yb[u][:, :], ob[:, slot, 0:D], qf[u][:, 0:D], ALU.mult))
                    dve.sem_inc(ring_free["o"][slot], 1)
                    link(nc.vector.tensor_tensor(yb[u][:, :], yb[u][:, :], x, ALU.add))
                    statistics(u, yb[u][:, :], LN_EPS)
                elif stage == "c_n":
                    slot = wait_attended(dve, w, "c", u)
                    link(nc.vector.tensor_scalar(qf[u][:, D:2 * D], ob[:, slot, D:2 * D], 1e-30, None, ALU.max))
                    link(nc.vector.reciprocal(qf[u][:, 0:D], qf[u][:, D:2 * D]))
                    nc.vector.tensor_tensor(xt[u][:, :, :].rearrange("p k n -> p (k n)"), ob[:, slot, 0:D], qf[u][:, 0:D], ALU.mult)\
                      .then_inc(ring_free["o"][slot], 1)
                elif stage in ("l0_o", "l1_o"):
                    wait_use(dve, w, xb_ready[u], 1 if stage == "l0_o" else 2, 2)
                    add_residual(w, u, stage, yb[u][:, :])
                    statistics(u, yb[u][:, :], LN_EPS)
                elif stage == "f_o":
                    add_residual(w, u, stage, x)
                    statistics(u, yb[u][:, :], LN_EPS)
                elif stage == "c_o":
                    slot = wait_full(dve, w, "pr", stage, u)
                    link(nc.vector.scalar_tensor_tensor(yb[u][:, :], yb[u][:, :], 1.0, pr[:, slot, 0:D], ALU.add, ALU.mult))
                    dve.sem_inc(ring_free["pr"][slot], 1)
                    link(nc.vector.tensor_tensor(yb[u][:, :], yb[u][:, :], x, ALU.add))
                    statistics(u, yb[u][:, :], LN_EPS)
                elif stage in ("l0_ln", "x0_ln", "f_ln", "l1_ln", "c_ln"):
                    layer_norm(w, u, stage[:-3], x, x_ready[u])
                elif stage == "c_rms":
                    wait_use(dve, w, x_ready[u], X_USE["l1"], 5)
                    link_alone(nc.vector.bn_stats(st[u][:, 0:6], x))
                    link(nc.vector.bn_aggr(st[u][:, 8:10], st[u][:, 0:6]))
                    link(nc.vector.scalar_tensor_tensor(st[u][:, 12:13], st[u][:, 8:9], st[u][:, 8:9], st[u][:, 9:10], ALU.mult, ALU.add))
                    nc.vector.tensor_scalar(st[u][:, 10:11], st[u][:, 12:13], RMS_EPS, None, ALU.add).then_inc(var_ready[u], 1)
                elif stage == "c_xT":
                    wait_use(dve, w, rstd_ready[u], NORM_USE["c_rms"], 7)
                    nc.vector.tensor_scalar(yb[u][:, :], x, st[u][:, 11:12], None, ALU.mult)\
                      .then_inc(xn_ready[u], 1)
                elif stage in ("f_gu0", "f_gu1"):
                    ht = sq[u][:, :].bitcast(f32)
                    c = int(stage[-1])
                    n, first = (512, 0) if c == 0 else (256, 512)
                    s, _ = at_slot(w, "sc", stage, u)
                    space = ffn_space(u)[c]
                    wait_use(dve, w, tanh_ready[u], c + 1, 2)
                    link(nc.vector.scalar_tensor_tensor(space, space, 1.0, sc[:, s, 0:n], ALU.add, ALU.mult))
                    nc.vector.tensor_tensor(ht[:, first:first + n], space, sc[:, s, n:2 * n], ALU.mult)\
                      .then_inc(ring_free["sc"][s], 1)
                elif stage[:-1] == "l1_P":
                    c = int(stage[-1])
                    s = wait_full(dve, w, "sc", stage, u)
                    p = wait_free(dve, w, "p", stage, u)
                    nc.vector.tensor_tensor(pb[:, p, :], sc[:, s, :], decay[:, 8 * c:8 * c + 8, :].rearrange("p h n -> p (h n)"), ALU.mult)\
                      .then_inc(ring_full["p"][p], 1)
                elif stage == "m_a":
                    s, _ = at_slot(w, "o", stage, u)
                    wait_use(dve, w, logits_ready[u], 1, 1)
                    dve.sem_inc(vec_held, 1)
                    logits = ob[:, s, MW - E:MW]
                    link_alone(nc.vector.max(st[u][:, 24:32], logits))
                    link(nc.vector.max_index(ix[u][:, :], st[u][:, 24:32], logits))
                    link(nc.vector.tensor_copy(st[u][:, 32:34], ix[u][:, 0:2]))
                    nc.vector.tensor_tensor(st[u][:, 19:20], st[u][:, 25:26], st[u][:, 24:25], ALU.subtract).then_inc(gap_ready[u], 1)
                elif stage == "m_b":
                    s, _ = at_slot(w, "o", "m_a", u)
                    wait_use(dve, w, egap_ready[u], 1, 1)
                    link(nc.vector.tensor_scalar(st[u][:, 21:22], st[u][:, 20:21], 1.0, 0.5, ALU.add, ALU.mult))
                    link(nc.vector.reciprocal(st[u][:, 22:23], st[u][:, 21:22]))
                    link(nc.vector.tensor_tensor(st[u][:, 23:24], st[u][:, 22:23], st[u][:, 20:21], ALU.mult))
                    link(nc.vector.tensor_scalar(st[u][:, 0:8], iota8[:, :], st[u][:, 32:33], st[u][:, 22:23], ALU.is_equal, ALU.mult))
                    link(nc.vector.tensor_scalar(st[u][:, 24:32], iota8[:, :], st[u][:, 33:34], st[u][:, 23:24], ALU.is_equal, ALU.mult))
                    link(nc.vector.tensor_tensor(st[u][:, 0:8], st[u][:, 0:8], st[u][:, 24:32], ALU.add))
                    nc.vector.tensor_tensor(yb[u][:, 0:128].rearrange("p (e r) -> p e r", e=E),
                                            ob[:, s, D:D + E * R].rearrange("p (e r) -> p e r", e=E),
                                            st[u][:, 0:8].unsqueeze(2).broadcast_to([128, E, R]), ALU.mult).then_inc(axw_ready[u], 1)
                elif stage == "m_o":
                    s, _ = at_slot(w, "o", "m_a", u)
                    wait_use(dve, w, expert_ready[u], 1, 1)
                    link(nc.vector.tensor_tensor(yb[u][:, :], ob[:, s, 0:D], x, ALU.add))
                    dve.sem_inc(ring_free["o"][s], 1)
                    statistics(u, yb[u][:, :], LN_EPS)
                elif stage == "m_ln":
                    layer_norm(w, u, "m", qf[u][:, 0:D], o_ready[u])

            run(dve, step)
            assert steps[0] == 2 * VEC_STEPS, steps[0]

        @block.tensor
        def _(pe):
            pe.wait_ge(w_loaded, N_W)
            pe.wait_ge(w_scaled, N_SCALED)
            pe.wait_ge(ones_set, 2)
            pe.wait_ge(keys_ones, U)

            def transpose2(w, u, stage, src):
                slot = wait_free(pe, w, "pr", stage, u)
                for k in range(KT):
                    ins = nc.tensor.transpose(pr[:, slot, 128 * k:128 * k + 128], src[:, 128 * k:128 * k + 128], ident[:, :])
                ins.then_inc(ring_full["pr"][slot], 1)

            def project(w, u, stage, k, work):
                slot = wait_free(pe, w, "pr", stage, u, k)
                for cols, left, right, tiles in work:
                    for i in range(tiles):
                        ins = nc.tensor.matmul(pr[:, slot, cols], left(i), right(i), start=(i == 0), stop=(i == tiles - 1))
                ins.then_inc(ring_full["pr"][slot], 1)

            def qk_work(u, w):
                return [(slice(128 * a, 128 * a + 128), lambda i, a=a: w[:, i, 128 * a:128 * a + 128], lambda i: xt[u][:, i, :], KT)
                        for a in range(4)]

            def out_work(u, w, src, tiles=KT):
                return [(slice(0, D), lambda i: src[:, i, :], lambda i: w[:, i, :], tiles)]

            def head0(n):
                half, i, g = n // 16, n // 4 % 4, n % 4
                return (4 * half + g) * 4 + i

            def head1(n):
                half, i, g = n // 8, n // 4 % 2, n % 4
                return (4 * half + g) * 2 + i

            def scores0(w, u, stage, k, left, right, mask):
                c, s = int(stage[-1]), wait_free(pe, w, "sc", stage, u)
                for j in range(2):
                    nc.tensor.matmul(sc[:, s, 512 * j:512 * j + 512], identb[:, :], mask[:, :].unsqueeze(1).broadcast_to([128, 4, 128]),
                                     start=True, stop=False, skip_group_check=True)
                for n in range(8):
                    h = head0(8 * c + n)
                    cols = slice(128 * h, 128 * h + 128)
                    ins = nc.tensor.matmul(sc[:, s, 128 * n:128 * n + 128], left[0:k, cols], right[0:k, cols],
                                           start=False, stop=(n % 4 == 3), skip_group_check=True)
                ins.then_inc(ring_full["sc"][s], 1)

            def scores_x(w, u, stage, k, left, right):
                c, s = int(stage[-1]), wait_free(pe, w, "sc", stage, u)
                for n in range(2):
                    h = 2 * c + n if stage[3] == "S" else headx(2 * c + n)
                    for half in range(2):
                        a = 256 * h + 128 * half
                        ins = nc.tensor.matmul(sc[:, s, 512 * n + 256 * half:512 * n + 256 * half + 256], left[0:k, a:a + 128],
                                               right[0:k, 256 * h:256 * h + 256], start=True, stop=True)
                ins.then_inc(ring_full["sc"][s], 1)

            def headx(n):
                return 2 * (n % 4) + n // 4

            def scores1(w, u, stage, k, left, right, row=None):
                c, s = int(stage[-1]), wait_free(pe, w, "sc", stage, u)
                if row is not None:
                    for j in range(2):
                        nc.tensor.matmul(sc[:, s, 512 * j:512 * j + 512], ones_row[:, :], row[:, :].unsqueeze(1).broadcast_to([1, 4, 128]),
                                         start=True, stop=False, skip_group_check=True)
                for n in range(8):
                    h = 8 * c + n if row is not None else head1(8 * c + n)
                    cols = slice(128 * h, 128 * h + 128)
                    ins = nc.tensor.matmul(sc[:, s, 128 * n:128 * n + 128], left[0:k, cols], right[0:k, cols],
                                           start=(row is None), stop=True, skip_group_check=True)
                ins.then_inc(ring_full["sc"][s], 1)

            def values(w, u, stage, todo):
                layer, c = stage[:-3], stage[-1]
                if c == "0":
                    wait_free(pe, w, "o", f"{layer}_P0", u)
                    if layer == "x0":
                        wait_use(pe, w, ct_ready[u], 1, 1)
                    else:
                        wait_freed(pe, w, "pr", f"{layer}_qk", u, 1)
                slot, _ = at_slot(w, "o", f"{layer}_P0", u)
                p = wait_full(pe, w, "p", f"{layer}_P{c}", u)
                pe.sem_inc(ring_free["sc"][at_slot(w, "sc", f"{layer}_P{c}", u)[0]], 1)
                for kind in range(2):
                    for g, src, cols, first, v, ones in todo:
                        w = v if kind == 0 else ones
                        if w is None:
                            continue
                        dst = cols if kind == 0 else slice(cols.start + D, cols.stop + D)
                        ins = nc.tensor.matmul(ob[32 * g:32 * g + 32, slot, dst], w, pb[:, p, src],
                                               start=(first and kind == 0), stop=True, skip_group_check=True)
                ins.then_inc(ring_free["p"][p], 1)

            def values_of(u, layer, c):
                todo = []
                if layer == "l0":
                    for n in range(8):
                        h, m = head0(8 * c + n), 8 * c + n
                        half, i, g = m // 16, m // 4 % 4, m % 4
                        todo.append((g, slice(128 * n, 128 * n + 128), slice(128 * half, 128 * half + 128), half == 0 and i == 0,
                                     v0[u][:, h, :], ones8[:, i, :]))
                elif layer == "x0":
                    for n in range(2):
                        h = headx(2 * c + n)
                        for half in range(2):
                            todo.append((h // 2, slice(512 * n + 256 * half, 512 * n + 256 * half + 256), slice(0, D), h % 2 == 0 and half == 0,
                                         vb[u][:, 8 * half + h, :], ones16[:, h % 2, :]))
                else:
                    for n in range(8):
                        h, m = head1(8 * c + n), 8 * c + n
                        half, i, g = m // 8, m // 4 % 2, m % 4
                        todo.append((g, slice(128 * n, 128 * n + 128), slice(128 * half, 128 * half + 128), half == 0 and i == 0,
                                     vb[u][:, h, :], ones16[:, i, :] if layer == "c" else None))
                return todo

            def xt_in(w, u, stage):
                slot = wait_freed(pe, w, "pr", stage.split("_")[0] + "_xT", u)

            def stack_in(w, u, layer):
                pe.wait_ge(stack_loaded[u], w.at(16 * 23, 16 * LOADS_UP_TO[layer]))

            def step(stage, u, w):
                x = xc[u][:, 0:D]
                if stage == "ctxT":
                    wait_use(pe, w, in_loaded[u], 3, 3, 16)
                    transpose2(w, u, stage, xc[u][:, D:2 * D])
                elif stage == "l0_xT":
                    transpose2(w, u, stage, x)
                elif stage in ("f_xT", "l1_xT", "m_xT"):
                    before = {"f": "x0", "l1": "f", "m": "c"}[stage[:-3]]
                    wait_use(pe, w, x_ready[u], X_USE[before], 5)
                    transpose2(w, u, stage, x)
                elif stage == "c_xT":
                    wait_use(pe, w, xn_ready[u], 1, 1)
                    transpose2(w, u, stage, yb[u][:, :])
                elif stage in ("l0_qk", "l1_qk"):
                    w_qk, w_v = (w_qk0, w_v0) if stage == "l0_qk" else (w_qk1, w_v1)
                    xt_in(w, u, stage)
                    project(w, u, stage, 0, qk_work(u, w_qk))
                    project(w, u, stage, 1, out_work(u, w_v, xt[u]))
                elif stage == "c_qk":
                    xt_in(w, u, stage)
                    wait_use(pe, w, ct_ready[u], 1, 1)
                    q_and_k = qk_work(u, w_qkc)
                    q_and_k = q_and_k[:2] + [(cols, left, lambda i: ct[u][:, i, :], KT) for cols, left, _, _ in q_and_k[2:]]
                    project(w, u, stage, 0, q_and_k)
                    project(w, u, stage, 1, [(slice(0, D), lambda i: ct[u][:, i, :], lambda i: w_vgc[:, i, 0:D], KT),
                                              (slice(D, 2 * D), lambda i: xt[u][:, i, :], lambda i: w_vgc[:, i, D:2 * D], KT)])
                elif stage[:-1] == "l0_S":
                    stack_in(w, u, "l0")
                    scores0(w, u, stage, K0, sq[u], sk[u], alibi_qk)
                elif stage[:-1] == "x0_S":
                    stack_in(w, u, "x0")
                    scores_x(w, u, stage, K1, sq[u], sk[u])
                elif stage[:-1] == "c_S":
                    stack_in(w, u, "c")
                    wait_use(pe, w, mask_ready[u], 2, 2)
                    scores1(w, u, stage, K1, sq[u], sk[u], mr[u])
                elif stage in ("l0_mx", "x0_mx", "c_mx"):
                    layer, rows = stage[:-3], H0 if stage == "l0_mx" else 16
                    wait_use(pe, w, mh_ready[u], MAX_USE[layer], 3)
                    slot = wait_free(pe, w, "pr", stage, u)
                    nc.tensor.matmul(pr[0:2 * rows, slot, 0:128], nh[u][:, 0:2 * rows], identb[:, :], start=True, stop=True)\
                      .then_inc(ring_full["pr"][slot], 1)
                elif stage[:-1] == "l0_P":
                    wait_use(pe, w, max_loaded[u], 1, 3, 16)
                    scores0(w, u, stage, K0 + 2, sk[u], sq[u], causal_kq)
                elif stage[:-1] == "x0_P":
                    wait_use(pe, w, max_loaded[u], 2, 3, 16)
                    scores_x(w, u, stage, K1 + 2, sk[u], sq[u])
                elif stage[:-1] == "l1_P":
                    stack_in(w, u, "l1")
                    scores1(w, u, stage, K1, sk[u], sq[u])
                elif stage[:-1] == "c_P":
                    wait_use(pe, w, max_loaded[u], 3, 3, 16)
                    scores1(w, u, stage, K1 + 2, sk[u], sq[u])
                elif stage[:-1] in ("l0_V", "x0_V", "l1_V", "c_V"):
                    values(w, u, stage, values_of(u, stage[:-3], int(stage[-1])))
                elif stage in ("l0_o", "l1_o", "c_o"):
                    layer = stage[:-2]
                    wait_freed(pe, w, "o", f"{layer}_P0", u)
                    project(w, u, stage, 0, out_work(u, {"l0": w_p0, "l1": w_o1, "c": w_oc}[layer], xt[u]))
                elif stage in ("f_gu0", "f_gu1"):
                    xt_in(w, u, stage)
                    s = wait_free(pe, w, "sc", stage, u)
                    first, tiles = (0, 8) if stage == "f_gu0" else (1024, 4)
                    for a in range(tiles):
                        for i in range(KT):
                            ins = nc.tensor.matmul(sc[:, s, 128 * a:128 * a + 128], w_gu[:, i, first + 128 * a:first + 128 * a + 128],
                                                   xt[u][:, i, :], start=(i == 0), stop=(i == KT - 1))
                    ins.then_inc(ring_full["sc"][s], 1)
                elif stage == "f_o":
                    for c in range(2):
                        wait_freed(pe, w, "sc", f"f_gu{c}", u)
                    ht = sq[u][:, :].bitcast(f32)
                    slot = wait_free(pe, w, "pr", stage, u)
                    for j in range(FT):
                        ins = nc.tensor.matmul(pr[:, slot, 0:D], ht[:, 128 * j:128 * j + 128], w_dn[:, j, :], start=(j == 0), stop=(j == FT - 1))
                    ins.then_inc(ring_full["pr"][slot], 1)
                elif stage == "m_a":
                    xt_in(w, u, stage)
                    s = wait_free(pe, w, "o", stage, u)
                    for i in range(KT):
                        ins = nc.tensor.matmul(ob[:, s, 0:MW], xt[u][:, i, :], w_m[:, i, :], start=(i == 0), stop=(i == KT - 1), skip_group_check=True)
                    ins.then_inc(logits_ready[u], 1)
                elif stage == "m_b":
                    wait_use(pe, w, axw_ready[u], 1, 1)
                    slot = wait_free(pe, w, "pr", stage, u)
                    nc.tensor.transpose(pr[:, slot, 0:128], yb[u][:, 0:128], ident[:, :]).then_inc(ring_full["pr"][slot], 1)
                elif stage == "m_o":
                    slot = wait_freed(pe, w, "pr", "m_b", u)
                    s, _ = at_slot(w, "o", "m_a", u)
                    nc.tensor.matmul(ob[:, s, 0:D], yb[u][:, 128:256], w_b[:, :], start=False, stop=True, skip_group_check=True)\
                      .then_inc(expert_ready[u], 1)

            run(pe, step)


def layouts(a):
    def heads(hd):
        p = np.arange(128)
        groups = 128 // hd
        return np.concatenate([(2 * (p % groups) + tile) * hd + p // groups for tile in range(2)])

    def tiled(v):
        return np.ascontiguousarray(v.reshape(-1, 128).T)

    p0, p1 = heads(HD0), heads(HD1)
    q0, k0 = p0, D + p0
    q1, k1 = p1, D + p1
    wa, ba = a["L0_attn_W_attn"], a["L0_attn_b_attn"]
    w1, b1 = a["L1_attn_w_qkv"].T, a["L1_attn_b_qkv"]
    wide = np.zeros((D, FT * 128 - INTER), np.float32)
    g, up = np.concatenate([a["L0_ffn_gate_w"].T, wide], 1), np.concatenate([a["L0_ffn_up_w"].T, wide], 1)
    down = np.concatenate([a["L0_ffn_down_w"].T, np.zeros((FT * 128 - INTER, D), np.float32)], 0)
    mask = a["mask_BxS2_bk0"]
    start = 2.0 ** (-2.0 ** (-(np.log2(H1) - 3)))
    slopes = np.array([start ** (i + 1) for i in range(H1)], np.float32)
    lam = np.exp(-slopes).astype(np.float32)
    i = np.arange(128)
    diff = (i[None, :] - i[:, None]).astype(np.float32)
    n = np.arange(H1)
    order = (4 * (n // 8) + n % 4) * 2 + n // 4 % 2
    decay = np.where(diff[:, None, :] >= 0, lam[order][None, :, None] ** np.maximum(diff, 0)[:, None, :], 0).astype(np.float32)
    causal = np.where(diff >= 0, 0.0, NEG)
    alibi = np.where(i[None, :] <= i[:, None], i[None, :] * (SLOPE / SCALE0), NEG)
    ones8, ones16 = np.zeros((128, 4, 32), np.float32), np.zeros((128, 2, 32), np.float32)
    for j in range(4):
        ones8[:, j, 8 * j:8 * j + 8] = 1
    for j in range(2):
        ones16[:, j, 16 * j:16 * j + 16] = 1
    return {
        "xc": np.concatenate([a["x"], a["ctx_2048"]], 2), "mask_col": mask.reshape(B, 128, 1), "mask_row": mask.reshape(B, 1, 128),
        "w_qk0": wa[:, np.concatenate([q0, k0])], "w_v0": wa[:, 2 * D:], "w_p0": a["L0_attn_W_proj"],
        "b_qk0": tiled(ba[np.concatenate([q0, k0])]), "b_v0": ba[2 * D:], "b_p0": a["L0_attn_b_proj"],
        "w_gu": np.concatenate([g[:, :512], up[:, :512], g[:, 512:], up[:, 512:]], 1), "w_dn": down,
        "gate_s": a["L0_ffn_gate_s"], "up_s": a["L0_ffn_up_s"], "down_s": a["L0_ffn_down_s"],
        "w_qk1": w1[:, np.concatenate([q1, k1])], "w_v1": w1[:, 2 * D:], "w_o1": a["L1_attn_w_out"].T,
        "b_qk1": tiled(b1[np.concatenate([q1, k1])]), "b_v1": b1[2 * D:], "b_o1": a["L1_attn_b_out"],
        "norm_w": tiled(a["L1_xattn_norm_w"]),
        "w_qkc": np.concatenate([a["L1_xattn_wq"].T[:, p1], a["L1_xattn_wk"].T[:, p1]], 1),
        "w_vgc": np.concatenate([a["L1_xattn_wv"].T, a["L1_xattn_wg"].T], 1), "w_oc": a["L1_xattn_wo"].T,
        "w_m": np.concatenate([a["L1_ffn_weight"].T, a["L1_ffn_lora_A"].reshape(E * R, D).T, a["L1_ffn_router_w"].T], 1),
        "w_b": a["L1_ffn_lora_B"].transpose(0, 2, 1).reshape(E * R, D),
        "ident": np.eye(128, dtype=np.float32), "decay": decay,
        "causal_kq": causal.astype(np.float32), "alibi_qk": alibi.astype(np.float32), "key_bias": (i * SLOPE).astype(np.float32).reshape(128, 1),
        "iota8": np.tile(np.arange(E, dtype=np.float32), (128, 1)), "ones8": ones8, "ones16": ones16,
    }


def kernel(**inputs):
    import concourse.bacc as bacc
    from concourse.bass_utils import run_bass_kernel_spmd

    nc = bacc.Bacc("TRN2", target_bir_lowering=False, num_devices=1)
    arrays, t = {}, {}
    for name, a in layouts({k: np.asarray(v) for k, v in inputs.items()}).items():
        a = np.ascontiguousarray(a)
        arrays[f"in_{name}"] = a
        t[name] = nc.dram_tensor(f"in_{name}", a.shape, mybir.dt.from_np(a.dtype), kind="ExternalInput").ap()
    out = nc.dram_tensor("out", (B, T, D), f32, kind="ExternalOutput").ap()
    decoder_kernel(nc, t, out)
    r = run_bass_kernel_spmd(nc, [arrays], core_ids=[0])
    return r.results[0]["out"]
```

```python
import numpy as np
import concourse.bass as bass
from concourse import mybir
from contextlib import ExitStack

f32, bf16, u8, u32 = mybir.dt.float32, mybir.dt.bfloat16, mybir.dt.uint8, mybir.dt.uint32
ACT = mybir.ActivationFunctionType
ALU = mybir.AluOpType
AX = mybir.AxisListType

B, T, D = 16, 128, 256
U = 4
NIT = B // U
KT = D // 128
H0, H1 = 32, 16
INTER, FT = 704, 6
E, R = 8, 16
MW = D + E * R + E
NEG = -1e30
LN_EPS, RMS_EPS = 1e-5, 1e-6
SLOPE = 2.0 ** (-8.0 / H0)
SCALE0, SCALEX = float(8) ** -0.5, 0.25
HD0, HD1 = 8, 16
K0 = 9 * HD0
K1 = 6 * HD1


def scores(layer, chunks):
    return [f"{layer}_{step}{c}" for c in range(chunks) for step in "PV"]


QUARTERS = [
    ["load", "ctx_v", "l0_qk", "l0_r", "l0_c", "l0_ld", "l0_S0", "l0_S1", "l0_S2", "l0_S3", "l0_mx",
     *scores("l0", 4), "l0_n", "l0_o", "l0_ln", "x0_a", "x0_r", "x0_c"],
    ["x0_ld", "x0_S0", "x0_S1", "x0_S2", "x0_S3", "x0_mx", *scores("x0", 4), "x0_n", "x0_ln"],
    ["f_xT", "f_gu0", "f_gu1", "f_o", "f_ln", "l1_xT", "l1_qk", "l1_r", "l1_c", "l1_ld", *scores("l1", 2),
     "l1_n", "l1_o", "l1_ln", "c_rms", "c_xT", "c_qk", "c_r", "c_c"],
    ["c_ld", "c_S0", "c_S1", "c_mx", *scores("c", 2), "c_n", "c_o", "c_ln", "m_xT", "m_a", "m_b", "m_o", "m_ln"],
]
MERGED = """
f_xT load x0_ld f_gu0 ctx_v f_gu1 l0_qk l0_r c_ld l0_c f_o c_S0 c_S1 f_ln l0_ld l1_xT c_mx x0_S0 x0_S1 l1_qk l0_S0
l0_S1 l0_S2 l0_S3 c_P0 l0_mx l1_r x0_S2 l1_c c_V0 c_P1 l0_P0 x0_S3 c_V1 l0_V0 c_n l1_ld l0_P1 x0_mx l0_V1 l0_P2
l1_P0 c_o l0_V2 l0_P3 l1_V0 l1_P1 l0_V3 c_ln l1_V1 l1_n l0_n m_xT x0_P0 l1_o l0_o m_a x0_V0 x0_P1 l0_ln l1_ln x0_V1
m_b x0_a c_rms x0_P2 x0_r m_o x0_V2 c_xT x0_P3 m_ln x0_V3 c_qk x0_c x0_n c_r x0_ln c_c
""".split()


SLOTS = {"sc": 2, "pr": 2, "o": 2, "p": 3}
TAKES = {
    "sc": {"f_gu0": 1, "f_gu1": 1},
    "pr": {"l0_qk": 2, "l0_mx": 1, "l0_o": 1, "x0_mx": 1, "f_xT": 1, "f_o": 1, "l1_xT": 1,
           "l1_qk": 2, "l1_o": 1, "c_xT": 1, "c_qk": 2, "c_mx": 1, "c_o": 1, "m_xT": 1, "m_b": 1},
    "o": {"l0_P0": 1, "x0_P0": 1, "l1_P0": 1, "c_P0": 1, "m_a": 1},
    "p": {},
}
CHUNKS = {"l0": 4, "x0": 4, "l1": 2, "c": 2}
for _layer, _chunks in CHUNKS.items():
    for _c in range(_chunks):
        TAKES["sc"][f"{_layer}_S{_c}"] = TAKES["sc"][f"{_layer}_P{_c}"] = TAKES["p"][f"{_layer}_P{_c}"] = 1
RING_TOTAL = {ring: U * sum(takes[s] for q in QUARTERS for s in q if s in takes) for ring, takes in TAKES.items()}
RELEASED_BY = {("o", "m_a"): "m_o", ("pr", "c_qk"): "c_r"}
for _layer, _chunks in CHUNKS.items():
    RELEASED_BY["o", f"{_layer}_P0"] = f"{_layer}_n"
    for _c in range(_chunks):
        RELEASED_BY["p", f"{_layer}_P{_c}"] = f"{_layer}_V{_c}"


def merged():
    of = {step: q for q, quarter in enumerate(QUARTERS) for step in quarter}
    for q, quarter in enumerate(QUARTERS):
        assert [step for step in MERGED if of[step] == q] == quarter
    done, held = {"load"}, {ring: ["load"] * n for ring, n in SLOTS.items()}
    for step in MERGED:
        for ring in SLOTS:
            n = TAKES[ring].get(step, 0)
            assert all(RELEASED_BY.get((ring, s), s) in done for s in held[ring][-SLOTS[ring]:][:n]), (step, ring)
            held[ring] += [step] * n
        done.add(step)
    return [(step, of[step]) for step in MERGED]


def sections():
    steps = []
    for k in range(4):
        for s, q in merged():
            u = (q - k) % 4
            steps.append((s, u, 1 if u + k >= 4 else 0))
    return {"first": [e for e in steps if e[2] == 1], "body": steps, "last": [e for e in steps if e[2] == 0]}


ORDER = sections()



def first_use():
    at = {}
    for ring, takes in TAKES.items():
        n = 0
        for section, steps in ORDER.items():
            if section == "last":
                n += (NIT - 2) * RING_TOTAL[ring]
            for stage, u, _ in steps:
                at[section, ring, stage, u] = n
                n += takes.get(stage, 0)
        assert RING_TOTAL[ring] % SLOTS[ring] == 0
    return at


RING_AT = first_use()

X_USE = {"l0": 1, "x0": 2, "f": 3, "l1": 4, "c": 5}
SPLIT_USE = {"l0": 1, "x0": 2, "l1": 3, "c": 4}
MAX_USE = {"l0": 1, "x0": 2, "c": 3}
NORM_USE = {"l0": 1, "x0": 2, "f": 3, "l1": 4, "c_rms": 5, "c": 6, "m": 7}
PART = 128 * 256
STORES_UP_TO, STORES = {"l0": 1, "x0": 7, "l1": 8, "c": 9}, 9
LOADS_UP_TO = {"l0": 5, "x0": 11, "l1": 17, "c": 23}
VEC_STEPS = 144 + 3 * U


class When:

    def __init__(self, section, group, lead, loop):
        self.section, self.group, self.lead, self.loop = section, group, lead, loop

    def at(self, per_group, extra):
        return self.group * per_group + (self.lead * per_group + extra)

    def batch(self, u):
        return self.group * U + (self.lead * U + u)


def run(engine, step):
    for stage, u, _ in ORDER["first"]:
        step(stage, u, When("first", 0, 0, 0))
    with engine.Fori(0, NIT - 1) as it:
        for stage, u, lead in ORDER["body"]:
            step(stage, u, When("body", it, lead, it))
    for stage, u, _ in ORDER["last"]:
        step(stage, u, When("last", NIT - 1, 0, 0))


def decoder_kernel(nc, t, out):
    ctx = ExitStack()
    with ctx:
        def sb(name, shape, dt=f32):
            return ctx.enter_context(nc.sbuf_tensor(name, shape, dt))

        def sem(name):
            return ctx.enter_context(nc.semaphore(name))

        def per_u(name):
            return [sem(f"{name}{u}") for u in range(U)]

        w_qk0, w_v0, w_p0 = sb("w_qk0", [128, KT, 512]), sb("w_v0", [128, KT, D]), sb("w_p0", [128, KT, D])
        w_gu, w_dn = sb("w_gu", [128, KT, 2 * FT * 128]), sb("w_dn", [128, FT, D])
        w_qk1, w_v1, w_o1 = sb("w_qk1", [128, KT, 512]), sb("w_v1", [128, KT, D]), sb("w_o1", [128, KT, D])
        w_qkc, w_vgc, w_oc = sb("w_qkc", [128, KT, 512]), sb("w_vgc", [128, KT, 512]), sb("w_oc", [128, KT, D])
        w_m, w_b = sb("w_m", [128, KT, MW]), sb("w_b", [128, D])
        b_qk0, b_qk1 = sb("b_qk0", [128, 4]), sb("b_qk1", [128, 4])
        bc_v0, bc_p0, bc_v1, bc_o1 = (sb(n, [128, D]) for n in ("bc_v0", "bc_p0", "bc_v1", "bc_o1"))
        norm_w = sb("norm_w", [128, KT])
        ident, identb = sb("ident", [128, 128]), sb("identb", [128, 128], bf16)
        decay = sb("decay", [128, H1, 128])
        causal_kq, alibi_qk = sb("causal_kq", [128, 128], bf16), sb("alibi_qk", [128, 128], bf16)
        key_bias, iota8 = sb("key_bias", [128, 1]), sb("iota8", [128, E])
        ones8, ones16 = sb("ones8", [128, 4, 32]), sb("ones16", [128, 2, 32])
        minus_half = sb("minus_half", [128, 1])

        loaded = [sb(f"loaded{u}", [128, 4 * D]) for u in range(U)]
        xc = [a[:, 0:2 * D] for a in loaded]
        xt, ct = ([a[:, at * D:(at + 1) * D].rearrange("p (k n) -> p k n", k=KT) for a in loaded]
                  for at in (2, 3))
        qf = [sb(f"qf{u}", [128, 512]) for u in range(U)]
        pt = [sb(f"pt{u}", [128, 2, 3, 256], bf16) for u in range(U)]
        sq = [sb(f"sq{u}", [128, 4096], bf16) for u in range(U)]
        sk = [sb(f"sk{u}", [128, 4096], bf16) for u in range(U)]
        v0 = [sb(f"v0{u}", [128, H0, 32]) for u in range(U)]
        vb = [sb(f"vb{u}", [128, H1, 32]) for u in range(U)]
        yb = [sb(f"yb{u}", [128, D]) for u in range(U)]
        nm = [sb(f"nm{u}", [128, H0]) for u in range(U)]
        nh = [sb(f"nh{u}", [128, 2 * H0], bf16) for u in range(U)]
        mx = [sb(f"mx{u}", [2 * H0, 128], bf16) for u in range(U)]
        st = [sb(f"st{u}", [128, 40]) for u in range(U)]
        ix = [sb(f"ix{u}", [128, 8], u32) for u in range(U)]
        mk8 = [sb(f"mk8{u}", [128, 1], u8) for u in range(U)]
        mr8 = [sb(f"mr8{u}", [128, 128], u8) for u in range(U)]
        mk = [sb(f"mk{u}", [128, 1]) for u in range(U)]
        mr = [sb(f"mr{u}", [128, 128], bf16) for u in range(U)]
        pb = sb("pb", [128, SLOTS["p"], 1024])

        sc = ctx.enter_context(nc.psum_tensor("sc", [128, 2, 1024], f32))
        pr = ctx.enter_context(nc.psum_tensor("pr", [128, 2, 512], f32))
        ob = ctx.enter_context(nc.psum_tensor("ob", [128, 2, 512], f32))
        scratch = [nc.dram_tensor(f"scratch{u}", (2 * 3 * 128 * 256,), bf16, kind="Internal").ap() for u in range(U)]

        ring_full = {r: [sem(f"{r}_full{i}") for i in range(n)] for r, n in SLOTS.items()}
        ring_free = {r: [sem(f"{r}_free{i}") for i in range(n)] for r, n in SLOTS.items()}
        first_loaded, early_loaded, w_loaded = sem("first_loaded"), sem("early_loaded"), sem("w_loaded")
        scales_loaded, w_scaled, narrowed = sem("scales_loaded"), sem("w_scaled"), sem("narrowed")
        pads_zero, ones_set, keys_ones = sem("pads_zero"), sem("ones_set"), sem("keys_ones")
        vec_held = sem("vec_held")
        in_loaded, out_stored = per_u("in_loaded"), per_u("out_stored")
        x_ready, xn_ready = per_u("x_ready"), per_u("xn_ready")
        pa_ready, r_ready = per_u("pa_ready"), per_u("r_ready")
        pb_ready, parts_ready = per_u("pb_ready"), per_u("parts_ready")
        parts_stored, stack_loaded = per_u("parts_stored"), per_u("stack_loaded")
        ct_ready = per_u("ct_ready")
        mh_ready, max_loaded = per_u("mh_ready"), per_u("max_loaded")
        var_ready, rstd_ready, xb_ready = per_u("var_ready"), per_u("rstd_ready"), per_u("xb_ready")
        tanh_ready, mask_ready = per_u("tanh_ready"), per_u("mask_ready")
        gap_ready, egap_ready, axw_ready = per_u("gap_ready"), per_u("egap_ready"), per_u("axw_ready")
        logits_ready, expert_ready, o_ready, vec_step = per_u("logits_ready"), per_u("expert_ready"), per_u("o_ready"), sem("vec_step")

        wide_masks = [pb[:, 2, D + 128 * i:D + 128 * i + 128] for i in range(2)]
        ffn_weights = [(w_gu, "w_gu"), (w_dn, "w_dn")]
        weights = [(w_qk1, "w_qk1"),
                   (w_v1, "w_v1"), (w_o1, "w_o1"), (w_qkc, "w_qkc"), (w_vgc, "w_vgc"), (w_oc, "w_oc"), (w_m, "w_m")]
        plain = [(w_b, "w_b"), (b_qk1, "b_qk1"), (decay, "decay"), (iota8, "iota8"), (norm_w, "norm_w")]
        first = [(w_qk0, "w_qk0"), (b_qk0, "b_qk0"), (w_v0, "w_v0")]
        first_spread = [(bc_v0, "b_v0")]
        early = [(ident, "ident"), (wide_masks[0], "causal_kq"),
                 (wide_masks[1], "alibi_qk"), (key_bias, "key_bias"), (ones8, "ones8"), (ones16, "ones16"), (w_p0, "w_p0")]
        early_spread = [(bc_p0, "b_p0")]
        spread = [(bc_v1, "b_v1"), (bc_o1, "b_o1")]
        N_SCALED = 2 + 4 * KT + FT + 1 + 2 * KT
        N_FIRST = 16 * (len(first) + len(first_spread))
        N_EARLY = 16 * (len(early) + len(early_spread))
        N_LATE = 16 * (len(ffn_weights) + len(weights) + len(plain) + len(spread))
        wide = sq[0][:, :].bitcast(f32)
        bc_gs, bc_us, bc_ds = wide[:, 0:FT * 128], wide[:, FT * 128:2 * FT * 128], wide[:, 2 * FT * 128:2 * FT * 128 + D]

        def ffn_space(u):
            return qf[u][:, :], pt[u][:, :, :, :].rearrange("p a b n -> p (a b n)").bitcast(f32)[:, 0:D]

        def enters(w, stage, u, name):
            return w.section == "first" and u == U - 1 and stage == name

        def part(u, c):
            return pt[u][:, :, c, :]

        def sides(ap):
            return ap.rearrange("p (s n) -> p s n", s=2)

        def on_all(name, n):
            return bass.AP(t[name].tensor, 0, [[0, 128], [1, n]])

        def flat(tensor, u_offset, *dims):
            return bass.AP(tensor, u_offset, [list(d) for d in dims])

        def pads(tensor, blocks, per, width):
            return bass.AP(tensor, 0, [[blocks * per * 32, 128], [per * 32, blocks], [32 + width, per], [1, width]])

        def at_slot(w, ring, stage, u, k=0):
            n = RING_AT[w.section, ring, stage, u] + k
            return n % SLOTS[ring], w.loop * (RING_TOTAL[ring] // SLOTS[ring]) + n // SLOTS[ring]

        def wait_full(eng, w, ring, stage, u, k=0):
            slot, before = at_slot(w, ring, stage, u, k)
            eng.wait_ge(ring_full[ring][slot], before + 1)
            return slot

        def wait_free(eng, w, ring, stage, u, k=0):
            slot, before = at_slot(w, ring, stage, u, k)
            eng.wait_ge(ring_free[ring][slot], before + 1)
            return slot

        def wait_freed(eng, w, ring, stage, u, k=0):
            slot, before = at_slot(w, ring, stage, u, k)
            eng.wait_ge(ring_free[ring][slot], before + 2)
            return slot

        def wait_attended(eng, w, layer, u):
            wait_freed(eng, w, "p", f"{layer}_P{CHUNKS[layer] - 1}", u)
            return at_slot(w, "o", f"{layer}_P0", u)[0]

        def wait_use(eng, w, semaphore, use, per_group, step=1):
            eng.wait_ge(semaphore, w.at(per_group * step, use * step))

        block = ctx.enter_context(nc.Block())

        @block.sync
        def _(sp):
            def load(group, signal):
                for dst, name in group:
                    if t[name].shape[0] > 128:
                        sp.dma_start(dst[:, :, :], t[name].rearrange("(k p) n -> p k n", p=128)).then_inc(signal, 16)
                    elif len(dst.shape) == 3:
                        dims = "p a b -> p (a b)"
                        sp.dma_start(dst[:, :, :].rearrange(dims), t[name].rearrange(dims)).then_inc(signal, 16)
                    else:
                        sp.dma_start(dst[:, :], t[name]).then_inc(signal, 16)

            def load_spread(group, signal):
                for dst, name in group:
                    sp.dma_start(dst[:, :], on_all(name, D)).then_inc(signal, 16)

            def load_scales():
                sp.dma_start(bc_gs[:, 0:INTER], on_all("gate_s", INTER)).then_inc(scales_loaded, 16)
                sp.dma_start(bc_us[:, 0:INTER], on_all("up_s", INTER)).then_inc(scales_loaded, 16)
                sp.dma_start(bc_ds, on_all("down_s", D)).then_inc(scales_loaded, 16)

            load(first, first_loaded)
            load_spread(first_spread, first_loaded)

            def store_parts(w, u, layer):
                wait_use(sp, w, parts_ready[u], SPLIT_USE[layer], 4)
                dst = flat(scratch[u].tensor, 0, (256, 128), (PART, 6), (1, 256))
                sp.dma_start(dst, pt[u][:, :, :, :].rearrange("p s c n -> p (s c) n")).then_inc(parts_stored[u], 16)

            def store_groups(w, u):
                wait_use(sp, w, parts_ready[u], SPLIT_USE["x0"], 4)
                for side in range(2):
                    for c in range(3):
                        dst = flat(scratch[u].tensor, (3 * side + c) * PART, (256, 8), (2048, 16), (1, 256))
                        sp.dma_start(dst, pt[u][:, side, c, :]).then_inc(parts_stored[u], 16)

            def load_stacks(w, u, layer):
                sp.wait_ge(parts_stored[u], w.at(16 * STORES, 16 * STORES_UP_TO[layer]))
                dram = scratch[u].tensor
                if layer == "l0":
                    for c in range(3):
                        sp.dma_start(sq[u][24 * c:24 * c + 24, :], flat(dram, c * PART, (0, 3), (4096, 8), (1, 4096)))\
                          .then_inc(stack_loaded[u], 16)
                    sp.dma_start(sk[u][0:72, :], flat(dram, 3 * PART, (0, 3), (4096, 24), (1, 4096))).then_inc(stack_loaded[u], 16)
                    sp.dma_start(sk[u][72:74, :], sk[u][96:98, :]).then_inc(stack_loaded[u], 16)
                    return
                for first, n, c in ((0, 3, 0), (48, 2, 1), (80, 1, 2)):
                    sp.dma_start(sq[u][first:first + 16 * n, 0:2048], flat(dram, c * PART, (0, n), (2048, 16), (1, 2048)))\
                      .then_inc(stack_loaded[u], 16)
                    sp.dma_start(sk[u][first:first + 16 * n, 0:2048], flat(dram, 3 * PART, (2048, 16 * n), (1, 2048)))\
                      .then_inc(stack_loaded[u], 16)

            def load_max(w, u, layer, rows, first):
                wait_freed(sp, w, "pr", f"{layer}_mx", u)
                sp.dma_start(sq[u][first:first + 2, 0:rows * 128], mx[u][0:2 * rows, :]).then_inc(max_loaded[u], 16)

            def step(stage, u, w):
                if stage == "load":
                    sp.wait_ge(out_stored[u], w.at(16, 16))
                    sp.dma_start(loaded[u][:, :], t["xc"][w.batch(u)]).then_inc(in_loaded[u], 16)
                    sp.dma_start(mk8[u][:, :], t["mask_col"][w.batch(u)]).then_inc(in_loaded[u], 16)
                    sp.dma_start(mr8[u][:, :], t["mask_row"][w.batch(u)].broadcast_to([128, 128])).then_inc(in_loaded[u], 16)
                    if enters(w, stage, u, "load"):
                        load(early, early_loaded)
                        load_spread(early_spread, early_loaded)
                elif stage in ("l0_c", "l1_c", "c_c"):
                    store_parts(w, u, stage[:-2])
                elif stage == "x0_c":
                    store_groups(w, u)
                elif stage in ("l0_ld", "x0_ld", "l1_ld", "c_ld"):
                    if stage == "l0_ld":
                        sp.wait_ge(keys_ones, U)
                    load_stacks(w, u, stage[:-3])
                    if enters(w, stage, u, "l0_ld"):
                        load(ffn_weights, w_loaded)
                        load_scales()
                    if enters(w, stage, u, "l1_ld"):
                        sp.wait_ge(w_scaled, N_SCALED)
                elif stage == "l0_mx":
                    load_max(w, u, "l0", H0, K0)
                    if enters(w, stage, u, "l0_mx"):
                        load(weights, w_loaded)
                        load(plain, w_loaded)
                        load_spread(spread, w_loaded)
                elif stage in ("x0_mx", "c_mx"):
                    load_max(w, u, stage[:-3], 16, K1)
                elif stage == "m_ln":
                    wait_use(sp, w, o_ready[u], 1, 1)
                    sp.dma_start(out[w.batch(u)], qf[u][:, 0:D]).then_inc(out_stored[u], 16)

            run(sp, step)
            for u in range(U):
                sp.wait_ge(out_stored[u], 16 * (NIT + 1))

        @block.gpsimd
        def _(pool):
            for u in reversed(range(U)):
                nc.gpsimd.memset(v0[u][:, :, :], 0.0).then_inc(pads_zero, 1)
                nc.gpsimd.memset(vb[u][:, :, :], 0.0).then_inc(pads_zero, 1)
            nc.gpsimd.memset(minus_half[:, :], -0.5).then_inc(ones_set, 1)
            pool.wait_ge(early_loaded, N_EARLY)
            pool.wait_ge(ones_set, 1)

            def rstd(w, u, layer):
                wait_use(pool, w, var_ready[u], NORM_USE[layer], 7)
                nc.gpsimd.tensor_tensor(st[u][:, 11:12], st[u][:, 10:11], minus_half[:, :], ALU.pow).then_inc(rstd_ready[u], 1)

            def step(stage, u, w):
                if stage == "l0_qk":
                    wait_use(pool, w, in_loaded[u], 3, 3, 16)
                    nc.gpsimd.tensor_tensor(yb[u][:, :], xc[u][:, 0:D], bc_p0[:, :], ALU.add).then_inc(xb_ready[u], 1)
                elif stage == "l1_xT":
                    if enters(w, stage, u, "l1_xT"):
                        pool.wait_ge(w_loaded, N_LATE)
                    wait_use(pool, w, x_ready[u], X_USE["f"], 5)
                    nc.gpsimd.tensor_tensor(yb[u][:, :], xc[u][:, 0:D], bc_o1[:, :], ALU.add).then_inc(xb_ready[u], 1)
                elif stage in ("l0_o", "f_o", "l1_o", "c_o", "m_o"):
                    rstd(w, u, stage[:-2])
                elif stage == "x0_n":
                    rstd(w, u, "x0")
                elif stage == "c_rms":
                    rstd(w, u, "c_rms")

            run(pool, step)

        @block.scalar
        def _(act):
            act.wait_ge(pads_zero, 2)

            def second_part(w, u, layer):
                wait_use(act, w, r_ready[u], SPLIT_USE[layer], 4)
                nc.scalar.activation(part(u, 1), sides(qf[u][:, :]), ACT.Copy).then_inc(pb_ready[u], 1)

            def max_rows(w, u, layer, rows):
                slot = wait_full(act, w, "pr", f"{layer}_mx", u)
                nc.scalar.activation(mx[u][0:2 * rows, :], pr[0:2 * rows, slot, 0:128], ACT.Copy).then_inc(ring_free["pr"][slot], 1)

            def exps(w, u, stage, scale, bias):
                s = wait_full(act, w, "sc", stage, u)
                p = wait_free(act, w, "p", stage, u)
                nc.scalar.activation(pb[:, p, :], sc[:, s, :], ACT.Exp, bias=bias, scale=scale).then_inc(ring_full["p"][p], 1)

            def step(stage, u, w):
                if enters(w, stage, u, "l0_P0"):
                    act.wait_ge(early_loaded, N_EARLY)
                    act.wait_ge(pads_zero, 2 * U)
                if stage == "ctx_v":
                    wait_use(act, w, in_loaded[u], 3, 3, 16)
                    src = ct[u].rearrange("p k (b2 h c) -> p (k b2) h c", b2=4, h=2)
                    nc.scalar.activation(pads(vb[u], 8, 2, 16), src, ACT.Copy).then_inc(ct_ready[u], 1)
                elif stage in ("f_xT", "l1_xT", "c_xT", "m_xT"):
                    slot = wait_full(act, w, "pr", stage, u)
                    src = pr[:, slot, 0:D].rearrange("p (k n) -> p k n", k=KT)
                    nc.scalar.activation(xt[u][:, :, :], src, ACT.Copy).then_inc(ring_free["pr"][slot], 1)
                elif stage in ("l0_qk", "l1_qk"):
                    slot = wait_freed(act, w, "pr", stage, u, 0)
                    nc.scalar.activation(part(u, 0), sides(qf[u][:, :]), ACT.Copy).then_inc(pa_ready[u], 1)
                elif stage == "x0_a":
                    wait_use(act, w, x_ready[u], X_USE["l0"], 5)
                    nc.scalar.activation(part(u, 0), sides(xc[u][:, :]), ACT.Copy).then_inc(pa_ready[u], 1)
                elif stage == "c_qk":
                    slot = wait_full(act, w, "pr", stage, u, 0)
                    nc.scalar.activation(part(u, 0), sides(pr[:, slot, :]), ACT.Copy).then_inc(pa_ready[u], 1)
                    slot = wait_full(act, w, "pr", stage, u, 1)
                    src = pr[:, slot, 0:D].rearrange("p (b h c) -> p b h c", b=8, h=2)
                    nc.scalar.activation(pads(vb[u], 8, 2, 16), src, ACT.Copy)
                    nc.scalar.activation(yb[u][:, :], pr[:, slot, D:2 * D], ACT.Tanh, scale=0.5).then_inc(ring_free["pr"][slot], 1)
                elif stage in ("l0_r", "x0_r", "l1_r", "c_r"):
                    second_part(w, u, stage[:-2])
                elif stage == "l0_mx":
                    max_rows(w, u, "l0", H0)
                elif stage in ("x0_mx", "c_mx"):
                    max_rows(w, u, stage[:-3], 16)
                elif stage[:-1] == "l0_P":
                    exps(w, u, stage, SCALE0, key_bias[:, 0:1])
                elif stage[:-1] == "x0_P":
                    exps(w, u, stage, SCALEX, 0.0)
                elif stage[:-1] == "c_P":
                    if stage == "c_P0":
                        wait_use(act, w, mask_ready[u], 2, 2)
                    exps(w, u, stage, SCALEX, mk[u][:, 0:1])
                elif stage in ("f_gu0", "f_gu1"):
                    c = int(stage[-1])
                    n = 512 if c == 0 else 256
                    s = wait_full(act, w, "sc", stage, u)
                    nc.scalar.activation(ffn_space(u)[c], sc[:, s, 0:n], ACT.Tanh, scale=0.5).then_inc(tanh_ready[u], 1)
                elif stage == "l1_n":
                    slot = wait_attended(act, w, "l1", u)
                    src = ob[:, slot, 0:D].rearrange("p (k n) -> p k n", k=KT)
                    nc.scalar.activation(xt[u][:, :, :], src, ACT.Copy).then_inc(ring_free["o"][slot], 1)
                elif stage == "m_a":
                    wait_use(act, w, gap_ready[u], 1, 1)
                    nc.scalar.activation(st[u][:, 20:21], st[u][:, 19:20], ACT.Exp).then_inc(egap_ready[u], 1)
                elif stage == "m_b":
                    slot = wait_full(act, w, "pr", stage, u)
                    nc.scalar.activation(yb[u][:, 128:256], pr[:, slot, 0:128], ACT.Copy).then_inc(ring_free["pr"][slot], 1)

            run(act, step)

        @block.vector
        def _(dve):
            for r, n in SLOTS.items():
                for i in range(n):
                    dve.sem_inc(ring_free[r][i], 1)
            for u in range(U):
                dve.sem_inc(out_stored[u], 16)
            pair_of_ones = float(np.array([0x3F803F80], np.uint32).view(np.float32)[0])
            for u in reversed(range(U)):
                nc.vector.memset(sk[u][96:98, :].bitcast(f32), pair_of_ones).then_inc(keys_ones, 1)
            dve.wait_ge(first_loaded, N_FIRST)
            dve.wait_ge(pads_zero, 2)

            def narrow_masks():
                dve.wait_ge(early_loaded, N_EARLY)
                dve.wait_ge(pads_zero, 2 * U)
                for narrow, wide_mask in ((causal_kq, wide_masks[0]), (alibi_qk, wide_masks[1]), (identb, ident)):
                    nc.vector.tensor_copy(narrow[:, :], wide_mask[:, :]).then_inc(narrowed, 1)

            def scale_weights():
                dve.wait_ge(w_loaded, N_LATE)
                dve.wait_ge(scales_loaded, 48)
                nc.vector.memset(bc_gs[:, INTER:FT * 128], 0.0).then_inc(w_scaled, 1)
                nc.vector.memset(bc_us[:, INTER:FT * 128], 0.0).then_inc(w_scaled, 1)
                dve.wait_ge(w_scaled, 2)
                for k in range(KT):
                    for first, tiles, scales, tile in ((0, 4, bc_gs, 0), (512, 4, bc_us, 0), (1024, 2, bc_gs, 4), (1280, 2, bc_us, 4)):
                        cols = w_gu[:, k, first:first + 128 * tiles]
                        nc.vector.tensor_tensor(cols, cols, scales[:, 128 * tile:128 * (tile + tiles)], ALU.mult).then_inc(w_scaled, 1)
                for j in range(FT):
                    nc.vector.scalar_tensor_tensor(w_dn[:, j, :], w_dn[:, j, :], 0.5, bc_ds, ALU.mult, ALU.mult).then_inc(w_scaled, 1)
                nc.vector.tensor_scalar(w_oc[:, :, :], w_oc[:, :, :], 0.5, None, ALU.mult).then_inc(w_scaled, 1)
                for k in range(KT):
                    for cols in (w_qkc[:, k, 0:D], w_vgc[:, k, D:2 * D]):
                        nc.vector.tensor_scalar(cols, cols, norm_w[:, k:k + 1], None, ALU.mult).then_inc(w_scaled, 1)

            steps, here = [0], [None]

            def link(ins):
                ins.then_inc(vec_step, 1)
                steps[0] += 1
                w = here[0]
                dve.wait_ge(vec_step, w.loop * VEC_STEPS + steps[0] + (w.section == "last") * (NIT - 2) * VEC_STEPS)

            def link_alone(ins):
                link(ins)
                dve.sem_inc(vec_held, 1)

            def residual(w, u, layer, use):
                wait_use(dve, w, pa_ready[u], use, 4)
                nc.vector.tensor_tensor(sides(qf[u][:, :]), sides(qf[u][:, :]), part(u, 0), ALU.subtract).then_inc(r_ready[u], 1)

            def third_part(w, u, layer):
                wait_use(dve, w, pb_ready[u], SPLIT_USE[layer], 4)
                nc.vector.tensor_tensor(part(u, 2), sides(qf[u][:, :]), part(u, 1), ALU.subtract).then_inc(parts_ready[u], 1)

            def statistics(u, src, eps):
                link_alone(nc.vector.bn_stats(st[u][:, 0:6], src))
                link(nc.vector.bn_aggr(st[u][:, 8:10], st[u][:, 0:6]))
                nc.vector.tensor_scalar(st[u][:, 10:11], st[u][:, 9:10], eps, None, ALU.add).then_inc(var_ready[u], 1)

            def layer_norm(w, u, layer, dst, ready):
                wait_use(dve, w, rstd_ready[u], NORM_USE[layer], 7)
                nc.vector.tensor_scalar(dst, yb[u][:, :], st[u][:, 8:9], st[u][:, 11:12], ALU.subtract, ALU.mult)\
                  .then_inc(ready, 1)

            def maxima(w, u, stage):
                layer, c = stage[:-3], int(stage[-1])
                s = wait_full(dve, w, "sc", stage, u)
                if layer == "l0":
                    half, i0 = c // 2, 2 * (c % 2)
                    dst = nm[u][:, :].rearrange("p (t g i) -> p t i g", t=2, g=4)[:, half, i0:i0 + 2, :]
                    src = sc[:, s, :].rearrange("p (i g n) -> p i g n", i=2, g=4)
                elif layer == "x0":
                    dst = nm[u][:, 4 * c:4 * c + 4]
                    src = sc[:, s, :].rearrange("p (a n) -> p a n", a=4)
                else:
                    dst = nm[u][:, 8 * c:8 * c + 8]
                    src = sc[:, s, :].rearrange("p (a n) -> p a n", a=8)
                nc.vector.tensor_reduce(dst, src, AX.X, ALU.max, negate=True).then_inc(ring_free["sc"][s], 1)

            def max_parts(w, u, layer, rows):
                for c in range(CHUNKS[layer] - 2, CHUNKS[layer]):
                    wait_freed(dve, w, "sc", f"{layer}_S{c}", u)
                link(nc.vector.tensor_copy(nh[u][:, 0:rows], nm[u][:, 0:rows]))
                nc.vector.tensor_tensor(nh[u][:, rows:2 * rows], nm[u][:, 0:rows], nh[u][:, 0:rows], ALU.subtract).then_inc(mh_ready[u], 1)

            def add_residual(w, u, stage, x):
                slot = wait_full(dve, w, "pr", stage, u)
                ins = nc.vector.tensor_tensor(yb[u][:, :], pr[:, slot, 0:D], x, ALU.add)
                ins.then_inc(ring_free["pr"][slot], 1)
                slot = wait_freed(dve, w, "pr", stage, u)

            def step(stage, u, w):
                here[0] = w
                if enters(w, stage, u, "l0_ld"):
                    narrow_masks()
                if enters(w, stage, u, "x0_ld"):
                    scale_weights()
                x = xc[u][:, 0:D]
                if stage == "ctx_v":
                    wait_use(dve, w, in_loaded[u], 3, 3, 16)
                    nc.vector.tensor_scalar(mr[u][:, :], mr8[u][:, :], -1.0, -NEG, ALU.add, ALU.mult).then_inc(mask_ready[u], 1)
                    nc.vector.tensor_scalar(mk[u][:, :], mk8[u][:, :], -1.0, -NEG, ALU.add, ALU.mult).then_inc(mask_ready[u], 1)
                elif stage in ("l0_qk", "l1_qk"):
                    layer = stage[:-3]
                    b_qk, bc_v = (b_qk0, bc_v0) if layer == "l0" else (b_qk1, bc_v1)
                    slot = wait_full(dve, w, "pr", stage, u, 0)
                    src = pr[:, slot, :].rearrange("p (a n) -> p a n", a=4)
                    bias = b_qk[:, :].unsqueeze(2).broadcast_to([128, 4, 128])
                    nc.vector.tensor_tensor(qf[u][:, :].rearrange("p (a n) -> p a n", a=4), src, bias, ALU.add)\
                      .then_inc(ring_free["pr"][slot], 1)
                    slot = wait_full(dve, w, "pr", stage, u, 1)
                    if layer == "l0":
                        dst, dims, kw = pads(v0[u], 8, 4, 8), "p (b h c) -> p b h c", dict(b=8, h=4)
                    else:
                        dst, dims, kw = pads(vb[u], 8, 2, 16), "p (b h c) -> p b h c", dict(b=8, h=2)
                    nc.vector.tensor_tensor(dst, pr[:, slot, 0:D].rearrange(dims, **kw), bc_v[:, :].rearrange(dims, **kw), ALU.add)\
                      .then_inc(ring_free["pr"][slot], 1)
                elif stage in ("l0_r", "l1_r"):
                    residual(w, u, stage[:-2], SPLIT_USE[stage[:-2]])
                elif stage == "x0_r":
                    wait_use(dve, w, pa_ready[u], SPLIT_USE["x0"], 4)
                    nc.vector.tensor_tensor(sides(qf[u][:, :]), sides(xc[u][:, :]), part(u, 0), ALU.subtract).then_inc(r_ready[u], 1)
                elif stage == "c_r":
                    wait_use(dve, w, pa_ready[u], SPLIT_USE["c"], 4)
                    slot, _ = at_slot(w, "pr", "c_qk", u, 0)
                    link(nc.vector.tensor_tensor(sides(qf[u][:, :]), sides(pr[:, slot, :]), part(u, 0), ALU.subtract))
                    dve.sem_inc(ring_free["pr"][slot], 1)
                    dve.sem_inc(r_ready[u], 1)
                elif stage in ("l0_c", "x0_c", "l1_c", "c_c"):
                    third_part(w, u, stage[:-2])
                elif stage[:-1] in ("l0_S", "x0_S", "c_S"):
                    maxima(w, u, stage)
                elif stage in ("l0_mx", "x0_mx", "c_mx"):
                    max_parts(w, u, stage[:-3], H0 if stage == "l0_mx" else 16)
                elif stage == "l0_n":
                    slot = wait_attended(dve, w, "l0", u)
                    link(nc.vector.reciprocal(qf[u][:, 0:D], ob[:, slot, D:2 * D]))
                    nc.vector.tensor_tensor(xt[u][:, :, :].rearrange("p k n -> p (k n)"), ob[:, slot, 0:D], qf[u][:, 0:D], ALU.mult)\
                      .then_inc(ring_free["o"][slot], 1)
                elif stage == "x0_n":
                    slot = wait_attended(dve, w, "x0", u)
                    link(nc.vector.reciprocal(qf[u][:, 0:D], ob[:, slot, D:2 * D]))
                    link(nc.vector.tensor_tensor(yb[u][:, :], ob[:, slot, 0:D], qf[u][:, 0:D], ALU.mult))
                    dve.sem_inc(ring_free["o"][slot], 1)
                    link(nc.vector.tensor_tensor(yb[u][:, :], yb[u][:, :], x, ALU.add))
                    statistics(u, yb[u][:, :], LN_EPS)
                elif stage == "c_n":
                    slot = wait_attended(dve, w, "c", u)
                    link(nc.vector.tensor_scalar(qf[u][:, D:2 * D], ob[:, slot, D:2 * D], 1e-30, None, ALU.max))
                    link(nc.vector.reciprocal(qf[u][:, 0:D], qf[u][:, D:2 * D]))
                    nc.vector.tensor_tensor(xt[u][:, :, :].rearrange("p k n -> p (k n)"), ob[:, slot, 0:D], qf[u][:, 0:D], ALU.mult)\
                      .then_inc(ring_free["o"][slot], 1)
                elif stage in ("l0_o", "l1_o"):
                    wait_use(dve, w, xb_ready[u], 1 if stage == "l0_o" else 2, 2)
                    add_residual(w, u, stage, yb[u][:, :])
                    statistics(u, yb[u][:, :], LN_EPS)
                elif stage == "f_o":
                    add_residual(w, u, stage, x)
                    statistics(u, yb[u][:, :], LN_EPS)
                elif stage == "c_o":
                    slot = wait_full(dve, w, "pr", stage, u)
                    link(nc.vector.scalar_tensor_tensor(yb[u][:, :], yb[u][:, :], 1.0, pr[:, slot, 0:D], ALU.add, ALU.mult))
                    dve.sem_inc(ring_free["pr"][slot], 1)
                    link(nc.vector.tensor_tensor(yb[u][:, :], yb[u][:, :], x, ALU.add))
                    statistics(u, yb[u][:, :], LN_EPS)
                elif stage in ("l0_ln", "x0_ln", "f_ln", "l1_ln", "c_ln"):
                    layer_norm(w, u, stage[:-3], x, x_ready[u])
                elif stage == "c_rms":
                    wait_use(dve, w, x_ready[u], X_USE["l1"], 5)
                    link_alone(nc.vector.bn_stats(st[u][:, 0:6], x))
                    link(nc.vector.bn_aggr(st[u][:, 8:10], st[u][:, 0:6]))
                    link(nc.vector.scalar_tensor_tensor(st[u][:, 12:13], st[u][:, 8:9], st[u][:, 8:9], st[u][:, 9:10], ALU.mult, ALU.add))
                    nc.vector.tensor_scalar(st[u][:, 10:11], st[u][:, 12:13], RMS_EPS, None, ALU.add).then_inc(var_ready[u], 1)
                elif stage == "c_xT":
                    wait_use(dve, w, rstd_ready[u], NORM_USE["c_rms"], 7)
                    nc.vector.tensor_scalar(yb[u][:, :], x, st[u][:, 11:12], None, ALU.mult)\
                      .then_inc(xn_ready[u], 1)
                elif stage in ("f_gu0", "f_gu1"):
                    ht = sq[u][:, :].bitcast(f32)
                    c = int(stage[-1])
                    n, first = (512, 0) if c == 0 else (256, 512)
                    s, _ = at_slot(w, "sc", stage, u)
                    space = ffn_space(u)[c]
                    wait_use(dve, w, tanh_ready[u], c + 1, 2)
                    link(nc.vector.scalar_tensor_tensor(space, space, 1.0, sc[:, s, 0:n], ALU.add, ALU.mult))
                    nc.vector.tensor_tensor(ht[:, first:first + n], space, sc[:, s, n:2 * n], ALU.mult)\
                      .then_inc(ring_free["sc"][s], 1)
                elif stage[:-1] == "l1_P":
                    c = int(stage[-1])
                    s = wait_full(dve, w, "sc", stage, u)
                    p = wait_free(dve, w, "p", stage, u)
                    nc.vector.tensor_tensor(pb[:, p, :], sc[:, s, :], decay[:, 8 * c:8 * c + 8, :].rearrange("p h n -> p (h n)"), ALU.mult)\
                      .then_inc(ring_full["p"][p], 1)
                elif stage == "m_a":
                    s, _ = at_slot(w, "o", stage, u)
                    wait_use(dve, w, logits_ready[u], 1, 1)
                    dve.sem_inc(vec_held, 1)
                    logits = ob[:, s, MW - E:MW]
                    link_alone(nc.vector.max(st[u][:, 24:32], logits))
                    link(nc.vector.max_index(ix[u][:, :], st[u][:, 24:32], logits))
                    link(nc.vector.tensor_copy(st[u][:, 32:34], ix[u][:, 0:2]))
                    nc.vector.tensor_tensor(st[u][:, 19:20], st[u][:, 25:26], st[u][:, 24:25], ALU.subtract).then_inc(gap_ready[u], 1)
                elif stage == "m_b":
                    s, _ = at_slot(w, "o", "m_a", u)
                    wait_use(dve, w, egap_ready[u], 1, 1)
                    link(nc.vector.tensor_scalar(st[u][:, 21:22], st[u][:, 20:21], 1.0, 0.5, ALU.add, ALU.mult))
                    link(nc.vector.reciprocal(st[u][:, 22:23], st[u][:, 21:22]))
                    link(nc.vector.tensor_tensor(st[u][:, 23:24], st[u][:, 22:23], st[u][:, 20:21], ALU.mult))
                    link(nc.vector.tensor_scalar(st[u][:, 0:8], iota8[:, :], st[u][:, 32:33], st[u][:, 22:23], ALU.is_equal, ALU.mult))
                    link(nc.vector.tensor_scalar(st[u][:, 24:32], iota8[:, :], st[u][:, 33:34], st[u][:, 23:24], ALU.is_equal, ALU.mult))
                    link(nc.vector.tensor_tensor(st[u][:, 0:8], st[u][:, 0:8], st[u][:, 24:32], ALU.add))
                    nc.vector.tensor_tensor(yb[u][:, 0:128].rearrange("p (e r) -> p e r", e=E),
                                            ob[:, s, D:D + E * R].rearrange("p (e r) -> p e r", e=E),
                                            st[u][:, 0:8].unsqueeze(2).broadcast_to([128, E, R]), ALU.mult).then_inc(axw_ready[u], 1)
                elif stage == "m_o":
                    s, _ = at_slot(w, "o", "m_a", u)
                    wait_use(dve, w, expert_ready[u], 1, 1)
                    link(nc.vector.tensor_tensor(yb[u][:, :], ob[:, s, 0:D], x, ALU.add))
                    dve.sem_inc(ring_free["o"][s], 1)
                    statistics(u, yb[u][:, :], LN_EPS)
                elif stage == "m_ln":
                    layer_norm(w, u, "m", qf[u][:, 0:D], o_ready[u])

            run(dve, step)
            assert steps[0] == 2 * VEC_STEPS, steps[0]

        @block.tensor
        def _(pe):
            pe.wait_ge(first_loaded, N_FIRST)

            def transpose2(w, u, stage, src):
                slot = wait_free(pe, w, "pr", stage, u)
                for k in range(KT):
                    ins = nc.tensor.transpose(pr[:, slot, 128 * k:128 * k + 128], src[:, 128 * k:128 * k + 128], ident[:, :])
                ins.then_inc(ring_full["pr"][slot], 1)

            def project(w, u, stage, k, work):
                slot = wait_free(pe, w, "pr", stage, u, k)
                for cols, left, right, tiles in work:
                    for i in range(tiles):
                        ins = nc.tensor.matmul(pr[:, slot, cols], left(i), right(i), start=(i == 0), stop=(i == tiles - 1))
                ins.then_inc(ring_full["pr"][slot], 1)

            def qk_work(u, w):
                return [(slice(128 * a, 128 * a + 128), lambda i, a=a: w[:, i, 128 * a:128 * a + 128], lambda i: xt[u][:, i, :], KT)
                        for a in range(4)]

            def out_work(u, w, src, tiles=KT):
                return [(slice(0, D), lambda i: src[:, i, :], lambda i: w[:, i, :], tiles)]

            def head0(n):
                half, i, g = n // 16, n // 4 % 4, n % 4
                return (4 * half + g) * 4 + i

            def head1(n):
                half, i, g = n // 8, n // 4 % 2, n % 4
                return (4 * half + g) * 2 + i

            unread = {}

            def scores_read(slot):
                if slot in unread:
                    stage, u, w = unread.pop(slot)
                    wait_full(pe, w, "p", stage, u)
                    pe.sem_inc(ring_free["sc"][slot], 1)

            def scores_slot(w, stage, u):
                slot, _ = at_slot(w, "sc", stage, u)
                scores_read(slot)
                wait_free(pe, w, "sc", stage, u)
                if "_P" in stage:
                    unread[slot] = stage, u, w
                return slot

            def scores0(w, u, stage, k, left, right, mask):
                c, s = int(stage[-1]), scores_slot(w, stage, u)
                for j in range(2):
                    nc.tensor.matmul(sc[:, s, 512 * j:512 * j + 512], identb[:, :], mask[:, :].unsqueeze(1).broadcast_to([128, 4, 128]),
                                     start=True, stop=False, skip_group_check=True)
                for n in range(8):
                    h = head0(8 * c + n)
                    cols = slice(128 * h, 128 * h + 128)
                    ins = nc.tensor.matmul(sc[:, s, 128 * n:128 * n + 128], left[0:k, cols], right[0:k, cols],
                                           start=False, stop=(n % 4 == 3), skip_group_check=True)
                ins.then_inc(ring_full["sc"][s], 1)

            def scores_x(w, u, stage, k, left, right):
                c, s = int(stage[-1]), scores_slot(w, stage, u)
                for n in range(2):
                    h = 2 * c + n if stage[3] == "S" else headx(2 * c + n)
                    for half in range(2):
                        a = 256 * h + 128 * half
                        ins = nc.tensor.matmul(sc[:, s, 512 * n + 256 * half:512 * n + 256 * half + 256], left[0:k, a:a + 128],
                                               right[0:k, 256 * h:256 * h + 256], start=True, stop=True)
                ins.then_inc(ring_full["sc"][s], 1)

            def headx(n):
                return 2 * (n % 4) + n // 4

            def scores1(w, u, stage, k, left, right, row=None):
                c, s = int(stage[-1]), scores_slot(w, stage, u)
                if row is not None:
                    for j in range(2):
                        nc.tensor.matmul(sc[:, s, 512 * j:512 * j + 512], identb[:, :], row[:, :].unsqueeze(1).broadcast_to([128, 4, 128]),
                                         start=True, stop=False, skip_group_check=True)
                for n in range(8):
                    h = 8 * c + n if row is not None else head1(8 * c + n)
                    cols = slice(128 * h, 128 * h + 128)
                    ins = nc.tensor.matmul(sc[:, s, 128 * n:128 * n + 128], left[0:k, cols], right[0:k, cols],
                                           start=(row is None), stop=True, skip_group_check=True)
                ins.then_inc(ring_full["sc"][s], 1)

            def values(w, u, stage, todo):
                layer, c = stage[:-3], stage[-1]
                if c == "0":
                    wait_free(pe, w, "o", f"{layer}_P0", u)
                    if layer == "x0":
                        wait_use(pe, w, ct_ready[u], 1, 1)
                slot, _ = at_slot(w, "o", f"{layer}_P0", u)
                p = wait_full(pe, w, "p", f"{layer}_P{c}", u)
                slot_of_scores, _ = at_slot(w, "sc", f"{layer}_P{c}", u)
                if unread.get(slot_of_scores, (None, None))[:2] == (f"{layer}_P{c}", u):
                    scores_read(slot_of_scores)
                for kind in range(2):
                    for g, src, cols, first, v, ones in todo:
                        left = v if kind == 0 else ones
                        if left is None:
                            continue
                        dst = cols if kind == 0 else slice(cols.start + D, cols.stop + D)
                        ins = nc.tensor.matmul(ob[32 * g:32 * g + 32, slot, dst], left, pb[:, p, src],
                                               start=(first and kind == 0), stop=True, skip_group_check=True)
                ins.then_inc(ring_free["p"][p], 1)

            def values_of(u, layer, c):
                todo = []
                if layer == "l0":
                    for n in range(8):
                        h, m = head0(8 * c + n), 8 * c + n
                        half, i, g = m // 16, m // 4 % 4, m % 4
                        todo.append((g, slice(128 * n, 128 * n + 128), slice(128 * half, 128 * half + 128), half == 0 and i == 0,
                                     v0[u][:, h, :], ones8[:, i, :]))
                elif layer == "x0":
                    for n in range(2):
                        h = headx(2 * c + n)
                        for half in range(2):
                            todo.append((h // 2, slice(512 * n + 256 * half, 512 * n + 256 * half + 256), slice(0, D), h % 2 == 0 and half == 0,
                                         vb[u][:, 8 * half + h, :], ones16[:, h % 2, :]))
                else:
                    for n in range(8):
                        h, m = head1(8 * c + n), 8 * c + n
                        half, i, g = m // 8, m // 4 % 2, m % 4
                        todo.append((g, slice(128 * n, 128 * n + 128), slice(128 * half, 128 * half + 128), half == 0 and i == 0,
                                     vb[u][:, h, :], ones16[:, i, :] if layer == "c" else None))
                return todo

            def xt_in(w, u, stage):
                wait_freed(pe, w, "pr", stage.split("_")[0] + "_xT", u)

            def stack_in(w, u, layer):
                pe.wait_ge(stack_loaded[u], w.at(16 * 23, 16 * LOADS_UP_TO[layer]))

            def step(stage, u, w):
                if enters(w, stage, u, "l0_S0"):
                    pe.wait_ge(early_loaded, N_EARLY)
                    pe.wait_ge(narrowed, 3)
                if enters(w, stage, u, "x0_P0"):
                    pe.wait_ge(keys_ones, U)
                if enters(w, stage, u, "f_xT"):
                    pe.wait_ge(w_loaded, N_LATE)
                    pe.wait_ge(w_scaled, N_SCALED)
                x = xc[u][:, 0:D]
                if stage in ("f_xT", "l1_xT", "m_xT"):
                    before = {"f": "x0", "l1": "f", "m": "c"}[stage[:-3]]
                    wait_use(pe, w, x_ready[u], X_USE[before], 5)
                    transpose2(w, u, stage, x)
                elif stage == "c_xT":
                    wait_use(pe, w, xn_ready[u], 1, 1)
                    transpose2(w, u, stage, yb[u][:, :])
                elif stage in ("l0_qk", "l1_qk"):
                    w_qk, w_v = (w_qk0, w_v0) if stage == "l0_qk" else (w_qk1, w_v1)
                    if stage == "l0_qk":
                        wait_use(pe, w, in_loaded[u], 3, 3, 16)
                    else:
                        xt_in(w, u, stage)
                    project(w, u, stage, 0, qk_work(u, w_qk))
                    project(w, u, stage, 1, out_work(u, w_v, xt[u]))
                elif stage == "c_qk":
                    xt_in(w, u, stage)
                    q_and_k = qk_work(u, w_qkc)
                    q_and_k = q_and_k[:2] + [(cols, left, lambda i: ct[u][:, i, :], KT) for cols, left, _, _ in q_and_k[2:]]
                    project(w, u, stage, 0, q_and_k)
                    project(w, u, stage, 1, [(slice(0, D), lambda i: ct[u][:, i, :], lambda i: w_vgc[:, i, 0:D], KT),
                                              (slice(D, 2 * D), lambda i: xt[u][:, i, :], lambda i: w_vgc[:, i, D:2 * D], KT)])
                elif stage[:-1] == "l0_S":
                    stack_in(w, u, "l0")
                    scores0(w, u, stage, K0, sq[u], sk[u], alibi_qk)
                elif stage[:-1] == "x0_S":
                    stack_in(w, u, "x0")
                    scores_x(w, u, stage, K1, sq[u], sk[u])
                elif stage[:-1] == "c_S":
                    stack_in(w, u, "c")
                    wait_use(pe, w, mask_ready[u], 2, 2)
                    scores1(w, u, stage, K1, sq[u], sk[u], mr[u])
                elif stage in ("l0_mx", "x0_mx", "c_mx"):
                    layer, rows = stage[:-3], H0 if stage == "l0_mx" else 16
                    wait_use(pe, w, mh_ready[u], MAX_USE[layer], 3)
                    slot = wait_free(pe, w, "pr", stage, u)
                    nc.tensor.matmul(pr[0:2 * rows, slot, 0:128], nh[u][:, 0:2 * rows], identb[:, :], start=True, stop=True)\
                      .then_inc(ring_full["pr"][slot], 1)
                elif stage[:-1] == "l0_P":
                    wait_use(pe, w, max_loaded[u], 1, 3, 16)
                    scores0(w, u, stage, K0 + 2, sk[u], sq[u], causal_kq)
                elif stage[:-1] == "x0_P":
                    wait_use(pe, w, max_loaded[u], 2, 3, 16)
                    scores_x(w, u, stage, K1 + 2, sk[u], sq[u])
                elif stage[:-1] == "l1_P":
                    stack_in(w, u, "l1")
                    scores1(w, u, stage, K1, sk[u], sq[u])
                elif stage[:-1] == "c_P":
                    wait_use(pe, w, max_loaded[u], 3, 3, 16)
                    scores1(w, u, stage, K1 + 2, sk[u], sq[u])
                elif stage[:-1] in ("l0_V", "x0_V", "l1_V", "c_V"):
                    values(w, u, stage, values_of(u, stage[:-3], int(stage[-1])))
                elif stage in ("l0_o", "l1_o", "c_o"):
                    layer = stage[:-2]
                    wait_freed(pe, w, "o", f"{layer}_P0", u)
                    project(w, u, stage, 0, out_work(u, {"l0": w_p0, "l1": w_o1, "c": w_oc}[layer], xt[u]))
                elif stage in ("f_gu0", "f_gu1"):
                    xt_in(w, u, stage)
                    s = scores_slot(w, stage, u)
                    first, tiles = (0, 8) if stage == "f_gu0" else (1024, 4)
                    for a in range(tiles):
                        for i in range(KT):
                            ins = nc.tensor.matmul(sc[:, s, 128 * a:128 * a + 128], w_gu[:, i, first + 128 * a:first + 128 * a + 128],
                                                   xt[u][:, i, :], start=(i == 0), stop=(i == KT - 1))
                    ins.then_inc(ring_full["sc"][s], 1)
                elif stage == "f_o":
                    for c in range(2):
                        wait_freed(pe, w, "sc", f"f_gu{c}", u)
                    ht = sq[u][:, :].bitcast(f32)
                    slot = wait_free(pe, w, "pr", stage, u)
                    for j in range(FT):
                        ins = nc.tensor.matmul(pr[:, slot, 0:D], ht[:, 128 * j:128 * j + 128], w_dn[:, j, :], start=(j == 0), stop=(j == FT - 1))
                    ins.then_inc(ring_full["pr"][slot], 1)
                elif stage == "m_a":
                    xt_in(w, u, stage)
                    s = wait_free(pe, w, "o", stage, u)
                    for i in range(KT):
                        ins = nc.tensor.matmul(ob[:, s, 0:MW], xt[u][:, i, :], w_m[:, i, :], start=(i == 0), stop=(i == KT - 1), skip_group_check=True)
                    ins.then_inc(logits_ready[u], 1)
                elif stage == "m_b":
                    wait_use(pe, w, axw_ready[u], 1, 1)
                    slot = wait_free(pe, w, "pr", stage, u)
                    nc.tensor.transpose(pr[:, slot, 0:128], yb[u][:, 0:128], ident[:, :]).then_inc(ring_full["pr"][slot], 1)
                elif stage == "m_o":
                    slot = wait_freed(pe, w, "pr", "m_b", u)
                    s, _ = at_slot(w, "o", "m_a", u)
                    nc.tensor.matmul(ob[:, s, 0:D], yb[u][:, 128:256], w_b[:, :], start=False, stop=True, skip_group_check=True)\
                      .then_inc(expert_ready[u], 1)

            run(pe, step)


def layouts(a):
    def heads(hd):
        p = np.arange(128)
        groups = 128 // hd
        return np.concatenate([(2 * (p % groups) + tile) * hd + p // groups for tile in range(2)])

    def tiled(v):
        return np.ascontiguousarray(v.reshape(-1, 128).T)

    def transposed(v):
        return v.transpose(0, 2, 1).reshape(B, KT, 128, T).transpose(0, 2, 1, 3).reshape(B, 128, KT * T)

    p0, p1 = heads(HD0), heads(HD1)
    q0, k0 = p0, D + p0
    q1, k1 = p1, D + p1
    wa, ba = a["L0_attn_W_attn"], a["L0_attn_b_attn"]
    w1, b1 = a["L1_attn_w_qkv"].T, a["L1_attn_b_qkv"]
    wide = np.zeros((D, FT * 128 - INTER), np.float32)
    g, up = np.concatenate([a["L0_ffn_gate_w"].T, wide], 1), np.concatenate([a["L0_ffn_up_w"].T, wide], 1)
    down = np.concatenate([a["L0_ffn_down_w"].T, np.zeros((FT * 128 - INTER, D), np.float32)], 0)
    mask = a["mask_BxS2_bk0"]
    start = 2.0 ** (-2.0 ** (-(np.log2(H1) - 3)))
    slopes = np.array([start ** (i + 1) for i in range(H1)], np.float32)
    lam = np.exp(-slopes).astype(np.float32)
    i = np.arange(128)
    diff = (i[None, :] - i[:, None]).astype(np.float32)
    n = np.arange(H1)
    order = (4 * (n // 8) + n % 4) * 2 + n // 4 % 2
    decay = np.where(diff[:, None, :] >= 0, lam[order][None, :, None] ** np.maximum(diff, 0)[:, None, :], 0).astype(np.float32)
    causal = np.where(diff >= 0, 0.0, NEG)
    alibi = np.where(i[None, :] <= i[:, None], i[None, :] * (SLOPE / SCALE0), NEG)
    ones8, ones16 = np.zeros((128, 4, 32), np.float32), np.zeros((128, 2, 32), np.float32)
    for j in range(4):
        ones8[:, j, 8 * j:8 * j + 8] = 1
    for j in range(2):
        ones16[:, j, 16 * j:16 * j + 16] = 1
    return {
        "xc": np.concatenate([a["x"], a["ctx_2048"], transposed(a["x"]), transposed(a["ctx_2048"])], 2), "mask_col": mask.reshape(B, 128, 1), "mask_row": mask.reshape(B, 1, 128),
        "w_qk0": wa[:, np.concatenate([q0, k0])], "w_v0": wa[:, 2 * D:], "w_p0": a["L0_attn_W_proj"],
        "b_qk0": tiled(ba[np.concatenate([q0, k0])]), "b_v0": ba[2 * D:], "b_p0": a["L0_attn_b_proj"],
        "w_gu": np.concatenate([g[:, :512], up[:, :512], g[:, 512:], up[:, 512:]], 1), "w_dn": down,
        "gate_s": a["L0_ffn_gate_s"], "up_s": a["L0_ffn_up_s"], "down_s": a["L0_ffn_down_s"],
        "w_qk1": w1[:, np.concatenate([q1, k1])], "w_v1": w1[:, 2 * D:], "w_o1": a["L1_attn_w_out"].T,
        "b_qk1": tiled(b1[np.concatenate([q1, k1])]), "b_v1": b1[2 * D:], "b_o1": a["L1_attn_b_out"],
        "norm_w": tiled(a["L1_xattn_norm_w"]),
        "w_qkc": np.concatenate([a["L1_xattn_wq"].T[:, p1], a["L1_xattn_wk"].T[:, p1]], 1),
        "w_vgc": np.concatenate([a["L1_xattn_wv"].T, a["L1_xattn_wg"].T], 1), "w_oc": a["L1_xattn_wo"].T,
        "w_m": np.concatenate([a["L1_ffn_weight"].T, a["L1_ffn_lora_A"].reshape(E * R, D).T, a["L1_ffn_router_w"].T], 1),
        "w_b": a["L1_ffn_lora_B"].transpose(0, 2, 1).reshape(E * R, D),
        "ident": np.eye(128, dtype=np.float32), "decay": decay,
        "causal_kq": causal.astype(np.float32), "alibi_qk": alibi.astype(np.float32), "key_bias": (i * SLOPE).astype(np.float32).reshape(128, 1),
        "iota8": np.tile(np.arange(E, dtype=np.float32), (128, 1)), "ones8": ones8, "ones16": ones16,
    }


def kernel(**inputs):
    import concourse.bacc as bacc
    from concourse.bass_utils import run_bass_kernel_spmd

    nc = bacc.Bacc("TRN2", target_bir_lowering=False, num_devices=1)
    arrays, t = {}, {}
    for name, a in layouts({k: np.asarray(v) for k, v in inputs.items()}).items():
        a = np.ascontiguousarray(a)
        arrays[f"in_{name}"] = a
        t[name] = nc.dram_tensor(f"in_{name}", a.shape, mybir.dt.from_np(a.dtype), kind="ExternalInput").ap()
    out = nc.dram_tensor("out", (B, T, D), f32, kind="ExternalOutput").ap()
    decoder_kernel(nc, t, out)
    r = run_bass_kernel_spmd(nc, [arrays], core_ids=[0])
    return r.results[0]["out"]
```
